# Optimizing a Trainium2 kernel written in Bass

```python
import numpy as np
import jax
import jax.numpy as jnp

def _softmax(x, axis=-1):
    return jax.nn.softmax(x, axis=axis)

def _gelu(x):
    return jax.nn.gelu(x, approximate=True)

def _silu(x):
    return jax.nn.silu(x)

def _sigmoid(x):
    return jax.nn.sigmoid(x)

def _layernorm(x, axis=-1, eps=1e-05):
    m = jnp.mean(x, axis=axis, keepdims=True)
    v = jnp.var(x, axis=axis, keepdims=True)
    return (x - m) / jnp.sqrt(v + eps)

def _scatter_add(tgt, idx, src, axis=0):
    return tgt.at[idx].add(src)

def _segment_sum(src, seg, n):
    return jax.ops.segment_sum(src, seg, n)
kernel_name = 'mk_decoder_preln_d2_seqx_r8_ee9d0e'

def setup_inputs(seed: int=0):
    np.random.seed(seed)
    _w = jnp.asarray

    def _rec_inputs():
        import jax
        import jax.numpy as jnp
        _rk = jax.random.key(seed)
        x = -0.0002928 + 1 * jax.random.normal(jax.random.fold_in(_rk, 1), (2, 512, 128), jnp.float32)
        _lenS = 512 - jax.random.randint(jax.random.fold_in(_rk, 7), (2,), 0, max(1, 512 // 4) + 1, jnp.int32)
        _lenS2 = 154 - jax.random.randint(jax.random.fold_in(_rk, 8), (2,), 0, max(1, 154 // 4) + 1, jnp.int32)
        _ctx_1024P = jax.random.normal(jax.random.fold_in(_rk, 11), (2, 16, 128), jnp.float32)
        _ctx_1024c = jax.random.dirichlet(jax.random.fold_in(_rk, 511), 0.3 * jnp.ones((16,), jnp.float32), (2, 154))
        _ctx_1024t = jnp.einsum('bsk,bkd->bsd', _ctx_1024c, _ctx_1024P)
        _ctx_1024t = _ctx_1024t * jax.lax.rsqrt(jnp.mean(jnp.square(_ctx_1024t)) + 1e-12) * 0.953939
        ctx_1024 = -1.39393e-06 + 0.999914 * (_ctx_1024t + 0.3 * jax.random.normal(jax.random.fold_in(_rk, 611), (2, 154, 128), jnp.float32))
        _validS = jnp.arange(512)[None, :] < _lenS[:, None]
        _validS2 = jnp.arange(154)[None, :] < _lenS2[:, None]
        _causal = jnp.tril(jnp.ones((512, 512), dtype=bool))
        mask_BxSxS2_bk1 = jnp.broadcast_to(_validS2[:, None, :], (2, 512, 154))
        return (x, ctx_1024, mask_BxSxS2_bk1)
    x, ctx_1024, mask_BxSxS2_bk1 = _rec_inputs()

    def _L0_attn_setup():
        import jax, jax.numpy as jnp
        import numpy as np
        DIM = 128
        N_HEADS = 16
        HEAD_DIM = DIM // N_HEADS
        B, T = (2, 256)
        ROPE_THETA = 32.0
        EPS = 1e-06

        def precompute_freqs_1d(dim, seq_len, theta):
            freqs = theta ** (-jnp.arange(0, dim, 2, dtype=jnp.float32) / dim)
            t = jnp.arange(seq_len, dtype=jnp.float32)
            ang = t[:, None] * freqs[None, :]
            return (jnp.cos(ang), jnp.sin(ang))

        def _rms_norm(t, w):
            var = jnp.mean(t * t, axis=-1, keepdims=True)
            return t * jax.lax.rsqrt(var + EPS) * w

        def _rope(q, k, cos, sin):
            cos = cos[None, None]
            sin = sin[None, None]
            q1, q2 = jnp.split(q, 2, axis=-1)
            k1, k2 = jnp.split(k, 2, axis=-1)
            q_out = jnp.concatenate([q1 * cos - q2 * sin, q2 * cos + q1 * sin], axis=-1)
            k_out = jnp.concatenate([k1 * cos - k2 * sin, k2 * cos + k1 * sin], axis=-1)
            return (q_out, k_out)
        key = jax.random.key(seed)
        k1, k2, k3, k4, k5 = jax.random.split(key, 5)
        x = jax.random.normal(k1, (B, T, DIM), dtype=jnp.float32)
        w_qkv = jax.random.normal(k2, (3 * DIM, DIM), dtype=jnp.float32) * DIM ** (-0.5)
        w_proj = jax.random.normal(k3, (DIM, DIM), dtype=jnp.float32) * DIM ** (-0.5)
        q_norm_w = 1.0 + 0.1 * jax.random.normal(k4, (HEAD_DIM,), dtype=jnp.float32)
        k_norm_w = 1.0 + 0.1 * jax.random.normal(k5, (HEAD_DIM,), dtype=jnp.float32)
        return {'x': x, 'w_qkv': w_qkv, 'w_proj': w_proj, 'q_norm_w': q_norm_w, 'k_norm_w': k_norm_w}
    _L0_attn_all = _L0_attn_setup()
    _L0_attn_in = {k: v for k, v in _L0_attn_all.items() if k in ('w_qkv', 'w_proj', 'q_norm_w', 'k_norm_w')}
    del _L0_attn_all

    def _L0_xattn_setup():
        import jax, jax.numpy as jnp
        import numpy as np
        DIM = 128
        HEADS = 16
        DIM_HEAD = 64
        INNER = HEADS * DIM_HEAD
        B, N = (2, 256)
        key = jax.random.key(seed)
        ks = jax.random.split(key, 8)
        q = jax.random.normal(ks[0], (B, N, DIM), dtype=jnp.float32)
        k = jax.random.normal(ks[1], (B, N, DIM), dtype=jnp.float32)
        v = jax.random.normal(ks[2], (B, N, DIM), dtype=jnp.float32)
        causal = jnp.triu(jnp.ones((N, N), dtype=jnp.bool_), k=1)
        mask = jnp.broadcast_to(causal, (B, N, N))
        s = 0.02
        Wq = jax.random.normal(ks[3], (DIM, INNER), dtype=jnp.float32) * s
        Wk = jax.random.normal(ks[4], (DIM, INNER), dtype=jnp.float32) * s
        Wv = jax.random.normal(ks[5], (DIM, INNER), dtype=jnp.float32) * s
        Wo = jax.random.normal(ks[6], (INNER, DIM), dtype=jnp.float32) * s
        bo = jnp.zeros((DIM,), dtype=jnp.float32)
        return {'q': q, 'k': k, 'v': v, 'mask': mask, 'Wq': Wq, 'Wk': Wk, 'Wv': Wv, 'Wo': Wo, 'bo': bo}
    _L0_xattn_all = _L0_xattn_setup()
    _L0_xattn_in = {k: v for k, v in _L0_xattn_all.items() if k in ('Wq', 'Wk', 'Wv', 'Wo', 'bo')}
    del _L0_xattn_all

    def _L0_ffn_setup():
        import jax, jax.numpy as jnp
        import numpy as np
        B, T, C, H, E, K, F = (2, 256, 128, 16, 8, 2, 256)
        EPS = 1e-05

        def layernorm(x, w):
            m = x.mean(-1, keepdims=True)
            v = x.var(-1, keepdims=True)
            return (x - m) * jax.lax.rsqrt(v + EPS) * w

        def attention(x, c_attn_w, c_proj_w):
            b, t, c = x.shape
            hd = c // H
            q, k, v = jnp.split(x @ c_attn_w, 3, axis=-1)
            q = q.reshape(b, t, H, hd).transpose(0, 2, 1, 3)
            k = k.reshape(b, t, H, hd).transpose(0, 2, 1, 3)
            v = v.reshape(b, t, H, hd).transpose(0, 2, 1, 3)
            att = jnp.einsum('bhqd,bhkd->bhqk', q, k) / jnp.sqrt(jnp.asarray(hd, x.dtype))
            causal = jnp.tril(jnp.ones((t, t), bool))
            att = jnp.where(causal, att, jnp.asarray(-jnp.inf, att.dtype))
            att = jax.nn.softmax(att, axis=-1)
            y = jnp.einsum('bhqk,bhkd->bhqd', att, v)
            y = y.transpose(0, 2, 1, 3).reshape(b, t, c)
            return y @ c_proj_w

        def moe_mlp(x, router_w, w1, w2):
            b, t, c = x.shape
            xf = x.reshape(-1, c)
            router_logits = xf @ router_w
            probs = jax.nn.softmax(router_logits.astype(jnp.float32), axis=-1)
            rw, sel = jax.lax.top_k(probs, K)
            rw = rw / rw.sum(axis=-1, keepdims=True)
            rw = rw.astype(x.dtype)
            w1e = w1.reshape(c, E, F).transpose(1, 0, 2)
            w2e = w2.reshape(E, F, c)
            h = jax.nn.gelu(jnp.einsum('nc,ecf->enf', xf, w1e), approximate=False)
            y_all = jnp.einsum('enf,efc->nec', h, w2e)
            y_sel = jnp.take_along_axis(y_all, sel[:, :, None], axis=1)
            y = (y_sel * rw[:, :, None]).sum(axis=1)
            return y.reshape(b, t, c)
        key = jax.random.key(seed)
        ks = jax.random.split(key, 6)
        s = 0.02
        return {'x': jax.random.normal(ks[0], (B, T, C), jnp.float32), 'ln1_w': jnp.ones((C,), jnp.float32), 'c_attn_w': jax.random.normal(ks[1], (C, 3 * C), jnp.float32) * s, 'c_proj_w': jax.random.normal(ks[2], (C, C), jnp.float32) * s, 'ln2_w': jnp.ones((C,), jnp.float32), 'router_w': jax.random.normal(ks[3], (C, E), jnp.float32) * s, 'w1': jnp.clip(jax.random.normal(ks[4], (C, E * F), jnp.float32) * s, -0.06, 0.06), 'w2': jnp.clip(jax.random.normal(ks[5], (E * F, C), jnp.float32) * s, -0.06, 0.06)}
    _L0_ffn_all = _L0_ffn_setup()
    _L0_ffn_in = {k: v for k, v in _L0_ffn_all.items() if k in ('ln1_w', 'c_attn_w', 'c_proj_w', 'ln2_w', 'router_w', 'w1', 'w2')}
    del _L0_ffn_all

    def _L1_attn_setup():
        import jax, jax.numpy as jnp
        import numpy as np
        key = jax.random.key(seed)
        B, N, D = (32, 128, 128)
        x = jax.random.normal(key, (B, N, D), dtype=jnp.float32)
        return {'x': x}
    _L1_attn_all = _L1_attn_setup()
    _L1_attn_in = {k: v for k, v in _L1_attn_all.items() if k in ()}
    del _L1_attn_all

    def _L1_xattn_setup():
        import jax, jax.numpy as jnp
        import numpy as np
        EMBED = 128
        B, I, J = (8, 256, 256)
        SCALE = EMBED ** (-0.5)
        key = jax.random.key(seed)
        ks = jax.random.split(key, 5)
        s = EMBED ** (-0.5)
        return {'q_in': jax.random.normal(ks[0], (B, I, EMBED), dtype=jnp.float32), 'k_v': jax.random.normal(ks[1], (B, J, EMBED), dtype=jnp.float32), 'Wq': jax.random.normal(ks[2], (EMBED, EMBED), dtype=jnp.float32) * s, 'bq': jnp.zeros((EMBED,), dtype=jnp.float32), 'Wk': jax.random.normal(ks[3], (EMBED, EMBED), dtype=jnp.float32) * s, 'bk': jnp.zeros((EMBED,), dtype=jnp.float32), 'Wv': jax.random.normal(ks[4], (EMBED, EMBED), dtype=jnp.float32) * s, 'bv': jnp.zeros((EMBED,), dtype=jnp.float32)}
    _L1_xattn_all = _L1_xattn_setup()
    _L1_xattn_in = {k: v for k, v in _L1_xattn_all.items() if k in ('Wq', 'bq', 'Wk', 'bk', 'Wv', 'bv')}
    del _L1_xattn_all

    def _L1_ffn_setup():
        import jax, jax.numpy as jnp
        import numpy as np
        B, T, D, E, H, K = (2, 256, 128, 8, 512, 2)
        key = jax.random.key(seed)
        ks = jax.random.split(key, 8)
        s = 0.02
        return {'x': jax.random.normal(ks[0], (B, T, D), jnp.float32), 'rw1': jax.random.normal(ks[1], (D, D), jnp.float32) * s, 'rb1': jnp.zeros((D,), jnp.float32), 'rw2': jax.random.normal(ks[2], (D, E), jnp.float32) * s, 'rb2': jnp.zeros((E,), jnp.float32), 'we1': jax.random.normal(ks[3], (E, D, H), jnp.float32) * s, 'be1': jnp.zeros((E, H), jnp.float32), 'we2': jax.random.normal(ks[4], (E, H, D), jnp.float32) * s, 'be2': jnp.zeros((E, D), jnp.float32)}
    _L1_ffn_all = _L1_ffn_setup()
    _L1_ffn_in = {k: v for k, v in _L1_ffn_all.items() if k in ('rw1', 'rb1', 'rw2', 'rb2', 'we1', 'be1', 'we2', 'be2')}
    del _L1_ffn_all
    return {'x': x, 'ctx_1024': ctx_1024, 'mask_BxSxS2_bk1': mask_BxSxS2_bk1, 'L0_attn_w_qkv': _L0_attn_in['w_qkv'], 'L0_attn_w_proj': _L0_attn_in['w_proj'], 'L0_attn_q_norm_w': _L0_attn_in['q_norm_w'], 'L0_attn_k_norm_w': _L0_attn_in['k_norm_w'], 'L0_xattn_Wq': _L0_xattn_in['Wq'], 'L0_xattn_Wk': _L0_xattn_in['Wk'], 'L0_xattn_Wv': _L0_xattn_in['Wv'], 'L0_xattn_Wo': _L0_xattn_in['Wo'], 'L0_xattn_bo': _L0_xattn_in['bo'], 'L0_ffn_ln1_w': _L0_ffn_in['ln1_w'], 'L0_ffn_c_attn_w': _L0_ffn_in['c_attn_w'], 'L0_ffn_c_proj_w': _L0_ffn_in['c_proj_w'], 'L0_ffn_ln2_w': _L0_ffn_in['ln2_w'], 'L0_ffn_router_w': _L0_ffn_in['router_w'], 'L0_ffn_w1': _L0_ffn_in['w1'], 'L0_ffn_w2': _L0_ffn_in['w2'], 'L1_xattn_Wq': _L1_xattn_in['Wq'], 'L1_xattn_bq': _L1_xattn_in['bq'], 'L1_xattn_Wk': _L1_xattn_in['Wk'], 'L1_xattn_bk': _L1_xattn_in['bk'], 'L1_xattn_Wv': _L1_xattn_in['Wv'], 'L1_xattn_bv': _L1_xattn_in['bv'], 'L1_ffn_rw1': _L1_ffn_in['rw1'], 'L1_ffn_rb1': _L1_ffn_in['rb1'], 'L1_ffn_rw2': _L1_ffn_in['rw2'], 'L1_ffn_rb2': _L1_ffn_in['rb2'], 'L1_ffn_we1': _L1_ffn_in['we1'], 'L1_ffn_be1': _L1_ffn_in['be1'], 'L1_ffn_we2': _L1_ffn_in['we2'], 'L1_ffn_be2': _L1_ffn_in['be2']}

def reference(x, ctx_1024, mask_BxSxS2_bk1, L0_attn_w_qkv, L0_attn_w_proj, L0_attn_q_norm_w, L0_attn_k_norm_w, L0_xattn_Wq, L0_xattn_Wk, L0_xattn_Wv, L0_xattn_Wo, L0_xattn_bo, L0_ffn_ln1_w, L0_ffn_c_attn_w, L0_ffn_c_proj_w, L0_ffn_ln2_w, L0_ffn_router_w, L0_ffn_w1, L0_ffn_w2, L1_xattn_Wq, L1_xattn_bq, L1_xattn_Wk, L1_xattn_bk, L1_xattn_Wv, L1_xattn_bv, L1_ffn_rw1, L1_ffn_rb1, L1_ffn_rw2, L1_ffn_rb2, L1_ffn_we1, L1_ffn_be1, L1_ffn_we2, L1_ffn_be2):
    import jax
    import jax.numpy as jnp

    def _L0_attn_ref(x, w_qkv, w_proj, q_norm_w, k_norm_w):
        import jax, jax.numpy as jnp
        import numpy as np
        DIM = 128
        N_HEADS = 16
        HEAD_DIM = DIM // N_HEADS
        B, T = (2, 256)
        ROPE_THETA = 32.0
        EPS = 1e-06

        def precompute_freqs_1d(dim, seq_len, theta):
            freqs = theta ** (-jnp.arange(0, dim, 2, dtype=jnp.float32) / dim)
            t = jnp.arange(seq_len, dtype=jnp.float32)
            ang = t[:, None] * freqs[None, :]
            return (jnp.cos(ang), jnp.sin(ang))

        def _rms_norm(t, w):
            var = jnp.mean(t * t, axis=-1, keepdims=True)
            return t * jax.lax.rsqrt(var + EPS) * w

        def _rope(q, k, cos, sin):
            cos = cos[None, None]
            sin = sin[None, None]
            q1, q2 = jnp.split(q, 2, axis=-1)
            k1, k2 = jnp.split(k, 2, axis=-1)
            q_out = jnp.concatenate([q1 * cos - q2 * sin, q2 * cos + q1 * sin], axis=-1)
            k_out = jnp.concatenate([k1 * cos - k2 * sin, k2 * cos + k1 * sin], axis=-1)
            return (q_out, k_out)
        Bc, Tc, C = x.shape
        scale = HEAD_DIM ** (-0.5)
        qkv = x @ w_qkv.T
        qkv = qkv.reshape(Bc, Tc, 3, N_HEADS, HEAD_DIM).transpose(2, 0, 3, 1, 4)
        q, k, v = (qkv[0], qkv[1], qkv[2])
        q = _rms_norm(q, q_norm_w)
        k = _rms_norm(k, k_norm_w)
        cos, sin = precompute_freqs_1d(HEAD_DIM, Tc, ROPE_THETA)
        q, k = _rope(q, k, cos, sin)
        attn = jnp.einsum('bhqd,bhkd->bhqk', q, k) * scale
        causal = jnp.triu(jnp.ones((Tc, Tc), dtype=bool), k=1)
        attn = jnp.where(causal, -jnp.inf, attn)
        attn = jax.nn.softmax(attn, axis=-1)
        out = jnp.einsum('bhqk,bhkd->bhqd', attn, v)
        out = out.transpose(0, 2, 1, 3).reshape(Bc, Tc, C)
        return out @ w_proj.T

    def _L0_xattn_ref(q, k, v, mask, Wq, Wk, Wv, Wo, bo):
        import jax, jax.numpy as jnp
        import numpy as np
        DIM = 128
        HEADS = 16
        DIM_HEAD = 64
        INNER = HEADS * DIM_HEAD
        B, N = (2, 256)
        h, d = (HEADS, DIM_HEAD)
        scale = d ** (-0.5)
        b, n, _ = q.shape

        def heads_split(x):
            return x.reshape(b, -1, h, d).transpose(0, 2, 1, 3)
        qh = heads_split(q @ Wq)
        kh = heads_split(k @ Wk)
        vh = heads_split(v @ Wv)
        dots = jnp.einsum('bhid,bhjd->bhij', qh, kh) * scale
        mask_value = -jnp.finfo(dots.dtype).max
        dots = jnp.where(mask[:, None, :, :], mask_value, dots)
        attn = jax.nn.softmax(dots, axis=-1)
        out = jnp.einsum('bhij,bhjd->bhid', attn, vh)
        out = out.transpose(0, 2, 1, 3).reshape(b, n, h * d)
        out = out @ Wo + bo
        return out

    def _L0_ffn_ref(x, ln1_w, c_attn_w, c_proj_w, ln2_w, router_w, w1, w2):
        import jax, jax.numpy as jnp
        import numpy as np
        B, T, C, H, E, K, F = (2, 256, 128, 16, 8, 2, 256)
        EPS = 1e-05

        def layernorm(x, w):
            m = x.mean(-1, keepdims=True)
            v = x.var(-1, keepdims=True)
            return (x - m) * jax.lax.rsqrt(v + EPS) * w

        def attention(x, c_attn_w, c_proj_w):
            b, t, c = x.shape
            hd = c // H
            q, k, v = jnp.split(x @ c_attn_w, 3, axis=-1)
            q = q.reshape(b, t, H, hd).transpose(0, 2, 1, 3)
            k = k.reshape(b, t, H, hd).transpose(0, 2, 1, 3)
            v = v.reshape(b, t, H, hd).transpose(0, 2, 1, 3)
            att = jnp.einsum('bhqd,bhkd->bhqk', q, k) / jnp.sqrt(jnp.asarray(hd, x.dtype))
            causal = jnp.tril(jnp.ones((t, t), bool))
            att = jnp.where(causal, att, jnp.asarray(-jnp.inf, att.dtype))
            att = jax.nn.softmax(att, axis=-1)
            y = jnp.einsum('bhqk,bhkd->bhqd', att, v)
            y = y.transpose(0, 2, 1, 3).reshape(b, t, c)
            return y @ c_proj_w

        def moe_mlp(x, router_w, w1, w2):
            b, t, c = x.shape
            xf = x.reshape(-1, c)
            router_logits = xf @ router_w
            probs = jax.nn.softmax(router_logits.astype(jnp.float32), axis=-1)
            rw, sel = jax.lax.top_k(probs, K)
            rw = rw / rw.sum(axis=-1, keepdims=True)
            rw = rw.astype(x.dtype)
            w1e = w1.reshape(c, E, F).transpose(1, 0, 2)
            w2e = w2.reshape(E, F, c)
            h = jax.nn.gelu(jnp.einsum('nc,ecf->enf', xf, w1e), approximate=False)
            y_all = jnp.einsum('enf,efc->nec', h, w2e)
            y_sel = jnp.take_along_axis(y_all, sel[:, :, None], axis=1)
            y = (y_sel * rw[:, :, None]).sum(axis=1)
            return y.reshape(b, t, c)
        x = x + attention(layernorm(x, ln1_w), c_attn_w, c_proj_w)
        x = x + moe_mlp(layernorm(x, ln2_w), router_w, w1, w2)
        return x

    def _L1_attn_ref(x):
        import jax, jax.numpy as jnp
        import numpy as np
        logp = jax.nn.log_softmax(x, axis=-1)
        p = jnp.exp(logp)
        neg_ent = jnp.sum(p * logp, axis=-1)
        cross = jnp.einsum('bid,bjd->bij', p, logp)
        kl = neg_ent[:, :, None] - cross
        attn = jax.nn.softmax(-kl, axis=-1)
        out = jnp.einsum('bij,bjd->bid', attn, x)
        return out

    def _L1_xattn_ref(q_in, k_v, Wq, bq, Wk, bk, Wv, bv):
        import jax, jax.numpy as jnp
        import numpy as np
        EMBED = 128
        B, I, J = (8, 256, 256)
        SCALE = EMBED ** (-0.5)
        q = q_in @ Wq + bq
        k = k_v @ Wk + bk
        v = k_v @ Wv + bv
        sim = jnp.einsum('bid,bjd->bij', q, k) * SCALE
        attn = jax.nn.softmax(sim, axis=-1)
        out = jnp.einsum('bij,bjd->bid', attn, v)
        return out

    def _L1_ffn_ref(x, rw1, rb1, rw2, rb2, we1, be1, we2, be2):
        import jax, jax.numpy as jnp
        import numpy as np
        B, T, D, E, H, K = (2, 256, 128, 8, 512, 2)
        b, t, d = x.shape
        xt = x.reshape(b * t, d)
        n = xt.shape[0]
        logits = jax.nn.silu(xt @ rw1 + rb1) @ rw2 + rb2
        _, idx = jax.lax.top_k(logits, K)
        mask = jnp.zeros((n, E), bool).at[jnp.arange(n)[:, None], idx].set(True)
        w = jax.nn.softmax(jnp.where(mask, logits, -jnp.inf), axis=1)
        h = jax.nn.silu(jnp.einsum('nd,edh->enh', xt, we1) + be1[:, None, :])
        eo = jnp.einsum('enh,ehd->end', h, we2) + be2[:, None, :]
        y = xt + jnp.einsum('ne,end->nd', w, eo)
        return y.reshape(b, t, d)
    x = x + _L0_attn_ref(_layernorm(x, axis=-1), L0_attn_w_qkv, L0_attn_w_proj, L0_attn_q_norm_w, L0_attn_k_norm_w)
    x = x + _L0_xattn_ref(_layernorm(x, axis=-1), ctx_1024, ctx_1024, mask_BxSxS2_bk1, L0_xattn_Wq, L0_xattn_Wk, L0_xattn_Wv, L0_xattn_Wo, L0_xattn_bo)
    x = x + _L0_ffn_ref(_layernorm(x, axis=-1), L0_ffn_ln1_w, L0_ffn_c_attn_w, L0_ffn_c_proj_w, L0_ffn_ln2_w, L0_ffn_router_w, L0_ffn_w1, L0_ffn_w2)
    x = x + _L1_attn_ref(_layernorm(x, axis=-1))
    x = x + _L1_xattn_ref(_layernorm(x, axis=-1), ctx_1024, L1_xattn_Wq, L1_xattn_bq, L1_xattn_Wk, L1_xattn_bk, L1_xattn_Wv, L1_xattn_bv)
    x = x + _L1_ffn_ref(_layernorm(x, axis=-1), L1_ffn_rw1, L1_ffn_rb1, L1_ffn_rw2, L1_ffn_rb2, L1_ffn_we1, L1_ffn_be1, L1_ffn_we2, L1_ffn_be2)
    return x

_drawn_inputs = setup_inputs


def setup_inputs(seed=0):
    import zlib

    import numpy as np

    out = dict(_drawn_inputs(seed))
    spreads = {'L0_xattn_bo': (0.0, 0.1),
     'L0_ffn_ln1_w': (1.0, 0.6),
     'L0_ffn_ln2_w': (1.0, 0.6),
     'L1_xattn_bq': (0.0, 0.8),
     'L1_xattn_bk': (0.0, 0.8),
     'L1_xattn_bv': (0.0, 0.1),
     'L1_ffn_rb1': (0.0, 0.8),
     'L1_ffn_rb2': (0.0, 0.1),
     'L1_ffn_be1': (0.0, 0.8),
     'L1_ffn_be2': (0.0, 0.33)}
    factors = {'L0_attn_q_norm_w': 4.095,
     'L0_attn_k_norm_w': 3.534,
     'L0_xattn_Wq': 8.0,
     'L0_xattn_Wk': 8.0,
     'L0_ffn_c_attn_w': 7.442,
     'L0_ffn_c_proj_w': 7.689,
     'L0_ffn_router_w': 4.89,
     'L0_ffn_w1': 4.247,
     'L0_ffn_w2': 4.164,
     'L1_ffn_rw1': 8.0,
     'L1_ffn_rw2': 8.0,
     'L1_ffn_we1': 4.828,
     'L1_ffn_we2': 4.479}
    for name, (base, spread) in spreads.items():
        noise = np.random.default_rng([zlib.crc32(name.encode()), seed]).standard_normal(out[name].shape)
        drawn = base * np.exp(spread * noise) if base else spread * noise
        out[name] = jnp.asarray(drawn.astype(out[name].dtype))
    for name, factor in factors.items():
        out[name] = (out[name] * factor).astype(out[name].dtype)
    return out
```

```python
from contextlib import ExitStack

import concourse.bass as bass
from concourse import mybir

P = 128
NB = 2
NT = 4
TOK = NT * P
CTX = 154
HC = CTX // 2
H = 16
HD = 8
XD = 64
XC = H * XD // P
NP = H // 2
TERM = 6
SLOT = 64
E = 8
F0 = 256 // P
F1 = 512 // P
EPS_LN = 1e-5
EPS_RMS = 1e-6
LOWEST = -3.4028234663852886e38
SELF_SCALE = HD ** -0.5
X_SCALE = XD ** -0.5
L1X_SCALE = P ** -0.5

ALU = mybir.AluOpType
ACT = mybir.ActivationFunctionType
FP = mybir.dt.float32
BF = mybir.dt.bfloat16
U8 = mybir.dt.uint8
AX = mybir.AxisListType.X

CHUNKS = [[(0, 0)], [(1, 0), (3, 384)], [(2, 0)]]
PT_AT = [0, TOK, 2 * TOK, TOK + 384]

C_ID, C_CAUSAL, C_CAUSALT, C_COS, C_SIN, C_TRI, C_END = 0, 128, 640, 768, 800, 832, 896


def decoder(nc, a, out):
    with ExitStack() as ctx:
        def sb(name, shape, dt=FP):
            return ctx.enter_context(nc.sbuf_tensor(name, shape, dt))

        sems = {}

        def sem(name):
            if name not in sems:
                sems[name] = ctx.enter_context(nc.semaphore(name))
            return sems[name]

        bank = [ctx.enter_context(nc.psum_tensor(f"bank{i}", [P, 512], FP)) for i in range(8)]

        con = sb("con", [P, C_END])
        ident = con[:, C_ID:C_ID + P]
        ident_bf = sb("ident_bf", [P, P], BF)
        causal = con[:, C_CAUSAL:C_CAUSAL + TOK]
        causalT_bf = sb("causalT_bf", [P, P], BF)
        cos = con[:, C_COS:C_COS + 32].rearrange("p (t d) -> p t d", t=NT)
        sin = con[:, C_SIN:C_SIN + 32].rearrange("p (t d) -> p t d", t=NT)
        tri = con[:, C_TRI:C_TRI + 64].rearrange("p (e j) -> p e j", e=E)
        w_qkv = [sb("w_qkv0", [P, 3 * P]), sb("w_qkv2", [P, 3 * P])]
        w_proj = [sb("w_proj0", [P, P]), sb("w_proj2", [P, P])]
        qk_w = sb("qk_w", [P, 2, HD])
        early = sb("early", [P, 4, H * XD])
        wq_x, wk_x, wv_x = early[:, 0, :], early[:, 1, :], early[:, 2, :]
        wo_x = early[:, 3, :].rearrange("p (c n) -> p c n", c=XC)
        ctxT = sb("ctxT", [P, NB * CTX])
        mask8 = sb("mask8", [P, NB * NT, CTX], U8)
        mask = sb("mask", [P, NB * NT, CTX])
        rows = sb("rows", [P, 4, P])
        bo, ln1_w, ln2_w, bv_row = (rows[:, i, :] for i in range(4))
        rb2 = sb("rb2", [P, E])
        cols = sb("cols", [P, 3 + E * F1])
        bq, bk, rb1, be1 = cols[:, 0:1], cols[:, 1:2], cols[:, 2:3], cols[:, 3:3 + E * F1]
        wq_l1 = sb("wq_l1", [P, 3, P])
        router = sb("router", [P, E])
        rw1 = sb("rw1", [P, P])
        rw2 = sb("rw2", [P, E])
        be2 = sb("be2", [E, P])
        values_x = sb("values_x", [P, NB * 2 * H * (XD + 1)])
        vx = values_x[0:HC, :].rearrange("p (b h n d) -> p b h n d", b=NB, h=2, n=H)
        w1 = [sb("w1_l0", [P, E * F0 * P]), early[:].rearrange("p a n -> p (a n)")]
        w2 = [sb("w2_l0", [P, E * F0, P]),
              values_x[:, 0:E * F1 * P].rearrange("p (c n) -> p c n", n=P)]

        x = sb("x", [P, NB * NT, P])
        y = sb("y", [P, NB * NT, P])
        z = sb("z", [P, NB * NT, P])
        zT = sb("zT", [P, NB, TOK])
        ln_stats = sb("ln_stats", [P, NT, 6])
        ln_mv = sb("ln_mv", [P, NT, 2])
        ln_var = sb("ln_var", [P, NT])
        ln_log = sb("ln_log", [P, NT])
        ln_r0 = sb("ln_r0", [P, NT])
        ln_t = sb("ln_t", [P, NT])
        ln_r = sb("ln_r", [P, NT])

        qk = sb("qk", [P, 2, NT * H, HD])
        rest = sb("rest", [P, 2, NT * H, HD])
        sq, rope_b = rest, rest
        rms_v = sb("rms_v", [P, 2 * NT * H])
        rms_l = sb("rms_l", [P, 2 * NT * H])
        rms_0 = sb("rms_0", [P, 2 * NT * H])
        rms_t = sb("rms_t", [P, 2 * NT * H])
        rope_c = sb("rope_c", [P, 2, NT, HD])
        rope_s = sb("rope_s", [P, 2, NT, HD])
        slots = sb("slots", [P, 2, NT * H * SLOT], BF)
        qs, ks = (slots[:, i, :].rearrange("p (n c) -> p n c", c=SLOT) for i in range(2))
        v9 = sb("v9", [P, NB, NT, H, HD + 1])
        qkT = sb("qkT", [P, 2, 2 * TOK], BF)
        qmT = sb("qmT", [P, 2, TOK], BF)
        s_scr = sb("s_scr", [P, 4, TOK])
        top = sb("top", [P, 2, NT, 2])
        pT = sb("pT", [P, 2, 2, 5 * TOK // 2])
        rsum = sb("rsum", [P, NT, 2])
        o_tok = sb("o_tok", [P, NT, P])
        oT = sb("oT", [P, TOK])

        kTx = sb("kTx", [P, NB, XC, CTX])
        wide = sb("wide", [P, 8, TOK])
        qTx = oxT = hT = wide
        xs = sb("xs", [P, 2, 2, CTX])
        xtop = sb("xtop", [P, 2, 2])
        xneg = sb("xneg", [P, 2, 2])
        xp = sb("xp", [P, 2, 2, CTX])
        xpT = sb("xpT", [HC, 2, 4 * P])
        xrs = sb("xrs", [P, 2, 2])
        ox = pT[:].rearrange("p a h n -> p (a h n)")[:, 0:NT * XC * P].rearrange(
            "p (t c n) -> p t c n", t=NT, c=XC)

        rT = sb("rT", [P, TOK])
        logit = sb("logit", [P, NT, E])
        g_max = sb("g_max", [P, NT])
        g_e = sb("g_e", [P, NT, E])
        g_cmp = sb("g_cmp", [P, NT * E, E])
        g_eq = sb("g_eq", [P, NT * E, E])
        g_rank = sb("g_rank", [P, NT * E])
        g_sum = sb("g_sum", [P, NT])
        gate = sb("gate", [P, NB, NT, E])
        gateT = sb("gateT", [E, TOK])

        a_max = sb("a_max", [P, NT])
        a_e = wide[:, 0, :].rearrange("p (t c) -> p t c", t=NT)
        a_sum = sb("a_sum", [P, NT])
        a_log = sb("a_log", [P, NT])
        a_nb = sb("a_nb", [P, NT])
        a_p = wide[:, 1, :].rearrange("p (t c) -> p t c", t=NT)
        a_lp = wide[:, 2, :].rearrange("p (t c) -> p t c", t=NT)
        a_scr = wide[:, 3, :].rearrange("p (t c) -> p t c", t=NT)
        a_ent = sb("a_ent", [P, NT])
        a_nent = sb("a_nent", [P, NT])
        a_pT = wide[:, 4, :]
        a_lpT = wide[:, 5, :]
        b_p, b_pT = (slots[:, i, :].bitcast(FP).rearrange("p (t k) -> p t k", t=NT) for i in range(2))
        b_sum = sb("b_sum", [P, NT])
        b_rs = sb("b_rs", [P, NT])
        k1T = sb("k1T", [P, NB, CTX])
        v1 = sb("v1", [HC, NB, 2, P])
        c_max = sb("c_max", [P, NT])
        c_neg = sb("c_neg", [P, NT])

        def tiles(b):
            return slice(NT * b, NT * b + NT)

        loads = [
            ("x", x[:], a["x"].rearrange("b (t p) c -> p (b t) c", p=P)),
            ("con", con[:], a["con"]),
            ("att0", w_qkv[0][:], a["w_qkvT"]),
            ("qk_w", qk_w[:, 0, :], a["qn"].to_broadcast([P, HD])),
            ("qk_w", qk_w[:, 1, :], a["kn"].to_broadcast([P, HD])),
            ("ctx", ctxT[:], a["ctxT"]),
            ("wk_x", wk_x, a["xWk"]),
            ("wv_x", wv_x, a["xWv"]),
            ("l1kv", wq_l1[:], a["l1_wqkv"].rearrange("j p c -> p j c")),
            ("cols", cols[:], a["cols"]),
            ("rows", rows[:, 0, :], a["bo"].to_broadcast([P, P])),
            ("rows", rows[:, 1, :], a["ln1"].to_broadcast([P, P])),
            ("rows", rows[:, 2, :], a["ln2"].to_broadcast([P, P])),
            ("rows", rows[:, 3, :], a["bv"].to_broadcast([P, P])),
            ("proj0", w_proj[0][:], a["w_projT"]),
            ("mask", mask8[:], a["mask"].rearrange("b (t p) k -> p (b t) k", p=P)),
            ("wq_x", wq_x, a["xWq"]),
            ("wo_x", wo_x, a["xWo"].rearrange("(c p) n -> p c n", p=P)),
            ("att2", w_qkv[1][:], a["c_attn"]),
            ("att2", w_proj[1][:], a["c_proj"]),
            ("router", router[:], a["router"]),
            ("moe0", w1[0][:], a["w1"]),
            ("moe0", w2[0][:], a["w2"].rearrange("(c p) n -> p c n", p=P)),
            ("l1r", rw1[:], a["rw1"]),
            ("l1r", rw2[:], a["rw2"]),
            ("l1r", rb2[:], a["rb2"].to_broadcast([P, E])),
            ("l1r", be2[:], a["be2"]),
            ("moe1", w1[1], a["we1"]),
            ("moe1", w2[1], a["we2"].rearrange("(c p) n -> p c n", p=P)),
        ]
        group_size = {}
        for g, _, _ in loads:
            group_size[g] = group_size.get(g, 0) + 16

        def loaded(eng, group):
            eng.wait_ge(sem(f"load_{group}"), group_size[group])

        x_stored = sem("x_stored")
        z_ready = sem("z_ready")
        x_added = sem("x_added")
        zT_full = sem("zT_full")
        zT_ready = sem("zT_ready")
        setup = sem("setup")
        log_in, log_out = sem("log_in"), sem("log_out")
        pre_full, pre_done = sem("pre_full"), sem("pre_done")

        block = ctx.enter_context(nc.Block())

        @block.sync
        def _(sp):
            for group, dst, src in loads:
                if group == "moe1":
                    sp.wait_ge(x_added, 4)
                sp.dma_start(dst, src).then_inc(sem(f"load_{group}"), 16)
            out_v = out.rearrange("b (t p) c -> p (b t) c", p=P)
            for b in range(NB):
                sp.wait_ge(x_added, 12 + b + 1)
                sp.dma_start(out_v[:, tiles(b), :], x[:, tiles(b), :]).then_inc(x_stored, 16)
            sp.wait_ge(x_stored, 16 * NB)

        @block.tensor
        def _(pe):
            mm, tr = nc.tensor.matmul, nc.tensor.transpose

            def context():
                i = 0

                def start():
                    if i >= 4:
                        pe.wait_ge(pre_done, i - 3)
                    return bank[i % 4]
                loaded(pe, "ctx")
                loaded(pe, "wk_x")
                for b in range(NB):
                    for c in range(XC):
                        o = start()
                        mm(o[:, 0:CTX], wk_x[:, c * P:c * P + P], ctxT[:, b * CTX:b * CTX + CTX],
                           start=True, stop=True).then_inc(pre_full, 1)
                        i += 1
                loaded(pe, "wv_x")
                for b in range(NB):
                    for h in range(2):
                        for w in range(2):
                            o = start()
                            at = b * CTX + h * HC
                            mm(o[0:HC, :], ctxT[:, at:at + HC], wv_x[:, 512 * w:512 * w + 512],
                               start=True, stop=True).then_inc(pre_full, 1)
                            i += 1
                loaded(pe, "l1kv")
                for b in range(NB):
                    o = start()
                    mm(o[:, 0:CTX], wq_l1[:, 1, :], ctxT[:, b * CTX:b * CTX + CTX],
                       start=True, stop=True).then_inc(pre_full, 1)
                    i += 1
                    for h in range(2):
                        o = start()
                        at = b * CTX + h * HC
                        mm(o[0:HC, 0:P], ctxT[:, at:at + HC], wq_l1[:, 2, :],
                           start=True, stop=True).then_inc(pre_full, 1)
                        i += 1

            def transpose_z(s, b):
                pe.wait_ge(z_ready, 2 * s + b + 1)
                for t in range(NT):
                    last = tr(bank[0][:, t * P:t * P + P], z[:, NT * b + t, :], ident)
                last.then_inc(zT_full, 1)
                pe.wait_ge(zT_ready, zt_index(s, b) + 1)

            def causal_attention(s, b):
                n = 0 if s == 0 else 1
                S = lambda name: sem(f"a{s}_{name}")
                transpose_z(s, b)
                loaded(pe, "att0" if s == 0 else "att2")
                if s == 2 or b == 1:
                    pe.wait_ge(x_added, 2 * s + b)
                for t in range(NT):
                    mm(bank[1 + t][:, 0:3 * P], zT[:, b, t * P:t * P + P], w_qkv[n][:],
                       start=True, stop=True).then_inc(S("qkv_full"), 1)
                pe.wait_ge(S("v_ready"), b + 1)
                pe.wait_ge(S("qk_copied"), 2 * (b + 1))

                def to_qkT(u):
                    g = NP * b + u
                    if u == 0:
                        pe.wait_ge(S("parts_ready"), 3 * (b + 1))
                    if g:
                        pe.wait_ge(S("qkT_ready"), g)
                    o = bank[1][:].bitcast(BF)
                    for i, src in enumerate((qs, ks)):
                        for t in range(NT):
                            at = t * H + 2 * u
                            last = tr(o[:, (NT * i + t) * P:(NT * i + t + 1) * P],
                                      src[:, at:at + 2, :].rearrange("p h c -> p (h c)"), ident_bf[:])
                    last.then_inc(S("qkT_full"), 1)

                def raw_scores(u, some):
                    g = NP * b + u
                    pe.wait_ge(S("qkT_ready"), g + 1)
                    for i in some:
                        n_item = 8 * g + i
                        if n_item >= 2:
                            pe.wait_ge(S("max_done"), n_item - 1)
                        hh, t = i % 2, i // 2
                        r = slice(SLOT * hh, SLOT * hh + SLOT)
                        mm(bank[2 + hh][:, 0:(t + 1) * P], qkT[r, g % 2, t * P:t * P + P],
                           qkT[r, g % 2, TOK:TOK + (t + 1) * P], start=True, stop=True)\
                            .then_inc(S("raw_full"), 1)

                def to_qmT(u):
                    g = NP * b + u
                    pe.wait_ge(S("max_ready"), g + 1)
                    if g:
                        pe.wait_ge(S("qmT_ready"), g)
                    o = bank[0][:].bitcast(BF)
                    for t in range(NT):
                        at = t * H + 2 * u
                        last = tr(o[:, t * P:t * P + P],
                                  qs[:, at:at + 2, :].rearrange("p h c -> p (h c)"), ident_bf[:])
                    last.then_inc(S("qmT_full"), 1)

                def scores(u, c):
                    g = NP * b + u
                    m = 6 * g + c
                    if m >= 3:
                        pe.wait_ge(S("pT_ready"), m - 2)
                    o = bank[4 + m % 3]
                    r = slice(SLOT * (c // 3), SLOT * (c // 3) + SLOT)
                    for j, at in CHUNKS[c % 3]:
                        q0, w = j, (NT - j) * P
                        mm(o[:, at:at + w], qkT[r, g % 2, TOK + j * P:TOK + j * P + P],
                           qmT[r, g % 2, q0 * P:TOK], start=True, stop=False)
                        last = mm(o[:, at:at + P], ident_bf[:], causalT_bf[:], start=False, stop=True)
                    last.then_inc(S("scores_full"), 1)

                def values(u, hh):
                    g = NP * b + u
                    if hh == 0 and g:
                        pe.wait_ge(S("o_done"), g)
                    pe.wait_ge(S("pT_ready"), 6 * g + 3 * (hh + 1))
                    for t in range(NT):
                        at = (2 * t + hh) * (HD + 1)
                        for j in range(t + 1):
                            col = PT_AT[j] + (t - j) * P
                            last = mm(bank[7][:, at:at + HD + 1], pT[:, g % 2, hh, col:col + P],
                                      v9[:, b, j, 2 * u + hh, :], start=(j == 0), stop=(j == t))
                    if hh:
                        last.then_inc(S("o_full"), 1)

                to_qkT(0)
                raw_scores(0, range(8))
                for u in range(NP):
                    if u + 1 < NP:
                        to_qkT(u + 1)
                    to_qmT(u)
                    pe.wait_ge(S("qmT_ready"), NP * b + u + 1)
                    for c in range(3):
                        scores(u, c)
                    if u + 1 < NP:
                        raw_scores(u + 1, range(4))
                    for c in range(3, 6):
                        scores(u, c)
                    if u + 1 < NP:
                        raw_scores(u + 1, range(4, 8))
                    values(u, 0)
                    values(u, 1)
                pe.wait_ge(S("o_done"), NP * (b + 1))
                for t in range(NT):
                    last = tr(bank[0][:, t * P:t * P + P], o_tok[:, t, :], ident)
                last.then_inc(S("oT_full"), 1)
                loaded(pe, "proj0" if s == 0 else "att2")
                pe.wait_ge(S("oT_ready"), b + 1)
                for t in range(NT):
                    last = mm(bank[7][:, t * P:t * P + P], oT[:, t * P:t * P + P], w_proj[n][:],
                              start=True, stop=True)
                last.then_inc(S("proj_full"), 1)

            def cross_attention(b):
                S = lambda name: sem(f"x_{name}")
                transpose_z(1, b)
                loaded(pe, "wq_x")
                pe.wait_ge(x_added, 2 + b)
                for c in range(XC):
                    n = XC * b + c
                    if c >= 2:
                        pe.wait_ge(S("q_ready"), n - 1)
                    mm(bank[c % 2][:], wq_x[:, c * P:c * P + P], zT[:, b, :], start=True, stop=True)\
                        .then_inc(S("q_full"), 1)
                pe.wait_ge(S("q_ready"), XC * (b + 1))

                def scores(i):
                    g = XC * NT * b + i
                    c, t = i // NT, i % NT
                    if g >= 2:
                        pe.wait_ge(S("max_done"), g - 1)
                    for hh in range(2):
                        r = slice(XD * hh, XD * hh + XD)
                        last = mm(bank[2 * (g % 2) + hh][:, 0:CTX], qTx[r, c, t * P:t * P + P],
                                  kTx[r, b, c, :], start=True, stop=True)
                    last.then_inc(S("s_full"), 1)

                def transposes(i):
                    g = XC * NT * b + i
                    pe.wait_ge(S("p_ready"), g + 1)
                    if g >= 2:
                        pe.wait_ge(S("pT_ready"), g - 1)
                    o = bank[4 + g % 2]
                    for hh in range(2):
                        for h in range(2):
                            k = 2 * hh + h
                            last = tr(o[0:HC, k * P:k * P + P], xp[:, g % 2, hh, h * HC:h * HC + HC], ident)
                    last.then_inc(S("pT_full"), 1)

                def values(i):
                    g = XC * NT * b + i
                    c = i // NT
                    pe.wait_ge(S("pT_ready"), g + 1)
                    if g >= 2:
                        pe.wait_ge(S("o_done"), g - 1)
                    o = bank[6 + g % 2]
                    for hh in range(2):
                        for h in range(2):
                            k = 2 * hh + h
                            last = mm(o[:, (XD + 1) * hh:(XD + 1) * (hh + 1)], xpT[:, g % 2, k * P:k * P + P],
                                      vx[:, b, h, 2 * c + hh, :], start=(h == 0), stop=(h == 1))
                    last.then_inc(S("o_full"), 1)

                n = XC * NT
                for i in range(n + 3):
                    if i < n:
                        scores(i)
                    if 2 <= i < n + 2:
                        transposes(i - 2)
                    if i >= 3:
                        values(i - 3)
                pe.wait_ge(S("o_done"), n * (b + 1))
                for c in range(XC):
                    if c >= 2:
                        pe.wait_ge(S("oT_ready"), XC * b + c - 1)
                    for t in range(NT):
                        last = tr(bank[c % 2][:, t * P:t * P + P], ox[:, t, c, :], ident)
                    last.then_inc(S("oT_full"), 1)
                loaded(pe, "wo_x")
                pe.wait_ge(S("oT_ready"), XC * (b + 1))
                for t in range(NT):
                    for c in range(XC):
                        last = mm(bank[7][:, t * P:t * P + P], oxT[:, c, t * P:t * P + P], wo_x[:, c, :],
                                  start=(c == 0), stop=(c == XC - 1))
                last.then_inc(S("proj_full"), 1)

            def experts(s, b):
                n, fc = (0, F0) if s == 3 else (1, F1)
                S = lambda name: sem(f"m{s}_{name}")
                transpose_z(s, b)
                pe.wait_ge(x_added, 2 * s + b)
                if s == 3:
                    loaded(pe, "router")
                    for t in range(NT):
                        last = mm(bank[1][:, t * E:t * E + E], zT[:, b, t * P:t * P + P], router[:],
                                  start=True, stop=True)
                else:
                    loaded(pe, "l1r")
                    mm(bank[2][:], rw1[:], zT[:, b, :], start=True, stop=True).then_inc(S("r_full"), 1)
                    pe.wait_ge(S("r_ready"), b + 1)
                    for t in range(NT):
                        last = mm(bank[1][:, t * E:t * E + E], rT[:, t * P:t * P + P], rw2[:],
                                  start=True, stop=True)
                last.then_inc(S("logit_full"), 1)
                loaded(pe, "moe0" if s == 3 else "moe1")

                def hidden(e):
                    for c in range(fc):
                        m = (E * b + e) * fc + c
                        if m >= 4:
                            pe.wait_ge(S("h_ready"), m - 3)
                        f = e * fc + c
                        mm(bank[2 + m % 4][:], w1[n][:, f * P:f * P + P], zT[:, b, :],
                           start=True, stop=True).then_inc(S("h_full"), 1)

                def down(e):
                    g = E * b + e
                    pe.wait_ge(S("h_ready"), (g + 1) * fc)
                    if g >= 2:
                        pe.wait_ge(S("e_done"), g - 1)
                    for t in range(NT):
                        for c in range(fc):
                            last = mm(bank[6 + g % 2][:, t * P:t * P + P],
                                      hT[:, (g * fc + c) % 8, t * P:t * P + P], w2[n][:, e * fc + c, :],
                                      start=(c == 0), stop=(c == fc - 1))
                    last.then_inc(S("e_full"), 1)

                for e in range(E + 1):
                    if e < E:
                        hidden(e)
                    if e:
                        down(e - 1)
                if s == 6:
                    pe.wait_ge(S("gate_ready"), b + 1)
                    for t in range(NT):
                        last = tr(bank[0][0:E, t * P:t * P + P], gate[:, b, t, :], ident)
                    last.then_inc(S("gT_full"), 1)
                    pe.wait_ge(S("gT_ready"), b + 1)
                    for t in range(NT):
                        last = mm(bank[1][:, t * P:t * P + P], gateT[:, t * P:t * P + P], be2[:],
                                  start=True, stop=True)
                    last.then_inc(S("be2_full"), 1)

            def divergence_attention(b):
                S = lambda name: sem(f"d_{name}")
                pe.wait_ge(x_added, 8 + b)
                pe.wait_ge(S("p_ready"), NT * (b + 1))
                for t in range(NT):
                    last = tr(bank[0][:, t * P:t * P + P], a_p[:, t, :], ident)
                last.then_inc(S("t_full"), 1)
                pe.wait_ge(S("lp_ready"), NT * (b + 1))
                for t in range(NT):
                    last = tr(bank[1][:, t * P:t * P + P], a_lp[:, t, :], ident)
                last.then_inc(S("t_full"), 1)
                pe.wait_ge(S("t_ready"), 2 * (b + 1))
                for t in range(NT):
                    mm(bank[2 + t][:], a_pT[:, t * P:t * P + P], a_lpT, start=True, stop=True)\
                        .then_inc(S("s_full"), 1)
                for t in range(NT):
                    pe.wait_ge(S("e_ready"), NT * b + t + 1)
                    g = NT * b + t
                    if t >= 2:
                        pe.wait_ge(S("eT_ready"), g - 1)
                    for j in range(NT):
                        last = tr(bank[t % 2][:, j * P:j * P + P], b_p[:, t, j * P:j * P + P], ident)
                    last.then_inc(S("eT_full"), 1)
                for t in range(NT):
                    pe.wait_ge(S("eT_ready"), NT * b + t + 1)
                    for j in range(NT):
                        last = mm(bank[7][:, t * P:t * P + P], b_pT[:, t, j * P:j * P + P],
                                  z[:, NT * b + j, :], start=(j == 0), stop=(j == NT - 1))
                last.then_inc(S("o_full"), 1)

            def cross_attention_1(b):
                S = lambda name: sem(f"c_{name}")
                transpose_z(5, b)
                pe.wait_ge(x_added, 10 + b)
                mm(bank[1][:], wq_l1[:, 0, :], zT[:, b, :], start=True, stop=True).then_inc(S("q_full"), 1)
                pe.wait_ge(S("q_ready"), b + 1)
                for t in range(NT):
                    last = mm(bank[2 + t // 2][:, t % 2 * CTX:t % 2 * CTX + CTX], oT[:, t * P:t * P + P],
                              k1T[:, b, :], start=True, stop=True)
                last.then_inc(S("s_full"), 1)
                for t in range(NT):
                    pe.wait_ge(S("p_ready"), NT * b + t + 1)
                    o = bank[4 + t // 2]
                    for h in range(2):
                        k = 2 * (t % 2) + h
                        last = tr(o[0:HC, k * P:k * P + P], b_p[:, t, h * HC:h * HC + HC], ident)
                    if t % 2:
                        last.then_inc(S("pT_full"), 1)
                pe.wait_ge(S("pT_ready"), 2 * (b + 1))
                for t in range(NT):
                    for h in range(2):
                        k = 2 * (t % 2) + h
                        last = mm(bank[7][:, t * P:t * P + P], b_pT[0:HC, t // 2, k * P:k * P + P],
                                  v1[:, b, h, :], start=(h == 0), stop=(h == 1))
                last.then_inc(S("o_full"), 1)

            pe.wait_ge(setup, 1)
            loaded(pe, "con")
            context()
            for b in range(NB):
                if b == 0:
                    pe.wait_ge(pre_done, PRE)
                causal_attention(0, b)
            for b in range(NB):
                cross_attention(b)
            for b in range(NB):
                causal_attention(2, b)
            for b in range(NB):
                experts(3, b)
            for b in range(NB):
                divergence_attention(b)
            for b in range(NB):
                cross_attention_1(b)
            for b in range(NB):
                experts(6, b)

        @block.scalar
        def _(act):
            af = nc.scalar.activation
            own = sem("act_own")
            own_n = [0]

            def link(ins):
                own_n[0] += 1
                ins.then_inc(own, 1)
                act.wait_ge(own, own_n[0])

            norms = [0]

            def layer_norm():
                norms[0] += 1
                act.wait_ge(log_in, norms[0])
                link(af(ln_log[:], ln_var[:], ACT.Ln))
                af(ln_r0[:], ln_log[:], ACT.Exp, scale=-0.5).then_inc(log_out, 1)

            def copy_zT(s, b):
                act.wait_ge(zT_full, zt_index(s, b) + 1)
                nc.scalar.copy(zT[:, b, :], bank[0][:]).then_inc(zT_ready, 1)

            def context():
                i = 0
                for b in range(NB):
                    for c in range(XC):
                        i += 1
                        act.wait_ge(pre_full, i)
                        nc.scalar.copy(kTx[:, b, c, :], bank[(i - 1) % 4][:, 0:CTX]).then_inc(pre_done, 1)
                act.wait_ge(setup, 1)
                for b in range(NB):
                    for h in range(2):
                        for w in range(2):
                            i += 1
                            act.wait_ge(pre_full, i)
                            nc.scalar.copy(vx[:, b, h, 8 * w:8 * w + 8, 0:XD],
                                           bank[(i - 1) % 4][0:HC, :].rearrange("p (h d) -> p h d", d=XD))\
                                .then_inc(pre_done, 1)
                loaded(act, "cols")
                for b in range(NB):
                    i += 1
                    act.wait_ge(pre_full, i)
                    af(k1T[:, b, :], bank[(i - 1) % 4][:, 0:CTX], ACT.Identity, bias=bk).then_inc(pre_done, 1)
                    for h in range(2):
                        i += 1
                        act.wait_ge(pre_full, i)
                        nc.scalar.copy(v1[:, b, h, :], bank[(i - 1) % 4][0:HC, 0:P]).then_inc(pre_done, 1)

            def causal_attention(s, b):
                S = lambda name: sem(f"a{s}_{name}")
                copy_zT(s, b)
                for t in range(2):
                    act.wait_ge(S("qkv_full"), NT * b + t + 1)
                    rows_t = slice(t * H, t * H + H)
                    src = bank[1 + t][:, 0:3 * P].rearrange("p (j h d) -> p j h d", j=3, h=H)
                    af(qk[:, 0, rows_t, :], src[:, 0], ACT.Copy, scale=1.0 if s == 0 else SELF_SCALE)
                    nc.scalar.copy(qk[:, 1, rows_t, :], src[:, 1])
                    nc.scalar.copy(v9[:, b, t, :, 0:HD], src[:, 2]).then_inc(S("qk_copied"), 1)
                if s == 0:
                    act.wait_ge(S("rms_in"), b + 1)
                    link(af(rms_l[:], rms_v[:], ACT.Ln))
                    af(rms_0[:], rms_l[:], ACT.Exp, scale=-0.5).then_inc(S("rms_out"), 1)
                act.wait_ge(S("qk_ready"), b + 1)
                n = NT * H

                def parts(i, dst, at, times):
                    src = (qk[:, i] if at == 0 else rest[:, i]).unsqueeze(2).to_broadcast([P, n, times, HD])
                    return nc.scalar.copy(dst[:, :, at:at + times * HD].rearrange("p n (r d) -> p n r d", r=times), src)

                parts(0, qs, 0, 3)
                parts(1, ks, 0, 1).then_inc(S("part1"), 1)
                act.wait_ge(S("rest1"), b + 1)
                parts(0, qs, 3 * HD, 2)
                parts(1, ks, HD, 1).then_inc(S("part2"), 1)

                def copy_qkT(u):
                    g = NP * b + u
                    act.wait_ge(S("qkT_full"), g + 1)
                    nc.scalar.copy(qkT[:, g % 2, :], bank[1][:].bitcast(BF)).then_inc(S("qkT_ready"), 1)

                def copy_qmT(u):
                    g = NP * b + u
                    act.wait_ge(S("qmT_full"), g + 1)
                    nc.scalar.copy(qmT[:, g % 2, :], bank[0][:].bitcast(BF)[:, 0:TOK])\
                        .then_inc(S("qmT_ready"), 1)

                copy_qkT(0)
                for u in range(NP):
                    g = NP * b + u
                    if u + 1 < NP:
                        copy_qkT(u + 1)
                    copy_qmT(u)
                    if g >= 2:
                        act.wait_ge(S("o_full"), g - 1)
                    for c in range(6):
                        m = 6 * g + c
                        act.wait_ge(S("scores_full"), m + 1)
                        at, w = TOK * (c % 3), TOK if c % 3 < 2 else TOK // 2
                        af(pT[:, g % 2, c // 3, at:at + w], bank[4 + m % 3][:, 0:w], ACT.Exp)\
                            .then_inc(S("pT_ready"), 1)
                act.wait_ge(S("oT_full"), b + 1)
                nc.scalar.copy(oT[:, :], bank[0][:]).then_inc(S("oT_ready"), 1)

            def cross_attention(b):
                S = lambda name: sem(f"x_{name}")
                copy_zT(1, b)
                for c in range(XC):
                    act.wait_ge(S("q_full"), XC * b + c + 1)
                    nc.scalar.copy(qTx[:, c, :], bank[c % 2][:]).then_inc(S("q_ready"), 1)
                n = XC * NT

                def exps(i):
                    g = n * b + i
                    act.wait_ge(S("neg_ready"), g + 1)
                    if g >= 2:
                        act.wait_ge(S("pT_full"), g - 1)
                    for hh in range(2):
                        last = af(xp[:, g % 2, hh, :], xs[:, g % 2, hh, :], ACT.Exp,
                                  bias=xneg[:, g % 2, hh:hh + 1], scale=X_SCALE)
                    last.then_inc(S("p_ready"), 1)

                def copy_pT(i):
                    g = n * b + i
                    act.wait_ge(S("pT_full"), g + 1)
                    if g >= 2:
                        act.wait_ge(S("o_full"), g - 1)
                    nc.scalar.copy(xpT[:, g % 2, :], bank[4 + g % 2][0:HC, :]).then_inc(S("pT_ready"), 1)

                for i in range(n + 1):
                    if i < n:
                        exps(i)
                    if i >= 1:
                        copy_pT(i - 1)
                for c in range(XC):
                    act.wait_ge(S("oT_full"), XC * b + c + 1)
                    nc.scalar.copy(oxT[:, c, :], bank[c % 2][:]).then_inc(S("oT_ready"), 1)

            def experts(s, b):
                fc = F0 if s == 3 else F1
                S = lambda name: sem(f"m{s}_{name}")
                copy_zT(s, b)
                if s == 6:
                    act.wait_ge(S("r_full"), b + 1)
                    af(rT[:], bank[2][:], ACT.Silu, bias=rb1).then_inc(S("r_ready"), 1)
                act.wait_ge(S("gate_in"), b + 1)
                af(g_e[:], logit[:], ACT.Exp).then_inc(S("gate_out"), 1)
                for e in range(E):
                    for c in range(fc):
                        m = (E * b + e) * fc + c
                        act.wait_ge(S("h_full"), m + 1)
                        if m >= 8:
                            act.wait_ge(S("e_full"), (m - 8) // fc + 1)
                        f = e * fc + c
                        if s == 3:
                            ins = af(hT[:, m % 8, :], bank[2 + m % 4][:], ACT.Gelu)
                        else:
                            ins = af(hT[:, m % 8, :], bank[2 + m % 4][:], ACT.Silu, bias=be1[:, f:f + 1])
                        ins.then_inc(S("h_ready"), 1)
                if s == 6:
                    act.wait_ge(S("gT_full"), b + 1)
                    nc.scalar.copy(gateT[:], bank[0][0:E, :]).then_inc(S("gT_ready"), 1)

            def divergence_attention(b):
                S = lambda name: sem(f"d_{name}")
                act.wait_ge(S("max_ready"), b + 1)
                for t in range(NT):
                    ins = af(a_e[:, t, :], z[:, NT * b + t, :], ACT.Exp, bias=a_max[:, t:t + 1],
                             accum_out=a_sum[:, t:t + 1])
                link(ins)
                af(a_log[:], a_sum[:], ACT.Ln).then_inc(S("log_ready"), 1)
                act.wait_ge(S("nb_ready"), b + 1)
                if b:
                    act.wait_ge(S("t_full"), 2 * b)
                for t in range(NT):
                    af(a_p[:, t, :], z[:, NT * b + t, :], ACT.Exp, bias=a_nb[:, t:t + 1])\
                        .then_inc(S("p_ready"), 1)
                act.wait_ge(S("t_full"), 2 * b + 1)
                nc.scalar.copy(a_pT, bank[0][:]).then_inc(S("t_ready"), 1)
                act.wait_ge(S("t_full"), 2 * b + 2)
                nc.scalar.copy(a_lpT, bank[1][:]).then_inc(S("t_ready"), 1)
                act.wait_ge(S("ent_ready"), b + 1)
                for t in range(NT):
                    act.wait_ge(S("s_full"), NT * b + t + 1)
                    af(b_p[:, t, :], bank[2 + t][:], ACT.Exp, bias=a_nent[:, t:t + 1],
                       accum_out=b_sum[:, t:t + 1]).then_inc(S("e_ready"), 1)
                for t in range(NT):
                    act.wait_ge(S("eT_full"), NT * b + t + 1)
                    nc.scalar.copy(b_pT[:, t, :], bank[t % 2][:]).then_inc(S("eT_ready"), 1)

            def cross_attention_1(b):
                S = lambda name: sem(f"c_{name}")
                copy_zT(5, b)
                act.wait_ge(S("q_full"), b + 1)
                af(oT[:, :], bank[1][:], ACT.Identity, bias=bq).then_inc(S("q_ready"), 1)
                act.wait_ge(S("neg_ready"), b + 1)
                for t in range(NT):
                    af(b_p[:, t, 0:CTX], bank[2 + t // 2][:, t % 2 * CTX:t % 2 * CTX + CTX], ACT.Exp,
                       bias=c_neg[:, t:t + 1], scale=L1X_SCALE, accum_out=b_sum[:, t:t + 1])\
                        .then_inc(S("p_ready"), 1)
                for i in range(2):
                    act.wait_ge(S("pT_full"), 2 * b + i + 1)
                    nc.scalar.copy(b_pT[0:HC, i, :], bank[4 + i][0:HC, :]).then_inc(S("pT_ready"), 1)

            layer_norm()
            layer_norm()
            context()
            stages = [lambda b: causal_attention(0, b), cross_attention, lambda b: causal_attention(2, b),
                      lambda b: experts(3, b), divergence_attention, cross_attention_1, lambda b: experts(6, b)]
            for s, stage in enumerate(stages):
                for b in range(NB):
                    stage(b)
                    if s < 6:
                        layer_norm()
                    if s == 1:
                        layer_norm()

        @block.vector
        def _(dve):
            v = nc.vector
            own = sem("dve_own")
            own_n = [0]

            def link(ins):
                own_n[0] += 1
                ins.then_inc(own, 1)
                dve.wait_ge(own, own_n[0])

            norms = [0]

            def inverse_root(r, r0, var, tmp):
                link(v.tensor_tensor(tmp, r0, r0, ALU.mult))
                link(v.tensor_tensor(tmp, tmp, var, ALU.mult))
                link(v.tensor_scalar(tmp, tmp, -0.5, 1.5, ALU.mult, ALU.add))
                link(v.tensor_tensor(r, r0, tmp, ALU.mult))

            def layer_norm(b, src, dst, weight=None, done=None):
                norms[0] += 1
                for t in range(NT):
                    ins = v.bn_stats(ln_stats[:, t, :], src[:, NT * b + t, :])
                link(ins)
                for t in range(NT):
                    ins = v.bn_aggr(ln_mv[:, t, :], ln_stats[:, t, :])
                link(ins)
                v.tensor_scalar(ln_var[:], ln_mv[:, :, 1], EPS_LN, None, ALU.add).then_inc(log_in, 1)
                dve.wait_ge(log_out, norms[0])
                dve.wait_ge(log_in, norms[0])
                inverse_root(ln_r[:], ln_r0[:], ln_var[:], ln_t[:])
                for t in range(NT):
                    ins = v.tensor_scalar(dst[:, NT * b + t, :], src[:, NT * b + t, :], ln_mv[:, t, 0:1],
                                          ln_r[:, t:t + 1], ALU.subtract, ALU.mult)
                if weight is not None:
                    link(ins)
                    d = dst[:, tiles(b), :]
                    ins = v.tensor_tensor(d, d, weight.unsqueeze(1).to_broadcast([P, NT, P]), ALU.mult)
                if done is None:
                    link(ins)
                else:
                    ins.then_inc(done, 1)

            def next_input(s, b):
                if s == 2:
                    loaded(dve, "rows")
                    layer_norm(b, x, y)
                    layer_norm(b, y, z, ln1_w, done=z_ready)
                elif s == 3:
                    layer_norm(b, y, z, ln2_w, done=z_ready)
                else:
                    layer_norm(b, x, z, done=z_ready)

            def make_constants():
                loaded(dve, "con")
                v.tensor_copy(ident_bf[:], ident)
                v.tensor_copy(causalT_bf[:], con[:, C_CAUSALT:C_CAUSALT + P])
                v.memset(v9[:, :, :, :, HD:HD + 1], 1.0)
                v.memset(vx[:, :, :, :, XD:XD + 1], 1.0)
                v.memset(qs[:, :, TERM * HD:SLOT], 0.0)
                link(v.memset(ks[:, :, TERM * HD:SLOT], 0.0))
                v.memset(ks[:, :, TERM * HD:TERM * HD + 2], 1.0).then_inc(setup, 1)
                loaded(dve, "qk_w")
                link(v.tensor_scalar(qk_w[:, 0, :], qk_w[:, 0, :], SELF_SCALE, None, ALU.mult))
                half = HD // 2
                for i in range(2):
                    v.tensor_tensor(rope_c[:, i], cos, qk_w[:, i, :].unsqueeze(1).to_broadcast([P, NT, HD]),
                                    ALU.mult)
                    for h in range(2):
                        link(v.tensor_tensor(
                            rope_s[:, i, :, half * h:half * h + half], sin[:, :, half * h:half * h + half],
                            qk_w[:, i, half - half * h:HD - half * h].unsqueeze(1).to_broadcast([P, NT, half]),
                            ALU.mult))

            def causal_attention(s, b):
                S = lambda name: sem(f"a{s}_{name}")
                for t in range(2, NT):
                    dve.wait_ge(S("qkv_full"), NT * b + t + 1)
                    rows_t = slice(t * H, t * H + H)
                    src = bank[1 + t][:, 0:3 * P].rearrange("p (j h d) -> p j h d", j=3, h=H)
                    v.tensor_scalar(qk[:, 0, rows_t, :], src[:, 0], 1.0 if s == 0 else SELF_SCALE, None,
                                    ALU.mult)
                    v.tensor_copy(qk[:, 1, rows_t, :], src[:, 1])
                    ins = v.tensor_copy(v9[:, b, t, :, 0:HD], src[:, 2])
                ins.then_inc(S("v_ready"), 1)
                dve.wait_ge(S("v_ready"), b + 1)
                dve.wait_ge(S("qk_copied"), 2 * (b + 1))
                n = NT * H
                both = qk[:].rearrange("p i n d -> p (i n) d")
                link(v.memset(qs[:, :, TERM * HD:TERM * HD + 2], 0.0))
                if s == 0:
                    link(v.tensor_tensor(sq[:].rearrange("p i n d -> p (i n) d"), both, both, ALU.mult))
                    link(v.tensor_reduce(rms_v[:], sq[:].rearrange("p i n d -> p (i n) d"), AX, ALU.add))
                    v.tensor_scalar(rms_v[:], rms_v[:], 1.0 / HD, EPS_RMS, ALU.mult, ALU.add)\
                        .then_inc(S("rms_in"), 1)
                    dve.wait_ge(S("rms_in"), b + 1)
                    dve.wait_ge(S("rms_out"), b + 1)
                    inverse_root(rms_l[:], rms_0[:], rms_v[:], rms_t[:])
                    link(v.tensor_tensor(both, both, rms_l[:].unsqueeze(2).to_broadcast([P, 2 * n, HD]), ALU.mult))
                    half = HD // 2
                    for i in range(2):
                        for h in range(2):
                            sh = slice(half * h, half * h + half)
                            so = slice(half - half * h, HD - half * h)
                            link(v.tensor_tensor(
                                rope_b[:, i, :, sh].rearrange("p (t h) d -> p t h d", t=NT),
                                qk[:, i, :, so].rearrange("p (t h) d -> p t h d", t=NT),
                                rope_s[:, i, :, sh].unsqueeze(2).to_broadcast([P, NT, H, half]), ALU.mult))
                        q_i = qk[:, i].rearrange("p (t h) d -> p t h d", t=NT)
                        link(v.tensor_tensor(q_i, q_i, rope_c[:, i].unsqueeze(2).to_broadcast([P, NT, H, HD]),
                                             ALU.mult))
                    link(v.tensor_tensor(both, both, rope_b[:].rearrange("p i n d -> p (i n) d"), ALU.add))
                dve.sem_inc(S("qk_ready"), 1)
                dve.wait_ge(S("part1"), b + 1)
                v.tensor_tensor(rest[:, 0], qk[:, 0], qs[:, :, 0:HD], ALU.subtract)
                v.tensor_tensor(rest[:, 1], qk[:, 1], ks[:, :, 0:HD], ALU.subtract)\
                    .then_inc(S("rest1"), 1)
                dve.wait_ge(S("rest1"), b + 1)
                dve.wait_ge(S("part2"), b + 1)
                v.tensor_tensor(qs[:, :, 5 * HD:6 * HD], rest[:, 0], qs[:, :, 3 * HD:4 * HD], ALU.subtract)\
                    .then_inc(S("parts_ready"), 1)
                v.tensor_tensor(ks[:, :, 2 * HD:3 * HD], rest[:, 1], ks[:, :, HD:2 * HD], ALU.subtract)
                v.tensor_copy(ks[:, :, 3 * HD:5 * HD], ks[:, :, 0:2 * HD]).then_inc(S("parts_ready"), 1)
                v.tensor_copy(ks[:, :, 5 * HD:6 * HD], ks[:, :, 0:HD]).then_inc(S("parts_ready"), 1)

                def maxima(u):
                    g = NP * b + u
                    for i in range(8):
                        dve.wait_ge(S("raw_full"), 8 * g + i + 1)
                        if 8 * g + i >= 4:
                            dve.wait_ge(S("max_done"), 8 * g + i - 3)
                        hh, t = i % 2, i // 2
                        w = (t + 1) * P
                        v.tensor_tensor_reduce(s_scr[:, i % 4, 0:w], bank[2 + hh][:, 0:w], causal[:, TOK - w:TOK], 1.0,
                                               LOWEST, ALU.add, ALU.max, top[:, g % 2, t, hh:hh + 1])\
                            .then_inc(S("max_done"), 1)
                    dve.wait_ge(S("max_done"), 8 * (g + 1))
                    q_t = qs.rearrange("p (t h) c -> p t h c", t=NT)[:, :, 2 * u:2 * u + 2, :]
                    link(v.tensor_scalar(q_t[:, :, :, TERM * HD], top[:, g % 2], -1.0, None, ALU.mult))
                    v.scalar_tensor_tensor(q_t[:, :, :, TERM * HD + 1], top[:, g % 2], -1.0,
                                           q_t[:, :, :, TERM * HD], ALU.mult, ALU.subtract)\
                        .then_inc(S("max_ready"), 1)

                def outputs(u):
                    g = NP * b + u
                    dve.wait_ge(S("o_full"), g + 1)
                    o = bank[7][:, 0:2 * NT * (HD + 1)].rearrange("p (t h d) -> p t h d", t=NT, h=2)
                    link(v.reciprocal(rsum[:], o[:, :, :, HD]))
                    dst = o_tok[:].rearrange("p t (h d) -> p t h d", h=H)[:, :, 2 * u:2 * u + 2, :]
                    v.tensor_tensor(dst, o[:, :, :, 0:HD], rsum[:].unsqueeze(3).to_broadcast([P, NT, 2, HD]),
                                    ALU.mult).then_inc(S("o_done"), 1)

                maxima(0)
                for u in range(NP):
                    if u + 1 < NP:
                        maxima(u + 1)
                    outputs(u)
                dve.wait_ge(S("proj_full"), b + 1)
                dst = x if s == 0 else y
                v.tensor_tensor(dst[:, tiles(b), :], dst[:, tiles(b), :],
                                bank[7][:].rearrange("p (t c) -> p t c", t=NT), ALU.add).then_inc(x_added, 1)
                dve.wait_ge(x_added, 2 * s + b + 1)

            def cross_attention(b):
                S = lambda name: sem(f"x_{name}")
                n = XC * NT
                if b == 0:
                    loaded(dve, "mask")
                    link(v.tensor_scalar(mask[:], mask8[:], LOWEST, None, ALU.mult))

                def maxima(i):
                    g = n * b + i
                    t = i % NT
                    dve.wait_ge(S("s_full"), g + 1)
                    if g >= 2:
                        dve.wait_ge(S("p_ready"), g - 1)
                    for hh in range(2):
                        ins = v.tensor_tensor_reduce(xs[:, g % 2, hh, :], bank[2 * (g % 2) + hh][:, 0:CTX],
                                                     mask[:, NT * b + t, :], 1.0, LOWEST, ALU.add, ALU.max,
                                                     xtop[:, g % 2, hh:hh + 1])
                    ins.then_inc(S("max_done"), 1)
                    dve.wait_ge(S("max_done"), g + 1)
                    v.tensor_scalar(xneg[:, g % 2, :], xtop[:, g % 2, :], -X_SCALE, None, ALU.mult)\
                        .then_inc(S("neg_ready"), 1)

                def outputs(i):
                    g = n * b + i
                    c, t = i // NT, i % NT
                    dve.wait_ge(S("o_full"), g + 1)
                    o = bank[6 + g % 2][:, 0:2 * (XD + 1)].rearrange("p (h d) -> p h d", h=2)
                    link(v.reciprocal(xrs[:, g % 2], o[:, :, XD]))
                    v.tensor_tensor(ox[:, t, c, :].rearrange("p (h d) -> p h d", h=2), o[:, :, 0:XD],
                                    xrs[:, g % 2].unsqueeze(2).to_broadcast([P, 2, XD]), ALU.mult)\
                        .then_inc(S("o_done"), 1)

                for i in range(n + 3):
                    if i < n:
                        maxima(i)
                    if i >= 3:
                        outputs(i - 3)
                xb = x[:, tiles(b), :]
                loaded(dve, "rows")
                link(v.tensor_tensor(xb, xb, bo.unsqueeze(1).to_broadcast([P, NT, P]), ALU.add))
                dve.wait_ge(S("proj_full"), b + 1)
                v.tensor_tensor(xb, xb, bank[7][:].rearrange("p (t c) -> p t c", t=NT), ALU.add)\
                    .then_inc(x_added, 1)
                dve.wait_ge(x_added, 2 + b + 1)

            def experts(s, b):
                S = lambda name: sem(f"m{s}_{name}")
                dve.wait_ge(S("logit_full"), b + 1)
                src = bank[1][:, 0:NT * E].rearrange("p (t e) -> p t e", t=NT)
                if s == 3:
                    link(v.tensor_copy(logit[:], src))
                else:
                    loaded(dve, "l1r")
                    link(v.tensor_tensor(logit[:], src, rb2[:].unsqueeze(1).to_broadcast([P, NT, E]), ALU.add))
                link(v.tensor_reduce(g_max[:], logit[:], AX, ALU.max))
                v.tensor_tensor(logit[:], logit[:], g_max[:].unsqueeze(2).to_broadcast([P, NT, E]), ALU.subtract)\
                    .then_inc(S("gate_in"), 1)
                dve.wait_ge(S("gate_in"), b + 1)
                dve.wait_ge(S("gate_out"), b + 1)
                if s == 3:
                    link(v.tensor_reduce(g_sum[:], g_e[:], AX, ALU.add))
                    link(v.reciprocal(g_sum[:], g_sum[:]))
                    link(v.tensor_tensor(g_e[:], g_e[:], g_sum[:].unsqueeze(2).to_broadcast([P, NT, E]), ALU.mult))
                by = g_e if s == 3 else logit
                l = by[:].rearrange("p t e -> p (t e)")
                shape = [P, NT, E, E]
                for t in range(NT):
                    mine = by[:, t, :].unsqueeze(2).to_broadcast([P, E, E])
                    others = by[:, t, :].unsqueeze(1).to_broadcast([P, E, E])
                    v.tensor_tensor(g_cmp[:, t * E:t * E + E, :], others, mine, ALU.is_gt)
                    link(v.tensor_tensor(g_eq[:, t * E:t * E + E, :], others, mine, ALU.is_equal))
                    ge = g_eq[:, t * E:t * E + E, :]
                    ins = v.tensor_tensor(ge, ge, tri, ALU.mult)
                link(ins)
                link(v.tensor_tensor(g_cmp[:], g_cmp[:], g_eq[:], ALU.add))
                link(v.tensor_reduce(g_rank[:], g_cmp[:], AX, ALU.add))
                ge = g_e[:].rearrange("p t e -> p (t e)")
                link(v.scalar_tensor_tensor(ge, g_rank[:], 1.5, ge, ALU.is_lt, ALU.mult))
                link(v.tensor_reduce(g_sum[:], g_e[:], AX, ALU.add))
                link(v.reciprocal(g_sum[:], g_sum[:]))
                v.tensor_tensor(gate[:, b], g_e[:], g_sum[:].unsqueeze(2).to_broadcast([P, NT, E]), ALU.mult)\
                    .then_inc(S("gate_ready"), 1)
                dve.wait_ge(S("gate_ready"), b + 1)
                total = y if s == 3 else z
                for e in range(E):
                    g = E * b + e
                    dve.wait_ge(S("e_full"), g + 1)
                    for t in range(NT):
                        dst = total[:, NT * b + t, :]
                        ins = v.scalar_tensor_tensor(dst, bank[6 + g % 2][:, t * P:t * P + P], gate[:, b, t, e:e + 1],
                                                     dst, ALU.mult, ALU.add)
                    ins.then_inc(S("e_done"), 1)
                    dve.wait_ge(S("e_done"), g + 1)
                tb, xb = total[:, tiles(b), :], x[:, tiles(b), :]
                if s == 6:
                    dve.wait_ge(S("be2_full"), b + 1)
                    link(v.tensor_tensor(tb, tb, bank[1][:].rearrange("p (t c) -> p t c", t=NT), ALU.add))
                v.tensor_tensor(xb, xb, tb, ALU.add).then_inc(x_added, 1)
                dve.wait_ge(x_added, 2 * s + b + 1)

            def divergence_attention(b):
                S = lambda name: sem(f"d_{name}")
                zb = z[:, tiles(b), :]
                v.tensor_reduce(a_max[:], zb, AX, ALU.max, negate=True).then_inc(S("max_ready"), 1)
                dve.wait_ge(S("max_ready"), b + 1)
                dve.wait_ge(S("log_ready"), b + 1)
                v.tensor_tensor(a_nb[:], a_max[:], a_log[:], ALU.subtract).then_inc(S("nb_ready"), 1)
                dve.wait_ge(S("nb_ready"), b + 1)
                if b:
                    dve.wait_ge(S("t_full"), 2 * b)
                for t in range(NT):
                    v.tensor_scalar(a_lp[:, t, :], z[:, NT * b + t, :], a_nb[:, t:t + 1], None, ALU.add)\
                        .then_inc(S("lp_ready"), 1)
                dve.wait_ge(S("lp_ready"), NT * (b + 1))
                dve.wait_ge(S("p_ready"), NT * (b + 1))
                for t in range(NT):
                    ins = v.tensor_tensor_reduce(a_scr[:, t, :], a_p[:, t, :], a_lp[:, t, :], 1.0, 0.0, ALU.mult,
                                                 ALU.add, a_ent[:, t:t + 1])
                link(ins)
                v.tensor_scalar(a_nent[:], a_ent[:], -1.0, None, ALU.mult).then_inc(S("ent_ready"), 1)
                dve.wait_ge(S("e_ready"), NT * (b + 1))
                link(v.reciprocal(b_rs[:], b_sum[:]))
                dve.wait_ge(S("o_full"), b + 1)
                for t in range(NT):
                    xt = x[:, NT * b + t, :]
                    ins = v.scalar_tensor_tensor(xt, bank[7][:, t * P:t * P + P], b_rs[:, t:t + 1], xt,
                                                 ALU.mult, ALU.add)
                ins.then_inc(x_added, 1)
                dve.wait_ge(x_added, 8 + b + 1)

            def cross_attention_1(b):
                S = lambda name: sem(f"c_{name}")
                if b == 0:
                    for bb in range(NB):
                        for h in range(2):
                            link(v.tensor_tensor(v1[:, bb, h, :], v1[:, bb, h, :], bv_row[0:HC, :], ALU.add))
                dve.wait_ge(S("s_full"), b + 1)
                for i in range(2):
                    ins = v.tensor_reduce(c_max[:, 2 * i:2 * i + 2],
                                          bank[2 + i][:, 0:2 * CTX].rearrange("p (t k) -> p t k", t=2), AX, ALU.max)
                link(ins)
                v.tensor_scalar(c_neg[:], c_max[:], -L1X_SCALE, None, ALU.mult).then_inc(S("neg_ready"), 1)
                dve.wait_ge(S("p_ready"), NT * (b + 1))
                link(v.reciprocal(b_rs[:], b_sum[:]))
                dve.wait_ge(S("o_full"), b + 1)
                for t in range(NT):
                    xt = x[:, NT * b + t, :]
                    ins = v.scalar_tensor_tensor(xt, bank[7][:, t * P:t * P + P], b_rs[:, t:t + 1], xt,
                                                 ALU.mult, ALU.add)
                ins.then_inc(x_added, 1)
                dve.wait_ge(x_added, 10 + b + 1)

            loaded(dve, "x")
            for b in range(NB):
                next_input(0, b)
            make_constants()
            dve.wait_ge(pre_done, PRE)
            stages = [lambda b: causal_attention(0, b), cross_attention, lambda b: causal_attention(2, b),
                      lambda b: experts(3, b), divergence_attention, cross_attention_1, lambda b: experts(6, b)]
            for s, stage in enumerate(stages):
                for b in range(NB):
                    stage(b)
                    if s < 6:
                        next_input(s + 1, b)


PRE = NB * XC + NB * 4 + NB * 3


def zt_index(s, b):
    return 2 * s + b - (2 if s > 4 else 0)


def kernel(**inputs):
    import numpy as np
    import concourse.bacc as bacc
    from concourse.bass_utils import run_bass_kernel_spmd

    def arr(name):
        return np.asarray(inputs[name])

    con = np.zeros((P, C_END), np.float32)
    r = np.arange(P)
    con[:, C_ID:C_ID + P] = np.eye(P, dtype=np.float32)
    con[:, C_CAUSAL + TOK - P:C_CAUSAL + TOK] = np.where(r[None, :] <= r[:, None], 0.0, -3.0e38)
    con[:, C_CAUSALT:C_CAUSALT + P] = np.where(r[:, None] <= r[None, :], 0.0, -3.0e38)
    freqs = np.float32(32.0) ** (-np.arange(0, HD, 2, dtype=np.float32) / np.float32(HD))
    ang = np.arange(TOK, dtype=np.float32)[:, None] * freqs[None, :].astype(np.float32)
    cs = np.concatenate([np.cos(ang), np.cos(ang)], 1).astype(np.float32)
    sn = np.concatenate([-np.sin(ang), np.sin(ang)], 1).astype(np.float32)
    con[:, C_COS:C_COS + 32] = cs.reshape(NT, P, HD).transpose(1, 0, 2).reshape(P, 32)
    con[:, C_SIN:C_SIN + 32] = sn.reshape(NT, P, HD).transpose(1, 0, 2).reshape(P, 32)
    e = np.arange(E)
    con[:, C_TRI:C_TRI + 64] = (e[None, :] < e[:, None]).astype(np.float32).reshape(1, 64)

    cols = np.concatenate([arr("L1_xattn_bq").reshape(1, P), arr("L1_xattn_bk").reshape(1, P),
                           arr("L1_ffn_rb1").reshape(1, P), arr("L1_ffn_be1").reshape(E * F1, P)]).T
    ins = {
        "x": arr("x"), "con": con, "w_qkvT": arr("L0_attn_w_qkv").T, "w_projT": arr("L0_attn_w_proj").T,
        "qn": arr("L0_attn_q_norm_w").reshape(1, HD), "kn": arr("L0_attn_k_norm_w").reshape(1, HD),
        "ctxT": arr("ctx_1024").reshape(NB * CTX, P).T, "xWq": arr("L0_xattn_Wq"), "xWk": arr("L0_xattn_Wk"),
        "xWv": arr("L0_xattn_Wv"), "xWo": arr("L0_xattn_Wo"), "bo": arr("L0_xattn_bo").reshape(1, P),
        "mask": arr("mask_BxSxS2_bk1"), "ln1": arr("L0_ffn_ln1_w").reshape(1, P),
        "ln2": arr("L0_ffn_ln2_w").reshape(1, P), "c_attn": arr("L0_ffn_c_attn_w"),
        "c_proj": arr("L0_ffn_c_proj_w"), "router": arr("L0_ffn_router_w"), "w1": arr("L0_ffn_w1"),
        "w2": arr("L0_ffn_w2"), "l1_wqkv": np.stack([arr("L1_xattn_Wq"), arr("L1_xattn_Wk"), arr("L1_xattn_Wv")]),
        "bv": arr("L1_xattn_bv").reshape(1, P), "cols": cols, "rw1": arr("L1_ffn_rw1"), "rw2": arr("L1_ffn_rw2"),
        "rb2": arr("L1_ffn_rb2").reshape(1, E), "be2": arr("L1_ffn_be2"),
        "we1": arr("L1_ffn_we1").transpose(1, 0, 2).reshape(P, E * F1 * P),
        "we2": arr("L1_ffn_we2").reshape(E * F1 * P, P),
    }
    nc = bacc.Bacc("TRN2", target_bir_lowering=False, num_devices=1)
    arrays, aps = {}, {}
    for name, value in ins.items():
        value = np.ascontiguousarray(value)
        arrays[f"in_{name}"] = value
        aps[name] = nc.dram_tensor(f"in_{name}", value.shape, mybir.dt.from_np(value.dtype),
                                   kind="ExternalInput").ap()
    out = nc.dram_tensor("out_x", (NB, TOK, P), FP, kind="ExternalOutput").ap()
    decoder(nc, aps, out)
    result = run_bass_kernel_spmd(nc, [arrays], core_ids=[0])
    return result.results[0]["out_x"]
```

```python
from contextlib import ExitStack

import concourse.bass as bass
from concourse import mybir

P = 128
NB = 2
NT = 4
TOK = NT * P
CTX = 154
REM = CTX - P
RP = 32
HC = CTX // 2
H = 16
HD = 8
XD = 64
XC = H * XD // P
NP = H // 2
TERM = 6
SLOT = 64
E = 8
F0 = 256 // P
F1 = 512 // P
EPS_LN = 1e-5
EPS_RMS = 1e-6
LOWEST = -3.4028234663852886e38
SELF_SCALE = HD ** -0.5
X_SCALE = XD ** -0.5
L1X_SCALE = P ** -0.5

ALU = mybir.AluOpType
ACT = mybir.ActivationFunctionType
FP = mybir.dt.float32
BF = mybir.dt.bfloat16
U8 = mybir.dt.uint8
AX = mybir.AxisListType.X

CHUNKS = [[(0, 0)], [(1, 0), (3, 384)], [(2, 0)]]
PT_AT = [0, TOK, 2 * TOK, TOK + 384]

C_ID, C_CAUSAL, C_CAUSALT, C_COS, C_SIN, C_TRI, C_END = 0, 128, 640, 768, 800, 832, 896


def decoder(nc, a, out):
    with ExitStack() as ctx:
        def sb(name, shape, dt=FP):
            return ctx.enter_context(nc.sbuf_tensor(name, shape, dt))

        sems = {}

        def sem(name):
            if name not in sems:
                sems[name] = ctx.enter_context(nc.semaphore(name))
            return sems[name]

        bank = [ctx.enter_context(nc.psum_tensor(f"bank{i}", [P, 512], FP)) for i in range(8)]

        con = sb("con", [P, C_END])
        ident = con[:, C_ID:C_ID + P]
        ident_bf = sb("ident_bf", [P, P], BF)
        causal = con[:, C_CAUSAL:C_CAUSAL + TOK]
        causalT_bf = sb("causalT_bf", [P, P], BF)
        cos = con[:, C_COS:C_COS + 32].rearrange("p (t d) -> p t d", t=NT)
        sin = con[:, C_SIN:C_SIN + 32].rearrange("p (t d) -> p t d", t=NT)
        tri = con[:, C_TRI:C_TRI + 64].rearrange("p (e j) -> p e j", e=E)
        w_qkv = [sb("w_qkv0", [P, 3 * P]), sb("w_qkv2", [P, 3 * P])]
        w_proj = [sb("w_proj0", [P, P]), sb("w_proj2", [P, P])]
        qk_w = sb("qk_w", [P, 2, HD])
        early = sb("early", [P, 4, H * XD])
        wq_x, wk_x, wv_x = early[:, 0, :], early[:, 1, :], early[:, 2, :]
        wo_x = early[:, 3, :].rearrange("p (c n) -> p c n", c=XC)
        ctxT = sb("ctxT", [P, NB * CTX])
        mask8 = sb("mask8", [P, NB * NT, CTX], U8)
        mask = sb("mask", [P, NB * NT, CTX])
        rows = sb("rows", [P, 4, P])
        bo, ln1_w, ln2_w, bv_row = (rows[:, i, :] for i in range(4))
        rb2 = sb("rb2", [P, E])
        cols = sb("cols", [P, 3 + E * F1])
        bq, bk, rb1, be1 = cols[:, 0:1], cols[:, 1:2], cols[:, 2:3], cols[:, 3:3 + E * F1]
        wq_l1 = sb("wq_l1", [P, 3, P])
        router = sb("router", [P, E])
        rw1 = sb("rw1", [P, P])
        rw2 = sb("rw2", [P, E])
        be2 = sb("be2", [E, P])
        values_x = sb("values_x", [P, 2 * NB * H * XD])
        vx = values_x[:, 0:NB * H * XD].rearrange("p (b n d) -> p b n d", b=NB, n=H)
        vr = values_x[0:2 * RP, NB * H * XD:].rearrange("p (b c n) -> p b c n", b=NB, c=XC)
        w1 = [sb("w1_l0", [P, E * F0 * P]), early[:].rearrange("p a n -> p (a n)")]
        w2 = [sb("w2_l0", [P, E * F0, P]),
              values_x[:].rearrange("p (c n) -> p c n", n=P)]

        x = sb("x", [P, NB * NT, P])
        y = sb("y", [P, NB * NT, P])
        z = sb("z", [P, NB * NT, P])
        zT = sb("zT", [P, NB, TOK])
        ln_stats = sb("ln_stats", [P, NT, 6])
        ln_mv = sb("ln_mv", [P, NT, 2])
        ln_var = sb("ln_var", [P, NT])
        ln_log = sb("ln_log", [P, NT])
        ln_r0 = sb("ln_r0", [P, NT])
        ln_t = sb("ln_t", [P, NT])
        ln_r = sb("ln_r", [P, NT])

        qk = sb("qk", [P, 2, NT * H, HD])
        rest = sb("rest", [P, 2, NT * H, HD])
        sq, rope_b = rest, rest
        rms_v = sb("rms_v", [P, 2 * NT * H])
        rms_l = sb("rms_l", [P, 2 * NT * H])
        rms_0 = sb("rms_0", [P, 2 * NT * H])
        rms_t = sb("rms_t", [P, 2 * NT * H])
        rope_c = sb("rope_c", [P, 2, NT, HD])
        rope_s = sb("rope_s", [P, 2, NT, HD])
        slots = sb("slots", [P, 2, NT * H * SLOT], BF)
        qs, ks = (slots[:, i, :].rearrange("p (n c) -> p n c", c=SLOT) for i in range(2))
        v9 = sb("v9", [P, NT, H, 32])
        o_quad = sb("o_quad", [P, TOK])
        qkT = sb("qkT", [P, 2, 2 * TOK], BF)
        qmT = sb("qmT", [P, 2, TOK], BF)
        s_scr = sb("s_scr", [P, 4, TOK])
        top = sb("top", [P, 2, NT, 2])
        pT = sb("pT", [P, 2, 2, 5 * TOK // 2])
        rsum = sb("rsum", [P, NT, 4])
        o_tok = sb("o_tok", [P, NT, P])
        oT = sb("oT", [P, TOK])

        kTx = sb("kTx", [P, NB, XC, CTX])
        wide = sb("wide", [P, 8, TOK])
        qTx = oxT = hT = wide
        xtop = sb("xtop", [P, 2, 2])
        xneg = sb("xneg", [P, 2, 2])
        xsum = sb("xsum", [P, 3, 2])
        xrs = sb("xrs", [P, 3, 2])
        flat = pT[:].rearrange("p a h n -> p (a h n)")
        xpT = flat[:, 0:4 * TOK].rearrange("p (a h q) -> p a h q", a=2, h=2)
        xrT = flat[0:2 * RP, 4 * TOK:6 * TOK].rearrange("p (a q) -> p a q", a=2)
        xp = flat[:, 6 * TOK:6 * TOK + 6 * CTX].rearrange("p (a h k) -> p a h k", a=3, h=2)
        xq = flat[:, 9 * TOK + P:9 * TOK + P + 6 * RP].rearrange("p (a h k) -> p a h k", a=3, h=2)
        xs = flat[:, 8 * TOK:8 * TOK + 4 * CTX].rearrange("p (a h k) -> p a h k", a=2, h=2)

        rT = sb("rT", [P, TOK])
        logit = sb("logit", [P, NT, E])
        g_max = sb("g_max", [P, NT])
        g_e = sb("g_e", [P, NT, E])
        g_cmp = sb("g_cmp", [P, NT * E, E])
        g_eq = sb("g_eq", [P, NT * E, E])
        g_rank = sb("g_rank", [P, NT * E])
        g_sum = sb("g_sum", [P, NT])
        gate = sb("gate", [P, NB, NT, E])
        gateT = sb("gateT", [E, TOK])

        a_max = sb("a_max", [P, NT])
        a_e = wide[:, 0, :].rearrange("p (t c) -> p t c", t=NT)
        a_sum = sb("a_sum", [P, NT])
        a_log = sb("a_log", [P, NT])
        a_nb = sb("a_nb", [P, NT])
        a_p = wide[:, 1, :].rearrange("p (t c) -> p t c", t=NT)
        a_lp = wide[:, 2, :].rearrange("p (t c) -> p t c", t=NT)
        a_scr = wide[:, 3, :].rearrange("p (t c) -> p t c", t=NT)
        a_ent = sb("a_ent", [P, NT])
        a_nent = sb("a_nent", [P, NT])
        a_pT = wide[:, 4, :]
        a_lpT = wide[:, 5, :]
        b_p, b_pT = (slots[:, i, :].bitcast(FP).rearrange("p (t k) -> p t k", t=NT) for i in range(2))
        b_sum = sb("b_sum", [P, NT])
        b_rs = sb("b_rs", [P, NT])
        k1T = sb("k1T", [P, NB, CTX])
        v1 = sb("v1", [HC, NB, 2, P])
        c_max = sb("c_max", [P, NT])
        c_neg = sb("c_neg", [P, NT])

        def tiles(b):
            return slice(NT * b, NT * b + NT)

        loads = [
            ("x", x[:], a["x"].rearrange("b (t p) c -> p (b t) c", p=P)),
            ("con", con[:], a["con"]),
            ("att0", w_qkv[0][:], a["w_qkvT"]),
            ("qk_w", qk_w[:, 0, :], a["qn"].to_broadcast([P, HD])),
            ("qk_w", qk_w[:, 1, :], a["kn"].to_broadcast([P, HD])),
            ("ctx", ctxT[:], a["ctxT"]),
            ("wk_x", wk_x, a["xWk"]),
            ("wv_x", wv_x, a["xWv"]),
            ("l1kv", wq_l1[:], a["l1_wqkv"].rearrange("j p c -> p j c")),
            ("cols", cols[:], a["cols"]),
            ("rows", rows[:, 0, :], a["bo"].to_broadcast([P, P])),
            ("rows", rows[:, 1, :], a["ln1"].to_broadcast([P, P])),
            ("rows", rows[:, 2, :], a["ln2"].to_broadcast([P, P])),
            ("rows", rows[:, 3, :], a["bv"].to_broadcast([P, P])),
            ("proj0", w_proj[0][:], a["w_projT"]),
            ("mask", mask8[:], a["mask"].rearrange("b (t p) k -> p (b t) k", p=P)),
            ("wq_x", wq_x, a["xWq"]),
            ("wo_x", wo_x, a["xWo"].rearrange("(c p) n -> p c n", p=P)),
            ("att2", w_qkv[1][:], a["c_attn"]),
            ("att2", w_proj[1][:], a["c_proj"]),
            ("router", router[:], a["router"]),
            ("moe0", w1[0][:], a["w1"]),
            ("moe0", w2[0][:], a["w2"].rearrange("(c p) n -> p c n", p=P)),
            ("l1r", rw1[:], a["rw1"]),
            ("l1r", rw2[:], a["rw2"]),
            ("l1r", rb2[:], a["rb2"].to_broadcast([P, E])),
            ("l1r", be2[:], a["be2"]),
            ("moe1", w1[1], a["we1"]),
            ("moe1", w2[1], a["we2"].rearrange("(c p) n -> p c n", p=P)),
        ]
        group_size = {}
        for g, _, _ in loads:
            group_size[g] = group_size.get(g, 0) + 16

        def loaded(eng, group):
            eng.wait_ge(sem(f"load_{group}"), group_size[group])

        x_stored = sem("x_stored")
        z_ready = sem("z_ready")
        x_added = sem("x_added")
        zT_full = sem("zT_full")
        zT_ready = sem("zT_ready")
        setup = sem("setup")
        log_in, log_out = sem("log_in"), sem("log_out")
        pre_full, pre_done = sem("pre_full"), sem("pre_done")

        block = ctx.enter_context(nc.Block())

        @block.sync
        def _(sp):
            for group, dst, src in loads:
                if group == "moe1":
                    sp.wait_ge(x_added, 4)
                sp.dma_start(dst, src).then_inc(sem(f"load_{group}"), 16)
            out_v = out.rearrange("b (t p) c -> p (b t) c", p=P)
            for b in range(NB):
                sp.wait_ge(x_added, 12 + b + 1)
                sp.dma_start(out_v[:, tiles(b), :], x[:, tiles(b), :]).then_inc(x_stored, 16)
            sp.wait_ge(x_stored, 16 * NB)

        @block.tensor
        def _(pe):
            mm, tr = nc.tensor.matmul, nc.tensor.transpose

            def context():
                i = 0

                def start():
                    if i >= 4:
                        pe.wait_ge(pre_done, i - 3)
                    return bank[i % 4]
                loaded(pe, "ctx")
                loaded(pe, "wk_x")
                for b in range(NB):
                    for c in range(XC):
                        o = start()
                        mm(o[:, 0:CTX], wk_x[:, c * P:c * P + P], ctxT[:, b * CTX:b * CTX + CTX],
                           start=True, stop=True).then_inc(pre_full, 1)
                        i += 1
                loaded(pe, "wv_x")
                for b in range(NB):
                    at = b * CTX
                    for w in range(2):
                        o = start()
                        mm(o[:], ctxT[:, at:at + P], wv_x[:, 512 * w:512 * w + 512],
                           start=True, stop=True).then_inc(pre_full, 1)
                        i += 1
                    o = start()
                    by_head = wv_x.rearrange("p (c h d) -> p c h d", h=2, d=XD)
                    for h in range(2):
                        last = mm(o[RP * h:RP * h + REM, :], ctxT[:, at + P:at + CTX], by_head[:, :, h, :],
                                  start=True, stop=True)
                    last.then_inc(pre_full, 1)
                    i += 1
                loaded(pe, "l1kv")
                for b in range(NB):
                    o = start()
                    mm(o[:, 0:CTX], wq_l1[:, 1, :], ctxT[:, b * CTX:b * CTX + CTX],
                       start=True, stop=True).then_inc(pre_full, 1)
                    i += 1
                    for h in range(2):
                        o = start()
                        at = b * CTX + h * HC
                        mm(o[0:HC, 0:P], ctxT[:, at:at + HC], wq_l1[:, 2, :],
                           start=True, stop=True).then_inc(pre_full, 1)
                        i += 1

            def transpose_z(s, b):
                pe.wait_ge(z_ready, 2 * s + b + 1)
                for t in range(NT):
                    last = tr(bank[0][:, t * P:t * P + P], z[:, NT * b + t, :], ident)
                last.then_inc(zT_full, 1)
                pe.wait_ge(zT_ready, zt_index(s, b) + 1)

            def causal_attention(s, b):
                n = 0 if s == 0 else 1
                S = lambda name: sem(f"a{s}_{name}")
                transpose_z(s, b)
                loaded(pe, "att0" if s == 0 else "att2")
                if s == 2 or b == 1:
                    pe.wait_ge(x_added, 2 * s + b)
                for t in range(NT):
                    mm(bank[1 + t][:, 0:3 * P], zT[:, b, t * P:t * P + P], w_qkv[n][:],
                       start=True, stop=True).then_inc(S("qkv_full"), 1)
                pe.wait_ge(S("v_ready"), b + 1)
                pe.wait_ge(S("qk_copied"), 2 * (b + 1))

                def to_qkT(u):
                    g = NP * b + u
                    if u == 0:
                        pe.wait_ge(S("parts_ready"), 3 * (b + 1))
                    if g:
                        pe.wait_ge(S("qkT_ready"), g)
                    o = bank[1][:].bitcast(BF)
                    for i, src in enumerate((qs, ks)):
                        for t in range(NT):
                            at = t * H + 2 * u
                            last = tr(o[:, (NT * i + t) * P:(NT * i + t + 1) * P],
                                      src[:, at:at + 2, :].rearrange("p h c -> p (h c)"), ident_bf[:])
                    last.then_inc(S("qkT_full"), 1)

                def raw_scores(u, some):
                    g = NP * b + u
                    pe.wait_ge(S("qkT_ready"), g + 1)
                    for i in some:
                        n_item = 8 * g + i
                        if n_item >= 2:
                            pe.wait_ge(S("max_done"), n_item - 1)
                        hh, t = i % 2, i // 2
                        r = slice(SLOT * hh, SLOT * hh + SLOT)
                        mm(bank[2 + hh][:, 0:(t + 1) * P], qkT[r, g % 2, t * P:t * P + P],
                           qkT[r, g % 2, TOK:TOK + (t + 1) * P], start=True, stop=True)\
                            .then_inc(S("raw_full"), 1)

                def to_qmT(u):
                    g = NP * b + u
                    pe.wait_ge(S("max_ready"), g + 1)
                    if g:
                        pe.wait_ge(S("qmT_ready"), g)
                    o = bank[0][:].bitcast(BF)
                    for t in range(NT):
                        at = t * H + 2 * u
                        last = tr(o[:, t * P:t * P + P],
                                  qs[:, at:at + 2, :].rearrange("p h c -> p (h c)"), ident_bf[:])
                    last.then_inc(S("qmT_full"), 1)

                def scores(u, c):
                    g = NP * b + u
                    m = 6 * g + c
                    if m >= 3:
                        pe.wait_ge(S("pT_ready"), m - 2)
                    o = bank[4 + m % 3]
                    r = slice(SLOT * (c // 3), SLOT * (c // 3) + SLOT)
                    for j, at in CHUNKS[c % 3]:
                        q0, w = j, (NT - j) * P
                        mm(o[:, at:at + w], qkT[r, g % 2, TOK + j * P:TOK + j * P + P],
                           qmT[r, g % 2, q0 * P:TOK], start=True, stop=False)
                        last = mm(o[:, at:at + P], ident_bf[:], causalT_bf[:], start=False, stop=True)
                    last.then_inc(S("scores_full"), 1)

                def values(u, hh):
                    g = NP * b + u
                    if u % 2 == 0 and hh == 0 and g:
                        pe.wait_ge(S("o_done"), g // 2)
                    pe.wait_ge(S("pT_ready"), 6 * g + 3 * (hh + 1))
                    quarter = 32 * (2 * (u % 2) + hh)
                    for j in range(NT):
                        w = (NT - j) * P
                        last = mm(bank[7][quarter:quarter + 32, j * P:TOK], v9[:, j, 2 * u + hh, :],
                                  pT[:, g % 2, hh, PT_AT[j]:PT_AT[j] + w], start=(j == 0), stop=(j == NT - 1))
                    last.then_inc(S("o_full"), 1)

                def turn_outputs(u):
                    pe.wait_ge(S("quad_ready"), (NP * b + u + 1) // 2)
                    for t in range(NT):
                        last = tr(bank[7][:, t * P:t * P + P], o_quad[:, t * P:t * P + P], ident)
                    last.then_inc(S("quad_full"), 1)

                to_qkT(0)
                raw_scores(0, range(8))
                for u in range(NP + 1):
                    if u < NP:
                        to_qmT(u)
                    if u + 1 < NP:
                        to_qkT(u + 1)
                    if u:
                        values(u - 1, 0)
                    if u < NP:
                        pe.wait_ge(S("qmT_ready"), NP * b + u + 1)
                        for c in range(3):
                            scores(u, c)
                    if u + 1 < NP:
                        raw_scores(u + 1, range(4))
                    if u:
                        values(u - 1, 1)
                    if u < NP:
                        for c in range(3, 6):
                            scores(u, c)
                    if u + 1 < NP:
                        raw_scores(u + 1, range(4, 8))
                    if u and u % 2 == 0:
                        turn_outputs(u - 1)
                pe.wait_ge(S("o_done"), NP // 2 * (b + 1))
                for t in range(NT):
                    last = tr(bank[0][:, t * P:t * P + P], o_tok[:, t, :], ident)
                last.then_inc(S("oT_full"), 1)
                loaded(pe, "proj0" if s == 0 else "att2")
                pe.wait_ge(S("oT_ready"), b + 1)
                for t in range(NT):
                    last = mm(bank[7][:, t * P:t * P + P], oT[:, t * P:t * P + P], w_proj[n][:],
                              start=True, stop=True)
                last.then_inc(S("proj_full"), 1)

            def cross_attention(b):
                S = lambda name: sem(f"x_{name}")
                transpose_z(1, b)
                loaded(pe, "wq_x")
                pe.wait_ge(x_added, 2 + b)
                for c in range(XC):
                    n = XC * b + c
                    if c >= 2:
                        pe.wait_ge(S("q_ready"), n - 1)
                    mm(bank[c % 2][:], wq_x[:, c * P:c * P + P], zT[:, b, :], start=True, stop=True)\
                        .then_inc(S("q_full"), 1)
                pe.wait_ge(S("q_ready"), XC * (b + 1))

                def scores(i):
                    g = XC * NT * b + i
                    c, t = i // NT, i % NT
                    if g >= 2:
                        pe.wait_ge(S("max_done"), g - 1)
                    for hh in range(2):
                        r = slice(XD * hh, XD * hh + XD)
                        last = mm(bank[2 * (g % 2) + hh][:, 0:CTX], qTx[r, c, t * P:t * P + P],
                                  kTx[r, b, c, :], start=True, stop=True)
                    last.then_inc(S("s_full"), 1)

                def transposes(i):
                    g = XC * NT * b + i
                    t = i % NT
                    pe.wait_ge(S("p_normed"), g + 1)
                    if g % 2 == 0 and g >= 4:
                        pe.wait_ge(S("pT_ready"), g // 2 - 1)
                    if t == 0 and g >= 4:
                        pe.wait_ge(S("rT_ready"), g // NT)
                    o = bank[4 + g // 2 % 2]
                    for hh in range(2):
                        at = (2 * (g % 2) + hh) * P
                        last = tr(o[:, at:at + P], xp[:, g % 3, hh, 0:P], ident)
                    if g % 2:
                        last.then_inc(S("pT_full"), 1)
                    last = tr(bank[6][0:2 * RP, t * P:t * P + P], xq[:, g % 3].rearrange("p h k -> p (h k)"), ident)
                    last.then_inc(S("rT_full"), 1)

                def values(c, part):
                    g = XC * b + c
                    if part == 0:
                        pe.wait_ge(S("pT_ready"), 2 * g + 2)
                        if g:
                            pe.wait_ge(S("oT_ready"), g)
                    if part < 2:
                        mm(bank[7][XD * part:XD * part + XD, :], vx[:, b, 2 * c + part, :],
                           xpT[:, g % 2, part, :], start=True, stop=True)
                    else:
                        pe.wait_ge(S("rT_ready"), g + 1)
                        mm(bank[7][:], vr[:, b, c, :], xrT[:, g % 2, :], start=False, stop=True,
                           skip_group_check=True).then_inc(S("o_full"), 1)

                n = XC * NT
                for i in range(n + 7):
                    if i < n:
                        scores(i)
                    if 3 <= i < n + 3:
                        transposes(i - 3)
                    for part in range(3):
                        c, r = divmod(i - 8 - part, NT)
                        if r == 0 and 0 <= c < XC:
                            values(c, part)
                loaded(pe, "wo_x")
                pe.wait_ge(S("oT_ready"), XC * (b + 1))
                for t in range(NT):
                    for c in range(XC):
                        last = mm(bank[7][:, t * P:t * P + P], oxT[:, c, t * P:t * P + P], wo_x[:, c, :],
                                  start=(c == 0), stop=(c == XC - 1))
                last.then_inc(S("proj_full"), 1)

            def experts(s, b):
                n, fc = (0, F0) if s == 3 else (1, F1)
                S = lambda name: sem(f"m{s}_{name}")
                transpose_z(s, b)
                pe.wait_ge(x_added, 2 * s + b)
                if s == 3:
                    loaded(pe, "router")
                    for t in range(NT):
                        last = mm(bank[1][:, t * E:t * E + E], zT[:, b, t * P:t * P + P], router[:],
                                  start=True, stop=True)
                else:
                    loaded(pe, "l1r")
                    mm(bank[2][:], rw1[:], zT[:, b, :], start=True, stop=True).then_inc(S("r_full"), 1)
                    pe.wait_ge(S("r_ready"), b + 1)
                    for t in range(NT):
                        last = mm(bank[1][:, t * E:t * E + E], rT[:, t * P:t * P + P], rw2[:],
                                  start=True, stop=True)
                last.then_inc(S("logit_full"), 1)
                loaded(pe, "moe0" if s == 3 else "moe1")

                def hidden(e):
                    for c in range(fc):
                        m = (E * b + e) * fc + c
                        if m >= 4:
                            pe.wait_ge(S("h_ready"), m - 3)
                        f = e * fc + c
                        mm(bank[2 + m % 4][:], w1[n][:, f * P:f * P + P], zT[:, b, :],
                           start=True, stop=True).then_inc(S("h_full"), 1)

                def down(e):
                    g = E * b + e
                    pe.wait_ge(S("h_ready"), (g + 1) * fc)
                    if g >= 2:
                        pe.wait_ge(S("e_done"), g - 1)
                    for t in range(NT):
                        for c in range(fc):
                            last = mm(bank[6 + g % 2][:, t * P:t * P + P],
                                      hT[:, (g * fc + c) % 8, t * P:t * P + P], w2[n][:, e * fc + c, :],
                                      start=(c == 0), stop=(c == fc - 1))
                    last.then_inc(S("e_full"), 1)

                for e in range(E + 1):
                    if e < E:
                        hidden(e)
                    if e:
                        down(e - 1)
                if s == 6:
                    pe.wait_ge(S("gate_ready"), b + 1)
                    for t in range(NT):
                        last = tr(bank[0][0:E, t * P:t * P + P], gate[:, b, t, :], ident)
                    last.then_inc(S("gT_full"), 1)
                    pe.wait_ge(S("gT_ready"), b + 1)
                    for t in range(NT):
                        last = mm(bank[1][:, t * P:t * P + P], gateT[:, t * P:t * P + P], be2[:],
                                  start=True, stop=True)
                    last.then_inc(S("be2_full"), 1)

            def divergence_attention(b):
                S = lambda name: sem(f"d_{name}")
                pe.wait_ge(x_added, 8 + b)
                pe.wait_ge(S("p_ready"), NT * (b + 1))
                for t in range(NT):
                    last = tr(bank[0][:, t * P:t * P + P], a_p[:, t, :], ident)
                last.then_inc(S("t_full"), 1)
                pe.wait_ge(S("lp_ready"), NT * (b + 1))
                for t in range(NT):
                    last = tr(bank[1][:, t * P:t * P + P], a_lp[:, t, :], ident)
                last.then_inc(S("t_full"), 1)
                pe.wait_ge(S("t_ready"), 2 * (b + 1))
                for t in range(NT):
                    mm(bank[2 + t][:], a_pT[:, t * P:t * P + P], a_lpT, start=True, stop=True)\
                        .then_inc(S("s_full"), 1)
                for t in range(NT):
                    pe.wait_ge(S("e_ready"), NT * b + t + 1)
                    g = NT * b + t
                    if t >= 2:
                        pe.wait_ge(S("eT_ready"), g - 1)
                    for j in range(NT):
                        last = tr(bank[t % 2][:, j * P:j * P + P], b_p[:, t, j * P:j * P + P], ident)
                    last.then_inc(S("eT_full"), 1)
                for t in range(NT):
                    pe.wait_ge(S("eT_ready"), NT * b + t + 1)
                    for j in range(NT):
                        last = mm(bank[7][:, t * P:t * P + P], b_pT[:, t, j * P:j * P + P],
                                  z[:, NT * b + j, :], start=(j == 0), stop=(j == NT - 1))
                last.then_inc(S("o_full"), 1)

            def cross_attention_1(b):
                S = lambda name: sem(f"c_{name}")
                transpose_z(5, b)
                pe.wait_ge(x_added, 10 + b)
                mm(bank[1][:], wq_l1[:, 0, :], zT[:, b, :], start=True, stop=True).then_inc(S("q_full"), 1)
                pe.wait_ge(S("q_ready"), b + 1)
                for t in range(NT):
                    last = mm(bank[2 + t // 2][:, t % 2 * CTX:t % 2 * CTX + CTX], oT[:, t * P:t * P + P],
                              k1T[:, b, :], start=True, stop=True)
                last.then_inc(S("s_full"), 1)
                for t in range(NT):
                    pe.wait_ge(S("p_ready"), NT * b + t + 1)
                    o = bank[4 + t // 2]
                    for h in range(2):
                        k = 2 * (t % 2) + h
                        last = tr(o[0:HC, k * P:k * P + P], b_p[:, t, h * HC:h * HC + HC], ident)
                    if t % 2:
                        last.then_inc(S("pT_full"), 1)
                pe.wait_ge(S("pT_ready"), 2 * (b + 1))
                for t in range(NT):
                    for h in range(2):
                        k = 2 * (t % 2) + h
                        last = mm(bank[7][:, t * P:t * P + P], b_pT[0:HC, t // 2, k * P:k * P + P],
                                  v1[:, b, h, :], start=(h == 0), stop=(h == 1))
                last.then_inc(S("o_full"), 1)

            pe.wait_ge(setup, 1)
            loaded(pe, "con")
            context()
            for b in range(NB):
                if b == 0:
                    pe.wait_ge(pre_done, PRE)
                causal_attention(0, b)
            for b in range(NB):
                cross_attention(b)
            for b in range(NB):
                causal_attention(2, b)
            for b in range(NB):
                experts(3, b)
            for b in range(NB):
                divergence_attention(b)
            for b in range(NB):
                cross_attention_1(b)
            for b in range(NB):
                experts(6, b)

        @block.scalar
        def _(act):
            af = nc.scalar.activation
            own = sem("act_own")
            own_n = [0]

            def link(ins):
                own_n[0] += 1
                ins.then_inc(own, 1)
                act.wait_ge(own, own_n[0])

            norms = [0]

            def use_log_exp():
                nc.scalar.preload_act_table_set("natural_log_exp_and_others")

            def layer_norm():
                norms[0] += 1
                act.wait_ge(log_in, norms[0])
                link(af(ln_log[:], ln_var[:], ACT.Ln))
                af(ln_r0[:], ln_log[:], ACT.Exp, scale=-0.5).then_inc(log_out, 1)

            def copy_zT(s, b):
                act.wait_ge(zT_full, zt_index(s, b) + 1)
                nc.scalar.copy(zT[:, b, :], bank[0][:]).then_inc(zT_ready, 1)

            def context():
                i = 0
                for b in range(NB):
                    for c in range(XC):
                        i += 1
                        act.wait_ge(pre_full, i)
                        nc.scalar.copy(kTx[:, b, c, :], bank[(i - 1) % 4][:, 0:CTX]).then_inc(pre_done, 1)
                act.wait_ge(setup, 1)
                for b in range(NB):
                    for w in range(2):
                        i += 1
                        act.wait_ge(pre_full, i)
                        nc.scalar.copy(vx[:, b, 8 * w:8 * w + 8, :],
                                       bank[(i - 1) % 4][:].rearrange("p (h d) -> p h d", d=XD))\
                            .then_inc(pre_done, 1)
                    i += 1
                    act.wait_ge(pre_full, i)
                    for h in range(2):
                        r = slice(RP * h, RP * h + REM)
                        last = nc.scalar.copy(vr[r, b, :, XD * h:XD * h + XD],
                                              bank[(i - 1) % 4][r, :].rearrange("p (c d) -> p c d", d=XD))
                    last.then_inc(pre_done, 1)
                loaded(act, "cols")
                for b in range(NB):
                    i += 1
                    act.wait_ge(pre_full, i)
                    af(k1T[:, b, :], bank[(i - 1) % 4][:, 0:CTX], ACT.Identity, bias=bk).then_inc(pre_done, 1)
                    for h in range(2):
                        i += 1
                        act.wait_ge(pre_full, i)
                        nc.scalar.copy(v1[:, b, h, :], bank[(i - 1) % 4][0:HC, 0:P]).then_inc(pre_done, 1)

            def causal_attention(s, b):
                S = lambda name: sem(f"a{s}_{name}")
                copy_zT(s, b)
                for t in range(2):
                    act.wait_ge(S("qkv_full"), NT * b + t + 1)
                    rows_t = slice(t * H, t * H + H)
                    src = bank[1 + t][:, 0:3 * P].rearrange("p (j h d) -> p j h d", j=3, h=H)
                    af(qk[:, 0, rows_t, :], src[:, 0], ACT.Copy, scale=1.0 if s == 0 else SELF_SCALE)
                    nc.scalar.copy(qk[:, 1, rows_t, :], src[:, 1])
                    nc.scalar.copy(v9[:, t, :, 0:HD], src[:, 2]).then_inc(S("qk_copied"), 1)
                if s == 0:
                    act.wait_ge(S("rms_in"), b + 1)
                    link(af(rms_l[:], rms_v[:], ACT.Ln))
                    af(rms_0[:], rms_l[:], ACT.Exp, scale=-0.5).then_inc(S("rms_out"), 1)
                act.wait_ge(S("qk_ready"), b + 1)
                n = NT * H

                def parts(i, dst, at, times):
                    src = (qk[:, i] if at == 0 else rest[:, i]).unsqueeze(2).to_broadcast([P, n, times, HD])
                    return nc.scalar.copy(dst[:, :, at:at + times * HD].rearrange("p n (r d) -> p n r d", r=times), src)

                parts(0, qs, 0, 3)
                parts(1, ks, 0, 1).then_inc(S("part1"), 1)
                act.wait_ge(S("rest1"), b + 1)
                parts(0, qs, 3 * HD, 2)
                parts(1, ks, HD, 1).then_inc(S("part2"), 1)

                def copy_qkT(u):
                    g = NP * b + u
                    act.wait_ge(S("qkT_full"), g + 1)
                    nc.scalar.copy(qkT[:, g % 2, :], bank[1][:].bitcast(BF)).then_inc(S("qkT_ready"), 1)

                def copy_qmT(u):
                    g = NP * b + u
                    act.wait_ge(S("qmT_full"), g + 1)
                    nc.scalar.copy(qmT[:, g % 2, :], bank[0][:].bitcast(BF)[:, 0:TOK])\
                        .then_inc(S("qmT_ready"), 1)

                def copy_quad(u):
                    act.wait_ge(S("o_full"), 2 * (NP * b + u + 1))
                    nc.scalar.copy(o_quad[:], bank[7][:]).then_inc(S("quad_ready"), 1)

                copy_qkT(0)
                for u in range(NP):
                    g = NP * b + u
                    copy_qmT(u)
                    if u + 1 < NP:
                        copy_qkT(u + 1)
                    for c in range(6):
                        if g >= 2 and c % 3 == 0:
                            act.wait_ge(S("o_full"), 2 * g - 3 + c // 3)
                        m = 6 * g + c
                        act.wait_ge(S("scores_full"), m + 1)
                        at, w = TOK * (c % 3), TOK if c % 3 < 2 else TOK // 2
                        af(pT[:, g % 2, c // 3, at:at + w], bank[4 + m % 3][:, 0:w], ACT.Exp)\
                            .then_inc(S("pT_ready"), 1)
                        if c == 3 and u and u % 2 == 0:
                            copy_quad(u - 1)
                copy_quad(NP - 1)
                act.wait_ge(S("oT_full"), b + 1)
                nc.scalar.copy(oT[:, :], bank[0][:]).then_inc(S("oT_ready"), 1)

            def cross_attention(b):
                S = lambda name: sem(f"x_{name}")
                copy_zT(1, b)
                for c in range(XC):
                    act.wait_ge(S("q_full"), XC * b + c + 1)
                    nc.scalar.copy(qTx[:, c, :], bank[c % 2][:]).then_inc(S("q_ready"), 1)
                n = XC * NT

                def exps(i):
                    g = n * b + i
                    act.wait_ge(S("neg_ready"), g + 1)
                    if g >= 3:
                        act.wait_ge(S("rT_full"), g - 2)
                    for hh in range(2):
                        last = af(xp[:, g % 3, hh, 0:CTX], xs[:, g % 2, hh, :], ACT.Exp,
                                  bias=xneg[:, g % 2, hh:hh + 1], scale=X_SCALE,
                                  accum_out=xsum[:, g % 3, hh:hh + 1])
                    last.then_inc(S("p_ready"), 1)

                def copy_pT(k):
                    g = n // 2 * b + k
                    act.wait_ge(S("pT_full"), g + 1)
                    if g >= 4:
                        act.wait_ge(S("o_full"), g // 2 - 1)
                    at = g % 2 * 2 * P
                    nc.scalar.copy(xpT[:, g // 2 % 2, :, at:at + 2 * P].rearrange("p h (t q) -> p t h q", t=2),
                                   bank[4 + g % 2][:].rearrange("p (t h q) -> p t h q", t=2, h=2))\
                        .then_inc(S("pT_ready"), 1)

                for i in range(n + 2):
                    if i < n:
                        exps(i)
                    if i >= 3 and i % 2:
                        copy_pT((i - 3) // 2)

            def experts(s, b):
                fc = F0 if s == 3 else F1
                S = lambda name: sem(f"m{s}_{name}")
                copy_zT(s, b)
                if s == 6:
                    act.wait_ge(S("r_full"), b + 1)
                    af(rT[:], bank[2][:], ACT.Silu, bias=rb1).then_inc(S("r_ready"), 1)
                act.wait_ge(S("gate_in"), b + 1)
                af(g_e[:], logit[:], ACT.Exp).then_inc(S("gate_out"), 1)
                for e in range(E):
                    for c in range(fc):
                        m = (E * b + e) * fc + c
                        act.wait_ge(S("h_full"), m + 1)
                        if m >= 8:
                            act.wait_ge(S("e_full"), (m - 8) // fc + 1)
                        f = e * fc + c
                        if s == 3:
                            ins = af(hT[:, m % 8, :], bank[2 + m % 4][:], ACT.Gelu)
                        else:
                            ins = af(hT[:, m % 8, :], bank[2 + m % 4][:], ACT.Silu, bias=be1[:, f:f + 1])
                        ins.then_inc(S("h_ready"), 1)
                use_log_exp()
                if s == 6:
                    act.wait_ge(S("gT_full"), b + 1)
                    nc.scalar.copy(gateT[:], bank[0][0:E, :]).then_inc(S("gT_ready"), 1)

            def divergence_attention(b):
                S = lambda name: sem(f"d_{name}")
                act.wait_ge(S("max_ready"), b + 1)
                for t in range(NT):
                    ins = af(a_e[:, t, :], z[:, NT * b + t, :], ACT.Exp, bias=a_max[:, t:t + 1],
                             accum_out=a_sum[:, t:t + 1])
                link(ins)
                af(a_log[:], a_sum[:], ACT.Ln).then_inc(S("log_ready"), 1)
                act.wait_ge(S("nb_ready"), b + 1)
                if b:
                    act.wait_ge(S("t_full"), 2 * b)
                for t in range(NT):
                    af(a_p[:, t, :], z[:, NT * b + t, :], ACT.Exp, bias=a_nb[:, t:t + 1])\
                        .then_inc(S("p_ready"), 1)
                act.wait_ge(S("t_full"), 2 * b + 1)
                nc.scalar.copy(a_pT, bank[0][:]).then_inc(S("t_ready"), 1)
                act.wait_ge(S("t_full"), 2 * b + 2)
                nc.scalar.copy(a_lpT, bank[1][:]).then_inc(S("t_ready"), 1)
                act.wait_ge(S("ent_ready"), b + 1)
                for t in range(NT):
                    act.wait_ge(S("s_full"), NT * b + t + 1)
                    af(b_p[:, t, :], bank[2 + t][:], ACT.Exp, bias=a_nent[:, t:t + 1],
                       accum_out=b_sum[:, t:t + 1]).then_inc(S("e_ready"), 1)
                for t in range(NT):
                    act.wait_ge(S("eT_full"), NT * b + t + 1)
                    nc.scalar.copy(b_pT[:, t, :], bank[t % 2][:]).then_inc(S("eT_ready"), 1)

            def cross_attention_1(b):
                S = lambda name: sem(f"c_{name}")
                copy_zT(5, b)
                act.wait_ge(S("q_full"), b + 1)
                af(oT[:, :], bank[1][:], ACT.Identity, bias=bq).then_inc(S("q_ready"), 1)
                act.wait_ge(S("neg_ready"), b + 1)
                for t in range(NT):
                    af(b_p[:, t, 0:CTX], bank[2 + t // 2][:, t % 2 * CTX:t % 2 * CTX + CTX], ACT.Exp,
                       bias=c_neg[:, t:t + 1], scale=L1X_SCALE, accum_out=b_sum[:, t:t + 1])\
                        .then_inc(S("p_ready"), 1)
                for i in range(2):
                    act.wait_ge(S("pT_full"), 2 * b + i + 1)
                    nc.scalar.copy(b_pT[0:HC, i, :], bank[4 + i][0:HC, :]).then_inc(S("pT_ready"), 1)

            use_log_exp()
            layer_norm()
            layer_norm()
            context()
            stages = [lambda b: causal_attention(0, b), cross_attention, lambda b: causal_attention(2, b),
                      lambda b: experts(3, b), divergence_attention, cross_attention_1, lambda b: experts(6, b)]
            for s, stage in enumerate(stages):
                for b in range(NB):
                    stage(b)
                    if s < 6:
                        layer_norm()
                    if s == 1:
                        layer_norm()

        @block.vector
        def _(dve):
            v = nc.vector
            own = sem("dve_own")
            own_n = [0]

            def link(ins):
                own_n[0] += 1
                ins.then_inc(own, 1)
                dve.wait_ge(own, own_n[0])

            norms = [0]

            def inverse_root(r, r0, var, tmp):
                link(v.tensor_tensor(tmp, r0, r0, ALU.mult))
                link(v.tensor_tensor(tmp, tmp, var, ALU.mult))
                link(v.tensor_scalar(tmp, tmp, -0.5, 1.5, ALU.mult, ALU.add))
                link(v.tensor_tensor(r, r0, tmp, ALU.mult))

            def layer_norm(b, src, dst, weight=None, done=None):
                norms[0] += 1
                for t in range(NT):
                    ins = v.bn_stats(ln_stats[:, t, :], src[:, NT * b + t, :])
                link(ins)
                for t in range(NT):
                    ins = v.bn_aggr(ln_mv[:, t, :], ln_stats[:, t, :])
                link(ins)
                v.tensor_scalar(ln_var[:], ln_mv[:, :, 1], EPS_LN, None, ALU.add).then_inc(log_in, 1)
                dve.wait_ge(log_out, norms[0])
                dve.wait_ge(log_in, norms[0])
                inverse_root(ln_r[:], ln_r0[:], ln_var[:], ln_t[:])
                for t in range(NT):
                    ins = v.tensor_scalar(dst[:, NT * b + t, :], src[:, NT * b + t, :], ln_mv[:, t, 0:1],
                                          ln_r[:, t:t + 1], ALU.subtract, ALU.mult)
                if weight is not None:
                    link(ins)
                    d = dst[:, tiles(b), :]
                    ins = v.tensor_tensor(d, d, weight.unsqueeze(1).to_broadcast([P, NT, P]), ALU.mult)
                if done is None:
                    link(ins)
                else:
                    ins.then_inc(done, 1)

            def next_input(s, b):
                if s == 2:
                    loaded(dve, "rows")
                    layer_norm(b, x, y)
                    layer_norm(b, y, z, ln1_w, done=z_ready)
                elif s == 3:
                    layer_norm(b, y, z, ln2_w, done=z_ready)
                else:
                    layer_norm(b, x, z, done=z_ready)

            def make_constants():
                loaded(dve, "con")
                v.tensor_copy(ident_bf[:], ident)
                v.tensor_copy(causalT_bf[:], con[:, C_CAUSALT:C_CAUSALT + P])
                link(v.memset(v9[:, :, :, HD:32], 0.0))
                v.memset(v9[:, :, :, HD:HD + 1], 1.0)
                v.memset(vr, 0.0)
                v.memset(qs[:, :, TERM * HD:SLOT], 0.0)
                link(v.memset(ks[:, :, TERM * HD:SLOT], 0.0))
                v.memset(ks[:, :, TERM * HD:TERM * HD + 2], 1.0).then_inc(setup, 1)
                loaded(dve, "qk_w")
                link(v.tensor_scalar(qk_w[:, 0, :], qk_w[:, 0, :], SELF_SCALE, None, ALU.mult))
                half = HD // 2
                for i in range(2):
                    v.tensor_tensor(rope_c[:, i], cos, qk_w[:, i, :].unsqueeze(1).to_broadcast([P, NT, HD]),
                                    ALU.mult)
                    for h in range(2):
                        link(v.tensor_tensor(
                            rope_s[:, i, :, half * h:half * h + half], sin[:, :, half * h:half * h + half],
                            qk_w[:, i, half - half * h:HD - half * h].unsqueeze(1).to_broadcast([P, NT, half]),
                            ALU.mult))

            def causal_attention(s, b):
                S = lambda name: sem(f"a{s}_{name}")
                for t in range(2, NT):
                    dve.wait_ge(S("qkv_full"), NT * b + t + 1)
                    rows_t = slice(t * H, t * H + H)
                    src = bank[1 + t][:, 0:3 * P].rearrange("p (j h d) -> p j h d", j=3, h=H)
                    v.tensor_scalar(qk[:, 0, rows_t, :], src[:, 0], 1.0 if s == 0 else SELF_SCALE, None,
                                    ALU.mult)
                    v.tensor_copy(qk[:, 1, rows_t, :], src[:, 1])
                    ins = v.tensor_copy(v9[:, t, :, 0:HD], src[:, 2])
                ins.then_inc(S("v_ready"), 1)
                dve.wait_ge(S("v_ready"), b + 1)
                dve.wait_ge(S("qk_copied"), 2 * (b + 1))
                n = NT * H
                both = qk[:].rearrange("p i n d -> p (i n) d")
                link(v.memset(qs[:, :, TERM * HD:TERM * HD + 2], 0.0))
                if s == 0:
                    link(v.tensor_tensor(sq[:].rearrange("p i n d -> p (i n) d"), both, both, ALU.mult))
                    link(v.tensor_reduce(rms_v[:], sq[:].rearrange("p i n d -> p (i n) d"), AX, ALU.add))
                    v.tensor_scalar(rms_v[:], rms_v[:], 1.0 / HD, EPS_RMS, ALU.mult, ALU.add)\
                        .then_inc(S("rms_in"), 1)
                    dve.wait_ge(S("rms_in"), b + 1)
                    dve.wait_ge(S("rms_out"), b + 1)
                    inverse_root(rms_l[:], rms_0[:], rms_v[:], rms_t[:])
                    link(v.tensor_tensor(both, both, rms_l[:].unsqueeze(2).to_broadcast([P, 2 * n, HD]), ALU.mult))
                    half = HD // 2
                    for i in range(2):
                        for h in range(2):
                            sh = slice(half * h, half * h + half)
                            so = slice(half - half * h, HD - half * h)
                            link(v.tensor_tensor(
                                rope_b[:, i, :, sh].rearrange("p (t h) d -> p t h d", t=NT),
                                qk[:, i, :, so].rearrange("p (t h) d -> p t h d", t=NT),
                                rope_s[:, i, :, sh].unsqueeze(2).to_broadcast([P, NT, H, half]), ALU.mult))
                        q_i = qk[:, i].rearrange("p (t h) d -> p t h d", t=NT)
                        link(v.tensor_tensor(q_i, q_i, rope_c[:, i].unsqueeze(2).to_broadcast([P, NT, H, HD]),
                                             ALU.mult))
                    link(v.tensor_tensor(both, both, rope_b[:].rearrange("p i n d -> p (i n) d"), ALU.add))
                dve.sem_inc(S("qk_ready"), 1)
                dve.wait_ge(S("part1"), b + 1)
                v.tensor_tensor(rest[:, 0], qk[:, 0], qs[:, :, 0:HD], ALU.subtract)
                v.tensor_tensor(rest[:, 1], qk[:, 1], ks[:, :, 0:HD], ALU.subtract)\
                    .then_inc(S("rest1"), 1)
                dve.wait_ge(S("rest1"), b + 1)
                dve.wait_ge(S("part2"), b + 1)
                v.tensor_tensor(qs[:, :, 5 * HD:6 * HD], rest[:, 0], qs[:, :, 3 * HD:4 * HD], ALU.subtract)\
                    .then_inc(S("parts_ready"), 1)
                v.tensor_tensor(ks[:, :, 2 * HD:3 * HD], rest[:, 1], ks[:, :, HD:2 * HD], ALU.subtract)
                v.tensor_copy(ks[:, :, 3 * HD:5 * HD], ks[:, :, 0:2 * HD]).then_inc(S("parts_ready"), 1)
                v.tensor_copy(ks[:, :, 5 * HD:6 * HD], ks[:, :, 0:HD]).then_inc(S("parts_ready"), 1)

                def maxima(u):
                    g = NP * b + u
                    for i in range(8):
                        dve.wait_ge(S("raw_full"), 8 * g + i + 1)
                        if 8 * g + i >= 4:
                            dve.wait_ge(S("max_done"), 8 * g + i - 3)
                        hh, t = i % 2, i // 2
                        w = (t + 1) * P
                        v.tensor_tensor_reduce(s_scr[:, i % 4, 0:w], bank[2 + hh][:, 0:w], causal[:, TOK - w:TOK], 1.0,
                                               LOWEST, ALU.add, ALU.max, top[:, g % 2, t, hh:hh + 1])\
                            .then_inc(S("max_done"), 1)
                    dve.wait_ge(S("max_done"), 8 * (g + 1))
                    q_t = qs.rearrange("p (t h) c -> p t h c", t=NT)[:, :, 2 * u:2 * u + 2, :]
                    link(v.tensor_scalar(q_t[:, :, :, TERM * HD], top[:, g % 2], -1.0, None, ALU.mult))
                    v.scalar_tensor_tensor(q_t[:, :, :, TERM * HD + 1], top[:, g % 2], -1.0,
                                           q_t[:, :, :, TERM * HD], ALU.mult, ALU.subtract)\
                        .then_inc(S("max_ready"), 1)

                def outputs(k):
                    dve.wait_ge(S("quad_full"), NP // 2 * b + k + 1)
                    o = bank[7][:].rearrange("p (t h d) -> p t h d", t=NT, h=4)
                    link(v.reciprocal(rsum[:], o[:, :, :, HD]))
                    dst = o_tok[:].rearrange("p t (h d) -> p t h d", h=H)[:, :, 4 * k:4 * k + 4, :]
                    v.tensor_tensor(dst, o[:, :, :, 0:HD], rsum[:].unsqueeze(3).to_broadcast([P, NT, 4, HD]),
                                    ALU.mult).then_inc(S("o_done"), 1)

                maxima(0)
                for u in range(NP + 1):
                    if u + 1 < NP:
                        maxima(u + 1)
                    if u and u % 2 == 0:
                        outputs(u // 2 - 1)
                dve.wait_ge(S("proj_full"), b + 1)
                dst = x if s == 0 else y
                v.tensor_tensor(dst[:, tiles(b), :], dst[:, tiles(b), :],
                                bank[7][:].rearrange("p (t c) -> p t c", t=NT), ALU.add).then_inc(x_added, 1)
                dve.wait_ge(x_added, 2 * s + b + 1)

            def cross_attention(b):
                S = lambda name: sem(f"x_{name}")
                n = XC * NT
                if b == 0:
                    loaded(dve, "mask")
                    v.memset(xq, 0.0)
                    link(v.tensor_scalar(mask[:], mask8[:], LOWEST, None, ALU.mult))

                def maxima(i):
                    g = n * b + i
                    t = i % NT
                    dve.wait_ge(S("s_full"), g + 1)
                    if g >= 2:
                        dve.wait_ge(S("p_ready"), g - 1)
                    for hh in range(2):
                        ins = v.tensor_tensor_reduce(xs[:, g % 2, hh, :], bank[2 * (g % 2) + hh][:, 0:CTX],
                                                     mask[:, NT * b + t, :], 1.0, LOWEST, ALU.add, ALU.max,
                                                     xtop[:, g % 2, hh:hh + 1])
                    ins.then_inc(S("max_done"), 1)
                    dve.wait_ge(S("max_done"), g + 1)
                    v.tensor_scalar(xneg[:, g % 2, :], xtop[:, g % 2, :], -X_SCALE, None, ALU.mult)\
                        .then_inc(S("neg_ready"), 1)

                def norm(i):
                    g = n * b + i
                    dve.wait_ge(S("p_ready"), g + 1)
                    link(v.reciprocal(xrs[:, g % 3, :], xsum[:, g % 3, :]))
                    v.tensor_tensor(xq[:, g % 3, :, 0:REM], xp[:, g % 3, :, P:CTX],
                                    xrs[:, g % 3, :].unsqueeze(2).to_broadcast([P, 2, REM]), ALU.mult)
                    for hh in range(2):
                        p = xp[:, g % 3, hh, 0:P]
                        ins = v.tensor_scalar(p, p, xrs[:, g % 3, hh:hh + 1], None, ALU.mult)
                    ins.then_inc(S("p_normed"), 1)

                def copy_rT(c):
                    g = XC * b + c
                    dve.wait_ge(S("rT_full"), NT * (g + 1))
                    if g >= 2:
                        dve.wait_ge(S("o_full"), g - 1)
                    v.tensor_copy(xrT[:, g % 2, :], bank[6][0:2 * RP, :]).then_inc(S("rT_ready"), 1)

                def copy_oT(c):
                    g = XC * b + c
                    dve.wait_ge(S("o_full"), g + 1)
                    v.tensor_copy(oxT[:, c, :], bank[7][:]).then_inc(S("oT_ready"), 1)

                for i in range(n + 12):
                    if i < n:
                        maxima(i)
                    if 1 <= i < n + 1:
                        norm(i - 1)
                    c, r = divmod(i - 7, NT)
                    if r == 0 and 0 <= c < XC:
                        copy_rT(c)
                    c, r = divmod(i - 11, NT)
                    if r == 0 and 0 <= c < XC:
                        copy_oT(c)
                xb = x[:, tiles(b), :]
                loaded(dve, "rows")
                link(v.tensor_tensor(xb, xb, bo.unsqueeze(1).to_broadcast([P, NT, P]), ALU.add))
                dve.wait_ge(S("proj_full"), b + 1)
                v.tensor_tensor(xb, xb, bank[7][:].rearrange("p (t c) -> p t c", t=NT), ALU.add)\
                    .then_inc(x_added, 1)
                dve.wait_ge(x_added, 2 + b + 1)

            def experts(s, b):
                S = lambda name: sem(f"m{s}_{name}")
                dve.wait_ge(S("logit_full"), b + 1)
                src = bank[1][:, 0:NT * E].rearrange("p (t e) -> p t e", t=NT)
                if s == 3:
                    link(v.tensor_copy(logit[:], src))
                else:
                    loaded(dve, "l1r")
                    link(v.tensor_tensor(logit[:], src, rb2[:].unsqueeze(1).to_broadcast([P, NT, E]), ALU.add))
                link(v.tensor_reduce(g_max[:], logit[:], AX, ALU.max))
                v.tensor_tensor(logit[:], logit[:], g_max[:].unsqueeze(2).to_broadcast([P, NT, E]), ALU.subtract)\
                    .then_inc(S("gate_in"), 1)
                dve.wait_ge(S("gate_in"), b + 1)
                dve.wait_ge(S("gate_out"), b + 1)
                if s == 3:
                    link(v.tensor_reduce(g_sum[:], g_e[:], AX, ALU.add))
                    link(v.reciprocal(g_sum[:], g_sum[:]))
                    link(v.tensor_tensor(g_e[:], g_e[:], g_sum[:].unsqueeze(2).to_broadcast([P, NT, E]), ALU.mult))
                by = g_e if s == 3 else logit
                l = by[:].rearrange("p t e -> p (t e)")
                shape = [P, NT, E, E]
                for t in range(NT):
                    mine = by[:, t, :].unsqueeze(2).to_broadcast([P, E, E])
                    others = by[:, t, :].unsqueeze(1).to_broadcast([P, E, E])
                    v.tensor_tensor(g_cmp[:, t * E:t * E + E, :], others, mine, ALU.is_gt)
                    link(v.tensor_tensor(g_eq[:, t * E:t * E + E, :], others, mine, ALU.is_equal))
                    ge = g_eq[:, t * E:t * E + E, :]
                    ins = v.tensor_tensor(ge, ge, tri, ALU.mult)
                link(ins)
                link(v.tensor_tensor(g_cmp[:], g_cmp[:], g_eq[:], ALU.add))
                link(v.tensor_reduce(g_rank[:], g_cmp[:], AX, ALU.add))
                ge = g_e[:].rearrange("p t e -> p (t e)")
                link(v.scalar_tensor_tensor(ge, g_rank[:], 1.5, ge, ALU.is_lt, ALU.mult))
                link(v.tensor_reduce(g_sum[:], g_e[:], AX, ALU.add))
                link(v.reciprocal(g_sum[:], g_sum[:]))
                v.tensor_tensor(gate[:, b], g_e[:], g_sum[:].unsqueeze(2).to_broadcast([P, NT, E]), ALU.mult)\
                    .then_inc(S("gate_ready"), 1)
                dve.wait_ge(S("gate_ready"), b + 1)
                total = y if s == 3 else z
                for e in range(E):
                    g = E * b + e
                    dve.wait_ge(S("e_full"), g + 1)
                    for t in range(NT):
                        dst = total[:, NT * b + t, :]
                        ins = v.scalar_tensor_tensor(dst, bank[6 + g % 2][:, t * P:t * P + P], gate[:, b, t, e:e + 1],
                                                     dst, ALU.mult, ALU.add)
                    ins.then_inc(S("e_done"), 1)
                    dve.wait_ge(S("e_done"), g + 1)
                tb, xb = total[:, tiles(b), :], x[:, tiles(b), :]
                if s == 6:
                    dve.wait_ge(S("be2_full"), b + 1)
                    link(v.tensor_tensor(tb, tb, bank[1][:].rearrange("p (t c) -> p t c", t=NT), ALU.add))
                v.tensor_tensor(xb, xb, tb, ALU.add).then_inc(x_added, 1)
                dve.wait_ge(x_added, 2 * s + b + 1)

            def divergence_attention(b):
                S = lambda name: sem(f"d_{name}")
                zb = z[:, tiles(b), :]
                v.tensor_reduce(a_max[:], zb, AX, ALU.max, negate=True).then_inc(S("max_ready"), 1)
                dve.wait_ge(S("max_ready"), b + 1)
                dve.wait_ge(S("log_ready"), b + 1)
                v.tensor_tensor(a_nb[:], a_max[:], a_log[:], ALU.subtract).then_inc(S("nb_ready"), 1)
                dve.wait_ge(S("nb_ready"), b + 1)
                if b:
                    dve.wait_ge(S("t_full"), 2 * b)
                for t in range(NT):
                    v.tensor_scalar(a_lp[:, t, :], z[:, NT * b + t, :], a_nb[:, t:t + 1], None, ALU.add)\
                        .then_inc(S("lp_ready"), 1)
                dve.wait_ge(S("lp_ready"), NT * (b + 1))
                dve.wait_ge(S("p_ready"), NT * (b + 1))
                for t in range(NT):
                    ins = v.tensor_tensor_reduce(a_scr[:, t, :], a_p[:, t, :], a_lp[:, t, :], 1.0, 0.0, ALU.mult,
                                                 ALU.add, a_ent[:, t:t + 1])
                link(ins)
                v.tensor_scalar(a_nent[:], a_ent[:], -1.0, None, ALU.mult).then_inc(S("ent_ready"), 1)
                dve.wait_ge(S("e_ready"), NT * (b + 1))
                link(v.reciprocal(b_rs[:], b_sum[:]))
                dve.wait_ge(S("o_full"), b + 1)
                for t in range(NT):
                    xt = x[:, NT * b + t, :]
                    ins = v.scalar_tensor_tensor(xt, bank[7][:, t * P:t * P + P], b_rs[:, t:t + 1], xt,
                                                 ALU.mult, ALU.add)
                ins.then_inc(x_added, 1)
                dve.wait_ge(x_added, 8 + b + 1)

            def cross_attention_1(b):
                S = lambda name: sem(f"c_{name}")
                if b == 0:
                    for bb in range(NB):
                        for h in range(2):
                            link(v.tensor_tensor(v1[:, bb, h, :], v1[:, bb, h, :], bv_row[0:HC, :], ALU.add))
                dve.wait_ge(S("s_full"), b + 1)
                for i in range(2):
                    ins = v.tensor_reduce(c_max[:, 2 * i:2 * i + 2],
                                          bank[2 + i][:, 0:2 * CTX].rearrange("p (t k) -> p t k", t=2), AX, ALU.max)
                link(ins)
                v.tensor_scalar(c_neg[:], c_max[:], -L1X_SCALE, None, ALU.mult).then_inc(S("neg_ready"), 1)
                dve.wait_ge(S("p_ready"), NT * (b + 1))
                link(v.reciprocal(b_rs[:], b_sum[:]))
                dve.wait_ge(S("o_full"), b + 1)
                for t in range(NT):
                    xt = x[:, NT * b + t, :]
                    ins = v.scalar_tensor_tensor(xt, bank[7][:, t * P:t * P + P], b_rs[:, t:t + 1], xt,
                                                 ALU.mult, ALU.add)
                ins.then_inc(x_added, 1)
                dve.wait_ge(x_added, 10 + b + 1)

            loaded(dve, "x")
            for b in range(NB):
                next_input(0, b)
            make_constants()
            dve.wait_ge(pre_done, PRE)
            stages = [lambda b: causal_attention(0, b), cross_attention, lambda b: causal_attention(2, b),
                      lambda b: experts(3, b), divergence_attention, cross_attention_1, lambda b: experts(6, b)]
            for s, stage in enumerate(stages):
                for b in range(NB):
                    stage(b)
                    if s < 6:
                        next_input(s + 1, b)


PRE = NB * (XC + 3 + 3)


def zt_index(s, b):
    return 2 * s + b - (2 if s > 4 else 0)


def kernel(**inputs):
    import numpy as np
    import concourse.bacc as bacc
    from concourse.bass_utils import run_bass_kernel_spmd

    def arr(name):
        return np.asarray(inputs[name])

    con = np.zeros((P, C_END), np.float32)
    r = np.arange(P)
    con[:, C_ID:C_ID + P] = np.eye(P, dtype=np.float32)
    con[:, C_CAUSAL + TOK - P:C_CAUSAL + TOK] = np.where(r[None, :] <= r[:, None], 0.0, -3.0e38)
    con[:, C_CAUSALT:C_CAUSALT + P] = np.where(r[:, None] <= r[None, :], 0.0, -3.0e38)
    freqs = np.float32(32.0) ** (-np.arange(0, HD, 2, dtype=np.float32) / np.float32(HD))
    ang = np.arange(TOK, dtype=np.float32)[:, None] * freqs[None, :].astype(np.float32)
    cs = np.concatenate([np.cos(ang), np.cos(ang)], 1).astype(np.float32)
    sn = np.concatenate([-np.sin(ang), np.sin(ang)], 1).astype(np.float32)
    con[:, C_COS:C_COS + 32] = cs.reshape(NT, P, HD).transpose(1, 0, 2).reshape(P, 32)
    con[:, C_SIN:C_SIN + 32] = sn.reshape(NT, P, HD).transpose(1, 0, 2).reshape(P, 32)
    e = np.arange(E)
    con[:, C_TRI:C_TRI + 64] = (e[None, :] < e[:, None]).astype(np.float32).reshape(1, 64)

    cols = np.concatenate([arr("L1_xattn_bq").reshape(1, P), arr("L1_xattn_bk").reshape(1, P),
                           arr("L1_ffn_rb1").reshape(1, P), arr("L1_ffn_be1").reshape(E * F1, P)]).T
    ins = {
        "x": arr("x"), "con": con, "w_qkvT": arr("L0_attn_w_qkv").T, "w_projT": arr("L0_attn_w_proj").T,
        "qn": arr("L0_attn_q_norm_w").reshape(1, HD), "kn": arr("L0_attn_k_norm_w").reshape(1, HD),
        "ctxT": arr("ctx_1024").reshape(NB * CTX, P).T, "xWq": arr("L0_xattn_Wq"), "xWk": arr("L0_xattn_Wk"),
        "xWv": arr("L0_xattn_Wv"), "xWo": arr("L0_xattn_Wo"), "bo": arr("L0_xattn_bo").reshape(1, P),
        "mask": arr("mask_BxSxS2_bk1"), "ln1": arr("L0_ffn_ln1_w").reshape(1, P),
        "ln2": arr("L0_ffn_ln2_w").reshape(1, P), "c_attn": arr("L0_ffn_c_attn_w"),
        "c_proj": arr("L0_ffn_c_proj_w"), "router": arr("L0_ffn_router_w"), "w1": arr("L0_ffn_w1"),
        "w2": arr("L0_ffn_w2"), "l1_wqkv": np.stack([arr("L1_xattn_Wq"), arr("L1_xattn_Wk"), arr("L1_xattn_Wv")]),
        "bv": arr("L1_xattn_bv").reshape(1, P), "cols": cols, "rw1": arr("L1_ffn_rw1"), "rw2": arr("L1_ffn_rw2"),
        "rb2": arr("L1_ffn_rb2").reshape(1, E), "be2": arr("L1_ffn_be2"),
        "we1": arr("L1_ffn_we1").transpose(1, 0, 2).reshape(P, E * F1 * P),
        "we2": arr("L1_ffn_we2").reshape(E * F1 * P, P),
    }
    nc = bacc.Bacc("TRN2", target_bir_lowering=False, num_devices=1)
    arrays, aps = {}, {}
    for name, value in ins.items():
        value = np.ascontiguousarray(value)
        arrays[f"in_{name}"] = value
        aps[name] = nc.dram_tensor(f"in_{name}", value.shape, mybir.dt.from_np(value.dtype),
                                   kind="ExternalInput").ap()
    out = nc.dram_tensor("out_x", (NB, TOK, P), FP, kind="ExternalOutput").ap()
    decoder(nc, aps, out)
    result = run_bass_kernel_spmd(nc, [arrays], core_ids=[0])
    return result.results[0]["out_x"]
```

```python
from contextlib import ExitStack

import concourse.bass as bass
from concourse import mybir

P = 128
NB = 2
NT = 4
TOK = NT * P
CTX = 154
REM = CTX - P
RP = 32
HC = CTX // 2
H = 16
HD = 8
XD = 64
XC = H * XD // P
NP = H // 2
TERM = 6
SLOT = 64
E = 8
F0 = 256 // P
F1 = 512 // P
EPS_LN = 1e-5
EPS_RMS = 1e-6
LOWEST = -3.4028234663852886e38
SELF_SCALE = HD ** -0.5
X_SCALE = XD ** -0.5
L1X_SCALE = P ** -0.5

ALU = mybir.AluOpType
ACT = mybir.ActivationFunctionType
FP = mybir.dt.float32
BF = mybir.dt.bfloat16
U8 = mybir.dt.uint8
AX = mybir.AxisListType.X

CHUNKS = [[(0, 0)], [(1, 0), (3, 384)], [(2, 0)]]
PT_AT = [0, TOK, 2 * TOK, TOK + 384]

C_ID, C_CAUSAL, C_CAUSALT, C_COS, C_SIN, C_TRI, C_END = 0, 128, 640, 768, 800, 832, 896


def decoder(nc, a, out):
    with ExitStack() as ctx:
        def sb(name, shape, dt=FP):
            return ctx.enter_context(nc.sbuf_tensor(name, shape, dt))

        sems = {}

        def sem(name):
            if name not in sems:
                sems[name] = ctx.enter_context(nc.semaphore(name))
            return sems[name]

        bank = [ctx.enter_context(nc.psum_tensor(f"bank{i}", [P, 512], FP)) for i in range(8)]

        con = sb("con", [P, C_END])
        ident = con[:, C_ID:C_ID + P]
        ident_bf = sb("ident_bf", [P, P], BF)
        causal = con[:, C_CAUSAL:C_CAUSAL + TOK]
        causalT_bf = sb("causalT_bf", [P, P], BF)
        cos = con[:, C_COS:C_COS + 32].rearrange("p (t d) -> p t d", t=NT)
        sin = con[:, C_SIN:C_SIN + 32].rearrange("p (t d) -> p t d", t=NT)
        tri = con[:, C_TRI:C_TRI + 64].rearrange("p (e j) -> p e j", e=E)
        w_qkv = [sb("w_qkv0", [P, 3 * P]), sb("w_qkv2", [P, 3 * P])]
        w_proj = [sb("w_proj0", [P, P]), sb("w_proj2", [P, P])]
        qk_w = sb("qk_w", [P, 2, HD])
        early = sb("early", [P, 4, H * XD])
        wq_x, wk_x, wv_x = early[:, 0, :], early[:, 1, :], early[:, 2, :]
        wo_x = early[:, 3, :].rearrange("p (c n) -> p c n", c=XC)
        ctxT = sb("ctxT", [P, NB * CTX])
        mask8 = sb("mask8", [P, NB * NT, CTX], U8)
        mask = sb("mask", [P, NB * NT, CTX])
        rows = sb("rows", [P, 4, P])
        bo, ln1_w, ln2_w, bv_row = (rows[:, i, :] for i in range(4))
        rb2 = sb("rb2", [P, E])
        cols = sb("cols", [P, 3 + E * F1])
        bq, bk, rb1, be1 = cols[:, 0:1], cols[:, 1:2], cols[:, 2:3], cols[:, 3:3 + E * F1]
        wq_l1 = sb("wq_l1", [P, 3, P])
        router = sb("router", [P, E])
        rw1 = sb("rw1", [P, P])
        rw2 = sb("rw2", [P, E])
        be2 = sb("be2", [E, P])
        values_x = sb("values_x", [P, 2 * NB * H * XD])
        vx = values_x[:, 0:NB * H * XD].rearrange("p (b n d) -> p b n d", b=NB, n=H)
        vr = values_x[0:2 * RP, NB * H * XD:].rearrange("p (b c n) -> p b c n", b=NB, c=XC)
        w1 = [sb("w1_l0", [P, E * F0 * P]), early[:].rearrange("p a n -> p (a n)")]
        w2 = [sb("w2_l0", [P, E * F0, P]),
              values_x[:].rearrange("p (c n) -> p c n", n=P)]

        x = sb("x", [P, NB * NT, P])
        y = sb("y", [P, NB * NT, P])
        z = sb("z", [P, NB * NT, P])
        zT = sb("zT", [P, NB, TOK])
        ln_stats = sb("ln_stats", [P, NT, 6])
        ln_mv = sb("ln_mv", [P, NT, 2])
        ln_var = sb("ln_var", [P, NT])
        ln_log = sb("ln_log", [P, NT])
        ln_r0 = sb("ln_r0", [P, NT])
        ln_t = sb("ln_t", [P, NT])
        ln_r = sb("ln_r", [P, NT])

        qk = sb("qk", [P, 2, NT * H, HD])
        rest = sb("rest", [P, 2, NT * H, HD])
        sq, rope_b = rest, rest
        rms_v = sb("rms_v", [P, 2 * NT * H])
        rms_l = sb("rms_l", [P, 2 * NT * H])
        rms_0 = sb("rms_0", [P, 2 * NT * H])
        rms_t = sb("rms_t", [P, 2 * NT * H])
        rope_c = sb("rope_c", [P, 2, NT, HD])
        rope_s = sb("rope_s", [P, 2, NT, HD])
        slots = sb("slots", [P, 2, NT * H * SLOT], BF)
        qs, ks = (slots[:, i, :].rearrange("p (n c) -> p n c", c=SLOT) for i in range(2))
        v9 = sb("v9", [P, NT, H, 32])
        o_quad = sb("o_quad", [P, TOK])
        qkT = sb("qkT", [P, 3, 3 * TOK], BF)
        qmT = sb("qmT", [P, 2, TOK], BF)
        s_scr = sb("s_scr", [P, 2, TOK], BF)
        top = sb("top", [P, 2, NT, 2])
        pT = sb("pT", [P, 2, 2, 5 * TOK // 2])
        rsum = sb("rsum", [P, NT, 4])
        o_tok = sb("o_tok", [P, NT, P])
        oT = sb("oT", [P, TOK])

        kTx = sb("kTx", [P, NB, XC, CTX])
        wide = sb("wide", [P, 8, TOK])
        qTx = oxT = hT = wide
        xneg = sb("xneg", [P, 2, 2])
        xsum = sb("xsum", [P, 4, 2])
        xrs = sb("xrs", [P, 4, 2])
        flat = pT[:].rearrange("p a h n -> p (a h n)")
        xpT = flat[:, 0:4 * TOK].rearrange("p (a h q) -> p a h q", a=2, h=2)
        xrT = flat[0:2 * RP, 4 * TOK:6 * TOK].rearrange("p (a q) -> p a q", a=2)
        xp = flat[:, 6 * TOK:6 * TOK + 8 * CTX].rearrange("p (a h k) -> p a h k", a=4, h=2)
        xq = o_quad[:, 0:8 * RP].rearrange("p (a h k) -> p a h k", a=4, h=2)
        xs = flat[:, 6 * TOK + 8 * CTX:6 * TOK + 12 * CTX].rearrange("p (a h k) -> p a h k", a=2, h=2)

        rT = sb("rT", [P, TOK])
        logit = sb("logit", [P, NT, E])
        g_max = sb("g_max", [P, NT])
        g_e = sb("g_e", [P, NT, E])
        g_cmp = sb("g_cmp", [P, NT * E, E])
        g_eq = sb("g_eq", [P, NT * E, E])
        g_rank = sb("g_rank", [P, NT * E])
        g_sum = sb("g_sum", [P, NT])
        gate = sb("gate", [P, NB, NT, E])
        gateT = sb("gateT", [E, TOK])

        a_max, a_sum, a_log, a_nb, a_ent, a_nent, b_sum, b_rs, c_max, c_neg = (
            sb(name, [P, NB, NT]) for name in ("a_max", "a_sum", "a_log", "a_nb", "a_ent", "a_nent",
                                               "b_sum", "b_rs", "c_max", "c_neg"))
        a_p, a_lp = ([wide[:, 4 * b + i, :].rearrange("p (t c) -> p t c", t=NT) for b in range(NB)] for i in range(2))
        a_pT, a_lpT = ([wide[:, 4 * b + i, :] for b in range(NB)] for i in (2, 3))
        a_scr = [flat[:, (8 + b) * TOK:(9 + b) * TOK].rearrange("p (t c) -> p t c", t=NT) for b in range(NB)]
        b_p, b_pT = ([slots[:, i, :].bitcast(FP).rearrange("p (t k) -> p t k", t=NT),
                      flat[:, 4 * i * TOK:4 * (i + 1) * TOK].rearrange("p (t k) -> p t k", t=NT)] for i in range(2))
        q1T = [oT[:], o_tok[:].rearrange("p t c -> p (t c)")]
        k1T = sb("k1T", [P, NB, CTX])
        v1 = sb("v1", [HC, NB, 2, P])

        def tiles(b):
            return slice(NT * b, NT * b + NT)

        loads = [
            ("x", x[:], a["x"].rearrange("b (t p) c -> p (b t) c", p=P)),
            ("ctx", ctxT[:], a["ctxT"]),
            ("wk_x", wk_x, a["xWk"]),
            ("con", con[:], a["con"]),
            ("att0", w_qkv[0][:], a["w_qkvT"]),
            ("qk_w", qk_w[:, 0, :], a["qn"].to_broadcast([P, HD])),
            ("qk_w", qk_w[:, 1, :], a["kn"].to_broadcast([P, HD])),
            ("wv_x", wv_x, a["xWv"]),
            ("l1kv", wq_l1[:], a["l1_wqkv"].rearrange("j p c -> p j c")),
            ("cols", cols[:], a["cols"]),
            ("rows", rows[:, 0, :], a["bo"].to_broadcast([P, P])),
            ("rows", rows[:, 1, :], a["ln1"].to_broadcast([P, P])),
            ("rows", rows[:, 2, :], a["ln2"].to_broadcast([P, P])),
            ("rows", rows[:, 3, :], a["bv"].to_broadcast([P, P])),
            ("proj0", w_proj[0][:], a["w_projT"]),
            ("mask", mask8[:], a["mask"].rearrange("b (t p) k -> p (b t) k", p=P)),
            ("wq_x", wq_x, a["xWq"]),
            ("wo_x", wo_x, a["xWo"].rearrange("(c p) n -> p c n", p=P)),
            ("att2", w_qkv[1][:], a["c_attn"]),
            ("att2", w_proj[1][:], a["c_proj"]),
            ("router", router[:], a["router"]),
            ("moe0", w1[0][:], a["w1"]),
            ("moe0", w2[0][:], a["w2"].rearrange("(c p) n -> p c n", p=P)),
            ("l1r", rw1[:], a["rw1"]),
            ("l1r", rw2[:], a["rw2"]),
            ("l1r", rb2[:], a["rb2"].to_broadcast([P, E])),
            ("l1r", be2[:], a["be2"]),
            ("moe1", w1[1], a["we1"]),
            ("moe1", w2[1], a["we2"].rearrange("(c p) n -> p c n", p=P)),
        ]
        group_size = {}
        for g, _, _ in loads:
            group_size[g] = group_size.get(g, 0) + 16

        def loaded(eng, group):
            eng.wait_ge(sem(f"load_{group}"), group_size[group])

        x_stored = sem("x_stored")
        z_ready = sem("z_ready")
        x_added = sem("x_added")
        zT_full = sem("zT_full")
        zT_ready = sem("zT_ready")
        setup = sem("setup")
        log_in, log_out = sem("log_in"), sem("log_out")
        zeroed = sem("zeroed")
        pre_full, pre_done = sem("pre_full"), sem("pre_done")

        qkv_bank = [bank[i] for i in (1, 2, 3, 0)]

        def context_bank(i):
            return bank[(0, 5, 6, 7)[i % 4]]

        block = ctx.enter_context(nc.Block())

        @block.sync
        def _(sp):
            for group, dst, src in loads:
                if group == "moe1":
                    sp.wait_ge(x_added, 4)
                sp.dma_start(dst, src).then_inc(sem(f"load_{group}"), 16)
            out_v = out.rearrange("b (t p) c -> p (b t) c", p=P)
            for b in range(NB):
                sp.wait_ge(x_added, 12 + b + 1)
                sp.dma_start(out_v[:, tiles(b), :], x[:, tiles(b), :]).then_inc(x_stored, 16)
            sp.wait_ge(x_stored, 16 * NB)

        @block.tensor
        def _(pe):
            mm, tr = nc.tensor.matmul, nc.tensor.transpose

            def context(part):
                some = CONTEXT_PARTS[part]
                for i in some:
                    if i >= 4:
                        pe.wait_ge(pre_done, i - 3)
                    o = context_bank(i)
                    kind, b, c = CONTEXT[i]
                    at = b * CTX
                    by_head = wv_x.rearrange("p (c h d) -> p c h d", h=2, d=XD)
                    if kind == "keys":
                        loaded(pe, "ctx")
                        loaded(pe, "wk_x")
                        last = mm(o[:, 0:CTX], wk_x[:, c * P:c * P + P], ctxT[:, at:at + CTX],
                                  start=True, stop=True)
                    elif kind == "values":
                        loaded(pe, "wv_x")
                        last = mm(o[:], ctxT[:, at:at + P], wv_x[:, 512 * c:512 * c + 512],
                                  start=True, stop=True)
                    elif kind == "rest":
                        for h in range(2):
                            last = mm(o[RP * h:RP * h + REM, :], ctxT[:, at + P:at + CTX], by_head[:, :, h, :],
                                      start=True, stop=True)
                    elif kind == "keys1":
                        loaded(pe, "l1kv")
                        last = mm(o[:, 0:CTX], wq_l1[:, 1, :], ctxT[:, at:at + CTX], start=True, stop=True)
                    else:
                        last = mm(o[0:HC, 0:P], ctxT[:, at + c * HC:at + c * HC + HC], wq_l1[:, 2, :],
                                  start=True, stop=True)
                    last.then_inc(pre_full, 1)

            def turn_z(s, b):
                pe.wait_ge(z_ready, 2 * s + b + 1)
                for t in range(NT):
                    last = tr(bank[0][:, t * P:t * P + P], z[:, NT * b + t, :], ident)
                last.then_inc(zT_full, 1)

            def transpose_z(s, b):
                turn_z(s, b)
                pe.wait_ge(zT_ready, zt_index(s, b) + 1)

            def project_qkv(s, b):
                n = 0 if s == 0 else 1
                S = lambda name: sem(f"a{s}_{name}")
                pe.wait_ge(zT_ready, zt_index(s, b) + 1)
                loaded(pe, "att0" if s == 0 else "att2")
                if b == 1:
                    pe.wait_ge(S("max_done"), 8 * NP)
                for t in range(NT):
                    mm(qkv_bank[t][:, 0:3 * P], zT[:, b, t * P:t * P + P], w_qkv[n][:],
                       start=True, stop=True).then_inc(S("qkv_full"), 1)

            def causal_attention(s, b):
                n = 0 if s == 0 else 1
                S = lambda name: sem(f"a{s}_{name}")
                if b == 0:
                    if s == 2:
                        pe.wait_ge(x_added, 2 * s)
                    turn_z(s, 0)
                    project_qkv(s, 0)
                pe.wait_ge(S("v_ready"), b + 1)
                pe.wait_ge(S("v_copied"), b + 1)
                if s == 0 and b == 0:
                    context(1)
                    context(2)
                    pe.wait_ge(pre_done, len(CONTEXT))
                    pe.wait_ge(setup, 1)
                    pe.wait_ge(zeroed, 2)

                def turn_qk(u):
                    g = NP * b + u
                    if u == 0:
                        pe.wait_ge(S("parts_ready"), 2 * (b + 1))
                    elif u < 3:
                        pe.wait_ge(S("qk_turned"), g)
                    else:
                        pe.wait_ge(S("qm_turned"), g - 1)
                    for j, src in enumerate((qs, ks)):
                        for t in range(NT):
                            at, to = t * H + 2 * u, j * TOK + t * P
                            last = tr(bank[0][:].bitcast(BF)[:, to:to + P],
                                      src[:, at:at + 2, :].rearrange("p h c -> p (h c)"), ident_bf[:])
                    last.then_inc(S("qk_full"), 1)

                def turn_qm(u):
                    g = NP * b + u
                    pe.wait_ge(S("max_ready"), g + 1)
                    pe.wait_ge(S("qk_turned"), NP * b + min(max(u + 2, 3), NP))
                    for t in range(NT):
                        at = t * H + 2 * u
                        last = tr(bank[0][:].bitcast(BF)[:, t * P:t * P + P],
                                  qs[:, at:at + 2, :].rearrange("p h c -> p (h c)"), ident_bf[:])
                    last.then_inc(S("qm_full"), 1)

                def raw_scores(u, some):
                    g = NP * b + u
                    pe.wait_ge(S("qk_turned"), g + 1)
                    for i in some:
                        n_item = 8 * g + i
                        if n_item >= 3:
                            pe.wait_ge(S("max_done"), n_item - 2)
                        hh, t = i % 2, i // 2
                        k0 = (1 + hh) * TOK
                        mm(bank[1 + n_item % 3][:, 0:(t + 1) * P], qkT[:, g % 3, t * P:t * P + P],
                           qkT[:, g % 3, k0:k0 + (t + 1) * P], start=True, stop=True)\
                            .then_inc(S("raw_full"), 1)

                def scores(u, c):
                    g = NP * b + u
                    m = 6 * g + c
                    if m >= 3:
                        pe.wait_ge(S("pT_ready"), m - 2)
                    o = bank[4 + m % 3]
                    for j, at in CHUNKS[c % 3]:
                        k0, w = (1 + c // 3) * TOK + j * P, (NT - j) * P
                        mm(o[:, at:at + w], qkT[:, g % 3, k0:k0 + P], qmT[:, g % 2, j * P:TOK],
                           start=True, stop=False)
                        last = mm(o[:, at:at + P], ident_bf[:], causalT_bf[:], start=False, stop=True)
                    last.then_inc(S("scores_full"), 1)

                def values(u, j):
                    g = NP * b + u
                    if j == 0:
                        if u % 2 == 0 and u:
                            pe.wait_ge(S("o_done"), g // 2)
                        if u == 0 and b:
                            pe.wait_ge(x_added, 2 * s + b)
                        pe.wait_ge(S("pT_ready"), 6 * (g + 1))
                    w = (NT - j) * P
                    for hh in range(2):
                        quarter = 32 * (2 * (u % 2) + hh)
                        last = mm(bank[7][quarter:quarter + 32, j * P:TOK], v9[:, j, 2 * u + hh, :],
                                  pT[:, g % 2, hh, PT_AT[j]:PT_AT[j] + w], start=(j == 0), stop=(j == NT - 1))
                    if j == NT - 1:
                        last.then_inc(S("o_full"), 1)

                def turn_outputs(u):
                    pe.wait_ge(S("quad_ready"), (NP * b + u + 1) // 2)
                    for t in range(NT):
                        last = tr(bank[7][:, t * P:t * P + P], o_quad[:, t * P:t * P + P], ident)
                    last.then_inc(S("quad_full"), 1)

                turn_qk(0)
                raw_scores(0, range(3))
                turn_qk(1)
                raw_scores(0, range(3, 8))
                turn_qk(2)
                raw_scores(1, range(2))
                turn_qm(0)
                raw_scores(1, range(2, 4))
                for u in range(NP):
                    pe.wait_ge(S("qm_turned"), NP * b + u + 1)
                    if u == NP - 1 and b == 0:
                        turn_z(s, 1)
                    value_steps = VALUES_AFTER_EVEN if u % 2 else VALUES_AFTER_ODD
                    for c in range(6):
                        scores(u, c)
                        if u + 1 < NP and c < 4:
                            raw_scores(u + 1, (4 + c,))
                        if u + 2 < NP and c >= 3:
                            raw_scores(u + 2, (c - 3,))
                        if u >= 2 and u % 2 and c == 1:
                            turn_outputs(u - 2)
                        if u:
                            for j in value_steps[c]:
                                values(u - 1, j)
                        if c == 4 and u + 1 < NP:
                            turn_qm(u + 1)
                        if u == NP - 1 and b == 0 and c == 2:
                            project_qkv(s, 1)
                    if u + 2 < NP:
                        raw_scores(u + 2, (3,))
                    if u + 3 < NP:
                        turn_qk(u + 3)
                for j in range(NT):
                    values(NP - 1, j)
                turn_outputs(NP - 1)
                pe.wait_ge(S("o_done"), NP // 2 * (b + 1))
                for t in range(NT):
                    last = tr(bank[4][:, t * P:t * P + P], o_tok[:, t, :], ident)
                last.then_inc(S("oT_full"), 1)
                loaded(pe, "proj0" if s == 0 else "att2")
                pe.wait_ge(S("oT_ready"), b + 1)
                for t in range(NT):
                    last = mm(bank[7][:, t * P:t * P + P], oT[:, t * P:t * P + P], w_proj[n][:],
                              start=True, stop=True)
                last.then_inc(S("proj_full"), 1)

            def cross_attention(b):
                S = lambda name: sem(f"x_{name}")
                transpose_z(1, b)
                loaded(pe, "wq_x")
                pe.wait_ge(x_added, 2 + b)
                for c in range(XC):
                    n = XC * b + c
                    if c >= 2:
                        pe.wait_ge(S("q_ready"), n - 1)
                    mm(bank[c % 2][:], wq_x[:, c * P:c * P + P], zT[:, b, :], start=True, stop=True)\
                        .then_inc(S("q_full"), 1)
                pe.wait_ge(S("q_ready"), XC * (b + 1))

                def scores(i):
                    g = XC * NT * b + i
                    c, t = i // NT, i % NT
                    if g >= 2:
                        pe.wait_ge(S("max_done"), g - 1)
                    for hh in range(2):
                        r = slice(XD * hh, XD * hh + XD)
                        last = mm(bank[2 * (g % 2) + hh][:, 0:CTX], qTx[r, c, t * P:t * P + P],
                                  kTx[r, b, c, :], start=True, stop=True)
                    last.then_inc(S("s_full"), 1)

                def transposes(i):
                    g = XC * NT * b + i
                    t = i % NT
                    pe.wait_ge(S("p_normed"), g + 1)
                    if g % 2 == 0 and g >= 4:
                        pe.wait_ge(S("pT_ready"), g // 2 - 1)
                    if t == 0 and g >= 4:
                        pe.wait_ge(S("rT_ready"), g // NT)
                    o = bank[4 + g // 2 % 2]
                    for hh in range(2):
                        at = (2 * (g % 2) + hh) * P
                        last = tr(o[:, at:at + P], xp[:, g % 4, hh, 0:P], ident)
                    if g % 2:
                        last.then_inc(S("pT_full"), 1)
                    last = tr(bank[6][0:2 * RP, t * P:t * P + P], xq[:, g % 4].rearrange("p h k -> p (h k)"), ident)
                    last.then_inc(S("rT_full"), 1)

                def values(c, part):
                    g = XC * b + c
                    if part == 0:
                        pe.wait_ge(S("pT_ready"), 2 * g + 2)
                        if g:
                            pe.wait_ge(S("oT_ready"), g)
                    if part < 2:
                        mm(bank[7][XD * part:XD * part + XD, :], vx[:, b, 2 * c + part, :],
                           xpT[:, g % 2, part, :], start=True, stop=True)
                    else:
                        pe.wait_ge(S("rT_ready"), g + 1)
                        mm(bank[7][:], vr[:, b, c, :], xrT[:, g % 2, :], start=False, stop=True,
                           skip_group_check=True).then_inc(S("o_full"), 1)

                n = XC * NT
                for i in range(n + 8):
                    if i < n:
                        scores(i)
                    if 4 <= i < n + 4:
                        transposes(i - 4)
                    for part, delay in enumerate((9, 9, 10)):
                        c, r = divmod(i - delay, NT)
                        if r == 0 and 0 <= c < XC:
                            values(c, part)
                loaded(pe, "wo_x")
                pe.wait_ge(S("oT_ready"), XC * (b + 1))
                for t in range(NT):
                    for c in range(XC):
                        last = mm(bank[7][:, t * P:t * P + P], oxT[:, c, t * P:t * P + P], wo_x[:, c, :],
                                  start=(c == 0), stop=(c == XC - 1))
                last.then_inc(S("proj_full"), 1)

            def experts(s):
                n, fc = (0, F0) if s == 3 else (1, F1)
                S = lambda name: sem(f"m{s}_{name}")

                def router_input(b):
                    if s == 3:
                        return
                    mm(bank[0][:], rw1[:], zT[:, b, :], start=True, stop=True).then_inc(S("r_full"), 1)

                def logits(b):
                    if s == 6:
                        pe.wait_ge(S("r_ready"), b + 1)
                    if b:
                        pe.wait_ge(S("gate_in"), b)
                    src, w = (zT[:, b, :], router) if s == 3 else (rT, rw2)
                    for t in range(NT):
                        last = mm(bank[1][:, t * E:t * E + E], src[:, t * P:t * P + P], w[:],
                                  start=True, stop=True)
                    last.then_inc(S("logit_full"), 1)

                def hidden(g):
                    b, e = divmod(g, E)
                    for c in range(fc):
                        m = g * fc + c
                        if m >= 4:
                            pe.wait_ge(S("h_ready"), m - 3)
                        f = e * fc + c
                        mm(bank[2 + m % 4][:], w1[n][:, f * P:f * P + P], zT[:, b, :],
                           start=True, stop=True).then_inc(S("h_full"), 1)

                def down(g):
                    e = g % E
                    pe.wait_ge(S("h_ready"), (g + 1) * fc)
                    if g >= 2:
                        pe.wait_ge(S("e_done"), g - 1)
                    for t in range(NT):
                        for c in range(fc):
                            last = mm(bank[6 + g % 2][:, t * P:t * P + P],
                                      hT[:, (g * fc + c) % 8, t * P:t * P + P], w2[n][:, e * fc + c, :],
                                      start=(c == 0), stop=(c == fc - 1))
                    last.then_inc(S("e_full"), 1)

                def turn_gates(b):
                    pe.wait_ge(S("gate_ready"), b + 1)
                    for t in range(NT):
                        last = tr(bank[0][0:E, t * P:t * P + P], gate[:, b, t, :], ident)
                    last.then_inc(S("gT_full"), 1)

                def second_bias(b):
                    pe.wait_ge(S("gT_ready"), b + 1)
                    if b == 0:
                        pe.wait_ge(S("gate_in"), NB)
                    else:
                        pe.wait_ge(x_added, 2 * s + b)
                    for t in range(NT):
                        last = mm(bank[1][:, t * P:t * P + P], gateT[:, t * P:t * P + P], be2[:],
                                  start=True, stop=True)
                    last.then_inc(S("be2_full"), 1)

                transpose_z(s, 0)
                loaded(pe, "router" if s == 3 else "l1r")
                router_input(0)
                loaded(pe, "moe0" if s == 3 else "moe1")
                for g in range(NB * E + 1):
                    if g < NB * E:
                        hidden(g)
                    if g == 0:
                        pe.wait_ge(x_added, 2 * s)
                        logits(0)
                    if g == 2:
                        pe.wait_ge(zT_ready, zt_index(s, 1) + 1)
                        router_input(1)
                    if g:
                        down(g - 1)
                    if g == 1:
                        turn_z(s, 1)
                    if g == 2:
                        logits(1)
                    if s == 6 and g % E == BIAS_STEP and g < NB * E:
                        turn_gates(g // E)
                    if s == 6 and g % E == BIAS_STEP + 1 and g < NB * E:
                        second_bias(g // E)

            def divergence_attention():
                S = lambda name: sem(f"d_{name}")
                pe.wait_ge(x_added, 8)
                own = [(bank[0], bank[1]), (bank[6], bank[7])]
                for b in range(NB):
                    pe.wait_ge(S("p_ready"), NT * (b + 1))
                    for t in range(NT):
                        last = tr(own[b][0][:, t * P:t * P + P], a_p[b][:, t, :], ident)
                    last.then_inc(S("t_full"), 1)
                    pe.wait_ge(S("lp_ready"), NT * (b + 1))
                    for t in range(NT):
                        last = tr(own[b][1][:, t * P:t * P + P], a_lp[b][:, t, :], ident)
                    last.then_inc(S("t_full"), 1)
                for b in range(NB):
                    pe.wait_ge(S("t_ready"), 2 * (b + 1))
                    for t in range(NT):
                        if b:
                            pe.wait_ge(S("e_ready"), NT * (b - 1) + t + 1)
                        mm(bank[2 + t][:], a_pT[b][:, t * P:t * P + P], a_lpT[b], start=True, stop=True)\
                            .then_inc(S("s_full"), 1)
                for b in range(NB):
                    for t in range(NT):
                        g = NT * b + t
                        pe.wait_ge(S("e_ready"), g + 1)
                        if t >= 2:
                            pe.wait_ge(S("eT_ready"), g - 1)
                        for j in range(NT):
                            last = tr(own[b][t % 2][:, j * P:j * P + P], b_p[b][:, t, j * P:j * P + P], ident)
                        last.then_inc(S("eT_full"), 1)
                for b in range(NB):
                    pe.wait_ge(S("eT_ready"), NT * (b + 1))
                    for t in range(NT):
                        for j in range(NT):
                            last = mm(own[b][0][:, t * P:t * P + P], b_pT[b][:, t, j * P:j * P + P],
                                      z[:, NT * b + j, :], start=(j == 0), stop=(j == NT - 1))
                    last.then_inc(S("o_full"), 1)

            def cross_attention_1():
                S = lambda name: sem(f"c_{name}")
                for b in range(NB):
                    transpose_z(5, b)
                    pe.wait_ge(x_added, 8 + b + 1)
                    mm(bank[6 if b else 1][:], wq_l1[:, 0, :], zT[:, b, :], start=True, stop=True)\
                        .then_inc(S("q_full"), 1)
                    pe.wait_ge(S("q_ready"), b + 1)
                    for t in range(NT):
                        last = mm(bank[2 + 2 * b + t // 2][:, t % 2 * CTX:t % 2 * CTX + CTX],
                                  q1T[b][:, t * P:t * P + P], k1T[:, b, :], start=True, stop=True)
                    last.then_inc(S("s_full"), 1)
                for b in range(NB):
                    for i in range(2):
                        pe.wait_ge(S("p_ready"), NT * b + 2 * i + 2)
                        for k in range(NT):
                            t, h = 2 * i + k // 2, k % 2
                            last = tr(bank[2 + 2 * b + i][0:HC, k * P:k * P + P],
                                      b_p[b][:, t, h * HC:h * HC + HC], ident)
                        last.then_inc(S("pT_full"), 1)
                for b in range(NB):
                    pe.wait_ge(S("pT_ready"), 2 * (b + 1))
                    for t in range(NT):
                        for h in range(2):
                            k = 2 * (t % 2) + h
                            last = mm(bank[1 if b else 7][:, t * P:t * P + P],
                                      b_pT[b][0:HC, t // 2, k * P:k * P + P],
                                      v1[:, b, h, :], start=(h == 0), stop=(h == 1))
                    last.then_inc(S("o_full"), 1)

            context(0)
            pe.wait_ge(pre_done, CONTEXT_PARTS[1][0])
            loaded(pe, "con")
            for b in range(NB):
                causal_attention(0, b)
            for b in range(NB):
                cross_attention(b)
            for b in range(NB):
                causal_attention(2, b)
            experts(3)
            divergence_attention()
            cross_attention_1()
            experts(6)

        @block.scalar
        def _(act):
            af = nc.scalar.activation
            own = sem("act_own")
            own_n = [0]

            def link(ins):
                own_n[0] += 1
                ins.then_inc(own, 1)
                act.wait_ge(own, own_n[0])

            norms = [0]

            def use_log_exp():
                nc.scalar.preload_act_table_set("natural_log_exp_and_others")

            def layer_norm():
                norms[0] += 1
                act.wait_ge(log_in, norms[0])
                link(af(ln_log[:], ln_var[:], ACT.Ln))
                af(ln_r0[:], ln_log[:], ACT.Exp, scale=-0.5).then_inc(log_out, 1)

            def copy_zT(s, b):
                act.wait_ge(zT_full, zt_index(s, b) + 1)
                nc.scalar.copy(zT[:, b, :], bank[0][:]).then_inc(zT_ready, 1)

            def context(part):
                for i in CONTEXT_PARTS[part]:
                    act.wait_ge(pre_full, i + 1)
                    o = context_bank(i)
                    kind, b, c = CONTEXT[i]
                    if kind == "keys":
                        last = nc.scalar.copy(kTx[:, b, c, :], o[:, 0:CTX])
                    elif kind == "values":
                        last = nc.scalar.copy(vx[:, b, 8 * c:8 * c + 8, :], o[:].rearrange("p (h d) -> p h d", d=XD))
                    elif kind == "rest":
                        for h in range(2):
                            rows_h = slice(RP * h, RP * h + REM)
                            last = nc.scalar.copy(vr[rows_h, b, :, XD * h:XD * h + XD],
                                                  o[rows_h, :].rearrange("p (c d) -> p c d", d=XD))
                    elif kind == "keys1":
                        loaded(act, "cols")
                        last = af(k1T[:, b, :], o[:, 0:CTX], ACT.Identity, bias=bk)
                    else:
                        last = nc.scalar.copy(v1[:, b, c, :], o[0:HC, 0:P])
                    last.then_inc(pre_done, 1)

            def copy_qk(s, b):
                S = lambda name: sem(f"a{s}_{name}")
                for t in range(2):
                    act.wait_ge(S("qkv_full"), NT * b + t + 1)
                    rows_t = slice(t * H, t * H + H)
                    src = qkv_bank[t][:, 0:3 * P].rearrange("p (j h d) -> p j h d", j=3, h=H)
                    af(qk[:, 0, rows_t, :], src[:, 0], ACT.Copy, scale=1.0 if s == 0 else SELF_SCALE)
                    nc.scalar.copy(qk[:, 1, rows_t, :], src[:, 1]).then_inc(S("qk_copied"), 1)

            def copy_v(s, b):
                S = lambda name: sem(f"a{s}_{name}")
                if b:
                    act.wait_ge(S("o_full"), NP)
                else:
                    act.wait_ge(zeroed, 2)
                for t in range(2):
                    ins = nc.scalar.copy(v9[:, t, :, 0:HD],
                                         qkv_bank[t][:, 2 * P:3 * P].rearrange("p (h d) -> p h d", h=H))
                ins.then_inc(S("v_copied"), 1)

            def inverse_rms(s, b):
                S = lambda name: sem(f"a{s}_{name}")
                act.wait_ge(S("rms_in"), b + 1)
                link(af(rms_l[:], rms_v[:], ACT.Ln))
                af(rms_0[:], rms_l[:], ACT.Exp, scale=-0.5).then_inc(S("rms_out"), 1)

            def first_parts(s, b):
                act.wait_ge(sem(f"a{s}_qk_ready"), b + 1)
                for i, dst in enumerate((qs, ks)):
                    nc.scalar.copy(dst[:, :, 0:HD], qk[:, i]).then_inc(sem(f"a{s}_part1"), 1)

            def second_parts(s, b):
                for i, (dst, at) in enumerate(((qs, 3 * HD), (ks, HD))):
                    act.wait_ge(sem(f"a{s}_rest1"), 2 * b + i + 1)
                    nc.scalar.copy(dst[:, :, at:at + HD], rest[:, i]).then_inc(sem(f"a{s}_part2"), 1)

            def causal_attention(s, b):
                S = lambda name: sem(f"a{s}_{name}")
                if b == 0:
                    copy_zT(s, 0)
                    copy_qk(s, 0)
                    copy_v(s, 0)
                    if s == 0:
                        context(1)
                        inverse_rms(s, 0)
                        context(2)
                if b == 0 or s == 0:
                    first_parts(s, b)
                second_parts(s, b)

                def copy_qkT(u, part):
                    g = NP * b + u
                    o = bank[0][:].bitcast(BF)
                    if part == 0:
                        act.wait_ge(S("qk_full"), g + 1)
                        nc.scalar.copy(qkT[:, g % 3, 0:TOK], o[:, 0:TOK])
                        return
                    r = slice(SLOT * (part - 1), SLOT * part)
                    last = nc.scalar.copy(qkT[r, g % 3, part * TOK:part * TOK + TOK], o[r, TOK:2 * TOK])
                    if part == 2:
                        last.then_inc(S("qk_turned"), 1)

                def copy_qmT(u):
                    g = NP * b + u
                    act.wait_ge(S("qm_full"), g + 1)
                    nc.scalar.copy(qmT[:, g % 2, :], bank[0][:].bitcast(BF)[:, 0:TOK]).then_inc(S("qm_turned"), 1)

                for u in range(3):
                    for part in range(3):
                        copy_qkT(u, part)
                copy_qmT(0)
                for u in range(NP):
                    g = NP * b + u
                    if g >= 2:
                        act.wait_ge(S("o_full"), g - 1)
                    if b == 0 and u == NP - 1:
                        copy_zT(s, 1)
                    if u and u + 2 < NP:
                        copy_qkT(u + 2, 0)
                    for c in range(6):
                        m = 6 * g + c
                        act.wait_ge(S("scores_full"), m + 1)
                        at, w = TOK * (c % 3), TOK if c % 3 < 2 else TOK // 2
                        af(pT[:, g % 2, c // 3, at:at + w], bank[4 + m % 3][:, 0:w], ACT.Exp)\
                            .then_inc(S("pT_ready"), 1)
                        if u and u + 2 < NP and c == 0:
                            copy_qkT(u + 2, 1)
                            copy_qkT(u + 2, 2)
                        if b == 1 and u == NP - 1 and c == 3:
                            layer_norm()
                        if u + 1 < NP and c == 4:
                            copy_qmT(u + 1)
                        if b == 0 and u == NP - 1 and c == 2:
                            copy_qk(s, 1)
                if b == 0:
                    if s == 0:
                        inverse_rms(s, 1)
                    else:
                        first_parts(s, 1)
                    copy_v(s, 1)
                act.wait_ge(S("oT_full"), b + 1)
                nc.scalar.copy(oT[:, :], bank[4][:]).then_inc(S("oT_ready"), 1)

            def cross_attention(b):
                S = lambda name: sem(f"x_{name}")
                copy_zT(1, b)
                for c in range(XC):
                    act.wait_ge(S("q_full"), XC * b + c + 1)
                    nc.scalar.copy(qTx[:, c, :], bank[c % 2][:]).then_inc(S("q_ready"), 1)
                n = XC * NT

                def exps(i):
                    g = n * b + i
                    act.wait_ge(S("max_done"), g + 1)
                    if g >= 4:
                        act.wait_ge(S("rT_full"), g - 3)
                    for hh in range(2):
                        last = af(xp[:, g % 4, hh, 0:CTX], xs[:, g % 2, hh, :], ACT.Exp,
                                  bias=xneg[:, g % 2, hh:hh + 1], scale=-1.0,
                                  accum_out=xsum[:, g % 4, hh:hh + 1])
                    last.then_inc(S("p_ready"), 1)

                def copy_pT(k):
                    g = n // 2 * b + k
                    act.wait_ge(S("pT_full"), g + 1)
                    if g >= 4:
                        act.wait_ge(S("o_full"), g // 2 - 1)
                    at = g % 2 * 2 * P
                    nc.scalar.copy(xpT[:, g // 2 % 2, :, at:at + 2 * P].rearrange("p h (t q) -> p t h q", t=2),
                                   bank[4 + g % 2][:].rearrange("p (t h q) -> p t h q", t=2, h=2))\
                        .then_inc(S("pT_ready"), 1)

                for i in range(n + 3):
                    if i < n:
                        exps(i)
                    if i >= 4 and i % 2 == 0:
                        copy_pT((i - 4) // 2)

            def experts(s):
                fc = F0 if s == 3 else F1
                S = lambda name: sem(f"m{s}_{name}")

                def router_input(b):
                    if s == 6:
                        act.wait_ge(S("r_full"), b + 1)
                        af(rT[:], bank[0][:], ACT.Silu, bias=rb1).then_inc(S("r_ready"), 1)

                def exp_logits(b):
                    act.wait_ge(S("gate_in"), b + 1)
                    af(g_e[:], logit[:], ACT.Exp).then_inc(S("gate_out"), 1)

                copy_zT(s, 0)
                layer_norm()
                if s == 3:
                    exp_logits(0)
                router_input(0)
                for g in range(NB * E):
                    for c in range(fc):
                        m = g * fc + c
                        act.wait_ge(S("h_full"), m + 1)
                        if m >= 8:
                            act.wait_ge(S("e_full"), (m - 8) // fc + 1)
                        f = g % E * fc + c
                        if s == 3:
                            ins = af(hT[:, m % 8, :], bank[2 + m % 4][:], ACT.Gelu)
                        else:
                            ins = af(hT[:, m % 8, :], bank[2 + m % 4][:], ACT.Silu, bias=be1[:, f:f + 1])
                        ins.then_inc(S("h_ready"), 1)
                    if g == 0 and s == 6:
                        exp_logits(0)
                    if g == 1:
                        copy_zT(s, 1)
                    if g == 2:
                        router_input(1)
                    if g == 3:
                        exp_logits(1)
                    if s == 6 and g % E == BIAS_STEP:
                        act.wait_ge(S("gT_full"), g // E + 1)
                        nc.scalar.copy(gateT[:], bank[0][0:E, :]).then_inc(S("gT_ready"), 1)
                    if s == 3 and g == E + 1:
                        use_log_exp()
                        layer_norm()
                if s == 3:
                    use_log_exp()
                    layer_norm()

            def divergence_attention():
                S = lambda name: sem(f"d_{name}")
                for b in range(NB):
                    act.wait_ge(S("max_ready"), b + 1)
                    for t in range(NT):
                        ins = af(a_scr[b][:, t, :], z[:, NT * b + t, :], ACT.Exp, bias=a_max[:, b, t:t + 1],
                                 accum_out=a_sum[:, b, t:t + 1])
                    link(ins)
                    af(a_log[:, b, :], a_sum[:, b, :], ACT.Ln).then_inc(S("log_ready"), 1)
                for b in range(NB):
                    act.wait_ge(S("nb_ready"), b + 1)
                    for t in range(NT):
                        af(a_p[b][:, t, :], z[:, NT * b + t, :], ACT.Exp, bias=a_nb[:, b, t:t + 1])\
                            .then_inc(S("p_ready"), 1)
                for b in range(NB):
                    act.wait_ge(S("t_full"), 2 * b + 1)
                    nc.scalar.copy(a_pT[b], bank[6 if b else 0][:]).then_inc(S("t_ready"), 1)
                    act.wait_ge(S("t_full"), 2 * b + 2)
                    nc.scalar.copy(a_lpT[b], bank[7 if b else 1][:]).then_inc(S("t_ready"), 1)
                for b in range(NB):
                    act.wait_ge(S("ent_ready"), b + 1)
                    for t in range(NT):
                        act.wait_ge(S("s_full"), NT * b + t + 1)
                        af(b_p[b][:, t, :], bank[2 + t][:], ACT.Exp, bias=a_nent[:, b, t:t + 1],
                           accum_out=b_sum[:, b, t:t + 1]).then_inc(S("e_ready"), 1)
                for b in range(NB):
                    for t in range(NT):
                        act.wait_ge(S("eT_full"), NT * b + t + 1)
                        nc.scalar.copy(b_pT[b][:, t, :], bank[6 * b + t % 2][:]).then_inc(S("eT_ready"), 1)

            def cross_attention_1():
                S = lambda name: sem(f"c_{name}")

                def queries(b):
                    copy_zT(5, b)
                    act.wait_ge(S("q_full"), b + 1)
                    af(q1T[b], bank[6 if b else 1][:], ACT.Identity, bias=bq).then_inc(S("q_ready"), 1)

                queries(0)
                layer_norm()
                for b in range(NB):
                    if b:
                        queries(1)
                    act.wait_ge(S("neg_ready"), b + 1)
                    for t in range(NT):
                        af(b_p[b][:, t, 0:CTX], bank[2 + 2 * b + t // 2][:, t % 2 * CTX:t % 2 * CTX + CTX], ACT.Exp,
                           bias=c_neg[:, b, t:t + 1], scale=L1X_SCALE, accum_out=b_sum[:, b, t:t + 1])\
                            .then_inc(S("p_ready"), 1)
                for b in range(NB):
                    for i in range(2):
                        act.wait_ge(S("pT_full"), 2 * b + i + 1)
                        nc.scalar.copy(b_pT[b][0:HC, i, :], bank[2 + 2 * b + i][0:HC, :]).then_inc(S("pT_ready"), 1)

            use_log_exp()
            layer_norm()
            context(0)
            layer_norm()
            for b in range(NB):
                causal_attention(0, b)
            layer_norm()
            for b in range(NB):
                cross_attention(b)
            for _ in range(2 * NB):
                layer_norm()
            for b in range(NB):
                causal_attention(2, b)
            experts(3)
            divergence_attention()
            layer_norm()
            cross_attention_1()
            layer_norm()
            experts(6)

        @block.gpsimd
        def _(pool):
            nc.gpsimd.memset(v9[:, :, :, HD + 1:32], 0.0)
            nc.gpsimd.memset(v9[:, :, :, HD:HD + 1], 1.0)
            nc.gpsimd.memset(vr, 0.0)
            nc.gpsimd.memset(qs[:, :, TERM * HD:SLOT], 0.0)
            nc.gpsimd.memset(ks[:, :, TERM * HD + 2:SLOT], 0.0)
            nc.gpsimd.memset(ks[:, :, TERM * HD:TERM * HD + 2], 1.0).then_inc(zeroed, 1)
            pool.wait_ge(zeroed, 1)
            for hh in range(2):
                other = slice(SLOT * (1 - hh), SLOT * (1 - hh) + SLOT)
                last = nc.gpsimd.memset(qkT[other, :, (1 + hh) * TOK:(2 + hh) * TOK], 0.0)
            last.then_inc(zeroed, 1)
            for g in range(NB * XC * NT):
                pool.wait_ge(sem("x_rs_ready"), g + 1)
                nc.gpsimd.tensor_tensor(xq[:, g % 4, :, 0:REM], xp[:, g % 4, :, P:CTX],
                                        xrs[:, g % 4, :].unsqueeze(2).to_broadcast([P, 2, REM]), ALU.mult)
                p = xp[:, g % 4, :, 0:P]
                nc.gpsimd.tensor_tensor(p, p, xrs[:, g % 4, :].unsqueeze(2).to_broadcast([P, 2, P]), ALU.mult)\
                    .then_inc(sem("x_p_normed"), 1)

        @block.vector
        def _(dve):
            v = nc.vector
            own = sem("dve_own")
            own_n = [0]

            def link(ins):
                own_n[0] += 1
                ins.then_inc(own, 1)
                dve.wait_ge(own, own_n[0])

            norms = [0]

            def inverse_root(r, r0, var, tmp):
                link(v.tensor_tensor(tmp, r0, r0, ALU.mult))
                link(v.tensor_tensor(tmp, tmp, var, ALU.mult))
                link(v.tensor_scalar(tmp, tmp, -0.5, 1.5, ALU.mult, ALU.add))
                link(v.tensor_tensor(r, r0, tmp, ALU.mult))

            def layer_norm(b, src, dst, weight=None, done=None):
                norms[0] += 1
                for t in range(NT):
                    ins = v.bn_stats(ln_stats[:, t, :], src[:, NT * b + t, :])
                link(ins)
                for t in range(NT):
                    ins = v.bn_aggr(ln_mv[:, t, :], ln_stats[:, t, :])
                link(ins)
                v.tensor_scalar(ln_var[:], ln_mv[:, :, 1], EPS_LN, None, ALU.add).then_inc(log_in, 1)
                dve.wait_ge(log_out, norms[0])
                dve.wait_ge(log_in, norms[0])
                inverse_root(ln_r[:], ln_r0[:], ln_var[:], ln_t[:])
                for t in range(NT):
                    ins = v.tensor_scalar(dst[:, NT * b + t, :], src[:, NT * b + t, :], ln_mv[:, t, 0:1],
                                          ln_r[:, t:t + 1], ALU.subtract, ALU.mult)
                if weight is not None:
                    link(ins)
                    d = dst[:, tiles(b), :]
                    ins = v.tensor_tensor(d, d, weight.unsqueeze(1).to_broadcast([P, NT, P]), ALU.mult)
                if done is None:
                    link(ins)
                else:
                    ins.then_inc(done, 1)

            def next_input(s, b):
                if s == 2:
                    loaded(dve, "rows")
                    layer_norm(b, x, y)
                    layer_norm(b, y, z, ln1_w, done=z_ready)
                elif s == 3:
                    layer_norm(b, y, z, ln2_w, done=z_ready)
                else:
                    layer_norm(b, x, z, done=z_ready)

            def make_constants():
                loaded(dve, "con")
                v.tensor_copy(ident_bf[:], ident)
                v.tensor_copy(causalT_bf[:], con[:, C_CAUSALT:C_CAUSALT + P]).then_inc(setup, 1)
                loaded(dve, "qk_w")
                link(v.tensor_scalar(qk_w[:, 0, :], qk_w[:, 0, :], SELF_SCALE, None, ALU.mult))
                half = HD // 2
                for i in range(2):
                    v.tensor_tensor(rope_c[:, i], cos, qk_w[:, i, :].unsqueeze(1).to_broadcast([P, NT, HD]),
                                    ALU.mult)
                    for h in range(2):
                        link(v.tensor_tensor(
                            rope_s[:, i, :, half * h:half * h + half], sin[:, :, half * h:half * h + half],
                            qk_w[:, i, half - half * h:HD - half * h].unsqueeze(1).to_broadcast([P, NT, half]),
                            ALU.mult))

            def copy_v(s, b):
                S = lambda name: sem(f"a{s}_{name}")
                if b:
                    dve.wait_ge(S("o_full"), NP)
                for t in range(2, NT):
                    ins = v.tensor_copy(v9[:, t, :, 0:HD],
                                        qkv_bank[t][:, 2 * P:3 * P].rearrange("p (h d) -> p h d", h=H))
                ins.then_inc(S("v_ready"), 1)

            def add_projected(s, b):
                dve.wait_ge(sem(f"a{s}_proj_full"), b + 1)
                dst = x if s == 0 else y
                v.tensor_tensor(dst[:, tiles(b), :], dst[:, tiles(b), :],
                                bank[7][:].rearrange("p (t c) -> p t c", t=NT), ALU.add).then_inc(x_added, 1)
                dve.wait_ge(x_added, 2 * s + b + 1)

            def copy_quad(s, b, k):
                S = lambda name: sem(f"a{s}_{name}")
                dve.wait_ge(S("o_full"), NP * b + 2 * k + 2)
                v.tensor_copy(o_quad[:], bank[7][:]).then_inc(S("quad_ready"), 1)

            def outputs(s, b, k):
                S = lambda name: sem(f"a{s}_{name}")
                dve.wait_ge(S("quad_full"), NP // 2 * b + k + 1)
                o = bank[7][:].rearrange("p (t h d) -> p t h d", t=NT, h=4)
                link(v.reciprocal(rsum[:], o[:, :, :, HD]))
                dst = o_tok[:].rearrange("p t (h d) -> p t h d", h=H)[:, :, 4 * k:4 * k + 4, :]
                v.tensor_tensor(dst, o[:, :, :, 0:HD], rsum[:].unsqueeze(3).to_broadcast([P, NT, 4, HD]),
                                ALU.mult).then_inc(S("o_done"), 1)

            def prepare(s, b):
                S = lambda name: sem(f"a{s}_{name}")
                for t in range(2, NT):
                    dve.wait_ge(S("qkv_full"), NT * b + t + 1)
                    rows_t = slice(t * H, t * H + H)
                    src = qkv_bank[t][:, 0:3 * P].rearrange("p (j h d) -> p j h d", j=3, h=H)
                    v.tensor_scalar(qk[:, 0, rows_t, :], src[:, 0], 1.0 if s == 0 else SELF_SCALE, None,
                                    ALU.mult)
                    ins = v.tensor_copy(qk[:, 1, rows_t, :], src[:, 1])
                link(ins)
                if b == 0:
                    copy_v(s, 0)
                dve.wait_ge(S("qk_copied"), 2 * (b + 1))
                n = NT * H
                both = qk[:].rearrange("p i n d -> p (i n) d")
                link(v.memset(qs[:, :, TERM * HD:TERM * HD + 2], 0.0))
                if s == 2:
                    dve.sem_inc(S("qk_ready"), 1)
                if s == 0:
                    link(v.tensor_tensor(sq[:].rearrange("p i n d -> p (i n) d"), both, both, ALU.mult))
                    link(v.tensor_reduce(rms_v[:], sq[:].rearrange("p i n d -> p (i n) d"), AX, ALU.add))
                    v.tensor_scalar(rms_v[:], rms_v[:], 1.0 / HD, EPS_RMS, ALU.mult, ALU.add)\
                        .then_inc(S("rms_in"), 1)
                    dve.wait_ge(S("rms_in"), b + 1)
                    dve.wait_ge(S("rms_out"), b + 1)
                    inverse_root(rms_l[:], rms_0[:], rms_v[:], rms_t[:])
                    link(v.tensor_tensor(both, both, rms_l[:].unsqueeze(2).to_broadcast([P, 2 * n, HD]), ALU.mult))
                if b == 1:
                    copy_quad(s, 0, NP // 2 - 1)
                    outputs(s, 0, NP // 2 - 1)
                    copy_v(s, 1)
                if s == 0:
                    half = HD // 2
                    for i in range(2):
                        for h in range(2):
                            sh = slice(half * h, half * h + half)
                            so = slice(half - half * h, HD - half * h)
                            link(v.tensor_tensor(
                                rope_b[:, i, :, sh].rearrange("p (t h) d -> p t h d", t=NT),
                                qk[:, i, :, so].rearrange("p (t h) d -> p t h d", t=NT),
                                rope_s[:, i, :, sh].unsqueeze(2).to_broadcast([P, NT, H, half]), ALU.mult))
                        q_i = qk[:, i].rearrange("p (t h) d -> p t h d", t=NT)
                        link(v.tensor_tensor(q_i, q_i, rope_c[:, i].unsqueeze(2).to_broadcast([P, NT, H, HD]),
                                             ALU.mult))
                    link(v.tensor_tensor(both, both, rope_b[:].rearrange("p i n d -> p (i n) d"), ALU.add))
                    dve.sem_inc(S("qk_ready"), 1)
                def again(parts, at, part, times=1):
                    dst = parts[:, :, at:at + times * HD].rearrange("p n (r d) -> p n r d", r=times)
                    src = parts[:, :, part:part + HD].unsqueeze(2).to_broadcast([P, NT * H, times, HD])
                    return v.tensor_copy(dst, src)

                for i, first in enumerate((qs, ks)):
                    dve.wait_ge(S("part1"), 2 * b + i + 1)
                    v.tensor_tensor(rest[:, i], qk[:, i], first[:, :, 0:HD], ALU.subtract)\
                        .then_inc(S("rest1"), 1)
                again(qs, HD, 0, 2)
                again(ks, 3 * HD, 0)
                again(ks, 5 * HD, 0)
                if b == 1:
                    add_projected(s, 0)
                for i, (parts, second, third) in enumerate(((qs, 3 * HD, 5 * HD), (ks, HD, 2 * HD))):
                    dve.wait_ge(S("rest1"), 2 * b + i + 1)
                    dve.wait_ge(S("part2"), 2 * b + i + 1)
                    v.tensor_tensor(parts[:, :, third:third + HD], rest[:, i], parts[:, :, second:second + HD],
                                    ALU.subtract)
                    again(parts, 4 * HD, second).then_inc(S("parts_ready"), 1)

            def causal_attention(s, b):
                S = lambda name: sem(f"a{s}_{name}")
                if b == 0:
                    prepare(s, 0)

                def maximum(n_item):
                    g, i = divmod(n_item, 8)
                    u = g % NP
                    dve.wait_ge(S("raw_full"), n_item + 1)
                    if n_item >= 2:
                        dve.wait_ge(S("max_done"), n_item - 1)
                    hh, t = i % 2, i // 2
                    w = (t + 1) * P
                    v.tensor_tensor_reduce(s_scr[:, i % 2, 0:w], bank[1 + n_item % 3][:, 0:w], causal[:, TOK - w:TOK],
                                           1.0, LOWEST, ALU.add, ALU.max, top[:, g % 2, t, hh:hh + 1])\
                        .then_inc(S("max_done"), 1)
                    if i < 7:
                        return
                    dve.wait_ge(S("max_done"), 8 * (g + 1))
                    q_t = qs.rearrange("p (t h) c -> p t h c", t=NT)[:, :, 2 * u:2 * u + 2, :]
                    link(v.tensor_scalar(q_t[:, :, :, TERM * HD], top[:, g % 2], -1.0, None, ALU.mult))
                    v.scalar_tensor_tensor(q_t[:, :, :, TERM * HD + 1], top[:, g % 2], -1.0,
                                           q_t[:, :, :, TERM * HD], ALU.mult, ALU.subtract)\
                        .then_inc(S("max_ready"), 1)

                first, end = 8 * NP * b, 8 * NP * (b + 1)
                for n_item in range(first, first + 12):
                    maximum(n_item)
                for u in range(NP):
                    if u >= 2 and u % 2:
                        copy_quad(s, b, u // 2 - 1)
                    for n_item in range(first + 12 + 8 * u, min(first + 20 + 8 * u, end)):
                        maximum(n_item)
                        if u >= 2 and u % 2 and n_item == first + 13 + 8 * u:
                            outputs(s, b, u // 2 - 1)
                    if u == NP - 1:
                        outputs(s, b, u // 2 - 1)
                    if b == 1 and u == NP - 1:
                        next_input(s + 1, 0)
                if b == 0:
                    prepare(s, 1)
                else:
                    copy_quad(s, 1, NP // 2 - 1)
                    outputs(s, 1, NP // 2 - 1)
                    add_projected(s, 1)
                    next_input(s + 1, 1)

            def cross_attention(b):
                S = lambda name: sem(f"x_{name}")
                n = XC * NT
                if b == 0:
                    loaded(dve, "mask")
                    loaded(dve, "rows")
                    dve.wait_ge(pre_done, len(CONTEXT))
                    for vb in range(NB):
                        for h in range(2):
                            ins = v.tensor_tensor(v1[:, vb, h, :], v1[:, vb, h, :], bv_row[0:HC, :], ALU.add)
                    v.memset(xq, 0.0)
                    link(v.tensor_scalar(mask[:], mask8[:], LOWEST, None, ALU.mult))

                def maxima(i):
                    g = n * b + i
                    t = i % NT
                    dve.wait_ge(S("s_full"), g + 1)
                    if g >= 2:
                        dve.wait_ge(S("p_ready"), g - 1)
                    for hh in range(2):
                        ins = v.tensor_tensor_reduce(xs[:, g % 2, hh, :], bank[2 * (g % 2) + hh][:, 0:CTX],
                                                     mask[:, NT * b + t, :], -X_SCALE, -LOWEST, ALU.add,
                                                     ALU.min, xneg[:, g % 2, hh:hh + 1])
                    ins.then_inc(S("max_done"), 1)

                def invert(i):
                    g = n * b + i
                    dve.wait_ge(S("p_ready"), g + 1)
                    v.reciprocal(xrs[:, g % 4, :], xsum[:, g % 4, :]).then_inc(S("rs_ready"), 1)

                def copy_rT(c):
                    g = XC * b + c
                    dve.wait_ge(S("rT_full"), NT * (g + 1))
                    if g >= 2:
                        dve.wait_ge(S("o_full"), g - 1)
                    v.tensor_copy(xrT[:, g % 2, :], bank[6][0:2 * RP, :]).then_inc(S("rT_ready"), 1)

                def copy_oT(c):
                    g = XC * b + c
                    dve.wait_ge(S("o_full"), g + 1)
                    v.tensor_copy(oxT[:, c, :], bank[7][:]).then_inc(S("oT_ready"), 1)

                for i in range(n + 13):
                    c, r = divmod(i - 8, NT)
                    if r == 0 and 0 <= c < XC:
                        copy_rT(c)
                    if i < n:
                        maxima(i)
                    if 1 <= i < n + 1:
                        invert(i - 1)
                    c, r = divmod(i - 12, NT)
                    if r == 0 and 0 <= c < XC:
                        copy_oT(c)
                xb = x[:, tiles(b), :]
                loaded(dve, "rows")
                link(v.tensor_tensor(xb, xb, bo.unsqueeze(1).to_broadcast([P, NT, P]), ALU.add))
                if b == 1:
                    next_input(2, 0)
                dve.wait_ge(S("proj_full"), b + 1)
                v.tensor_tensor(xb, xb, bank[7][:].rearrange("p (t c) -> p t c", t=NT), ALU.add)\
                    .then_inc(x_added, 1)
                dve.wait_ge(x_added, 2 + b + 1)

            def gate_logits(s, b):
                S = lambda name: sem(f"m{s}_{name}")
                dve.wait_ge(S("logit_full"), b + 1)
                src = bank[1][:, 0:NT * E].rearrange("p (t e) -> p t e", t=NT)
                if s == 3:
                    link(v.tensor_copy(logit[:], src))
                else:
                    loaded(dve, "l1r")
                    link(v.tensor_tensor(logit[:], src, rb2[:].unsqueeze(1).to_broadcast([P, NT, E]), ALU.add))
                link(v.tensor_reduce(g_max[:], logit[:], AX, ALU.max))
                v.tensor_tensor(logit[:], logit[:], g_max[:].unsqueeze(2).to_broadcast([P, NT, E]), ALU.subtract)\
                    .then_inc(S("gate_in"), 1)

            def gates(s, b):
                S = lambda name: sem(f"m{s}_{name}")
                dve.wait_ge(S("gate_in"), b + 1)
                dve.wait_ge(S("gate_out"), b + 1)
                if s == 3:
                    link(v.tensor_reduce(g_sum[:], g_e[:], AX, ALU.add))
                    link(v.reciprocal(g_sum[:], g_sum[:]))
                    link(v.tensor_tensor(g_e[:], g_e[:], g_sum[:].unsqueeze(2).to_broadcast([P, NT, E]), ALU.mult))
                by = g_e if s == 3 else logit
                for t in range(NT):
                    mine = by[:, t, :].unsqueeze(2).to_broadcast([P, E, E])
                    others = by[:, t, :].unsqueeze(1).to_broadcast([P, E, E])
                    v.tensor_tensor(g_cmp[:, t * E:t * E + E, :], others, mine, ALU.is_gt)
                    link(v.tensor_tensor(g_eq[:, t * E:t * E + E, :], others, mine, ALU.is_equal))
                    ge = g_eq[:, t * E:t * E + E, :]
                    ins = v.tensor_tensor(ge, ge, tri, ALU.mult)
                link(ins)
                link(v.tensor_tensor(g_cmp[:], g_cmp[:], g_eq[:], ALU.add))
                link(v.tensor_reduce(g_rank[:], g_cmp[:], AX, ALU.add))
                ge = g_e[:].rearrange("p t e -> p (t e)")
                link(v.scalar_tensor_tensor(ge, g_rank[:], 1.5, ge, ALU.is_lt, ALU.mult))
                link(v.tensor_reduce(g_sum[:], g_e[:], AX, ALU.add))
                link(v.reciprocal(g_sum[:], g_sum[:]))
                v.tensor_tensor(gate[:, b], g_e[:], g_sum[:].unsqueeze(2).to_broadcast([P, NT, E]), ALU.mult)\
                    .then_inc(S("gate_ready"), 1)
                dve.wait_ge(S("gate_ready"), b + 1)

            def experts(s):
                S = lambda name: sem(f"m{s}_{name}")
                total = y if s == 3 else z
                gate_logits(s, 0)
                gates(s, 0)
                for g in range(NB * E):
                    b, e = divmod(g, E)
                    dve.wait_ge(S("e_full"), g + 1)
                    for t in range(NT):
                        dst = total[:, NT * b + t, :]
                        ins = v.scalar_tensor_tensor(dst, bank[6 + g % 2][:, t * P:t * P + P], gate[:, b, t, e:e + 1],
                                                     dst, ALU.mult, ALU.add)
                    ins.then_inc(S("e_done"), 1)
                    dve.wait_ge(S("e_done"), g + 1)
                    if g == 1:
                        gate_logits(s, 1)
                    if g == 2:
                        gates(s, 1)
                    if e < E - 1:
                        continue
                    tb, xb = total[:, tiles(b), :], x[:, tiles(b), :]
                    if s == 6:
                        dve.wait_ge(S("be2_full"), b + 1)
                        link(v.tensor_tensor(tb, tb, bank[1][:].rearrange("p (t c) -> p t c", t=NT), ALU.add))
                    v.tensor_tensor(xb, xb, tb, ALU.add).then_inc(x_added, 1)
                    dve.wait_ge(x_added, 2 * s + b + 1)
                    if s == 3:
                        next_input(4, b)

            def divergence_attention():
                S = lambda name: sem(f"d_{name}")
                for b in range(NB):
                    dve.wait_ge(z_ready, 8 + b + 1)
                    v.tensor_reduce(a_max[:, b, :], z[:, tiles(b), :], AX, ALU.max, negate=True)\
                        .then_inc(S("max_ready"), 1)
                for b in range(NB):
                    dve.wait_ge(S("max_ready"), b + 1)
                    dve.wait_ge(S("log_ready"), b + 1)
                    v.tensor_tensor(a_nb[:, b, :], a_max[:, b, :], a_log[:, b, :], ALU.subtract)\
                        .then_inc(S("nb_ready"), 1)
                    dve.wait_ge(S("nb_ready"), b + 1)
                    for t in range(NT):
                        v.tensor_scalar(a_lp[b][:, t, :], z[:, NT * b + t, :], a_nb[:, b, t:t + 1], None, ALU.add)\
                            .then_inc(S("lp_ready"), 1)
                for b in range(NB):
                    dve.wait_ge(S("lp_ready"), NT * (b + 1))
                    dve.wait_ge(S("p_ready"), NT * (b + 1))
                    for t in range(NT):
                        ins = v.tensor_tensor_reduce(a_scr[b][:, t, :], a_p[b][:, t, :], a_lp[b][:, t, :], 1.0, 0.0,
                                                     ALU.mult, ALU.add, a_ent[:, b, t:t + 1])
                    link(ins)
                    v.tensor_scalar(a_nent[:, b, :], a_ent[:, b, :], -1.0, None, ALU.mult)\
                        .then_inc(S("ent_ready"), 1)
                for b in range(NB):
                    dve.wait_ge(S("e_ready"), NT * (b + 1))
                    link(v.reciprocal(b_rs[:, b, :], b_sum[:, b, :]))
                for b in range(NB):
                    add_normed(4, b, S("o_full"), bank[6 if b else 0])

            def add_normed(s, b, full, o):
                dve.wait_ge(full, b + 1)
                for t in range(NT):
                    xt = x[:, NT * b + t, :]
                    ins = v.scalar_tensor_tensor(xt, o[:, t * P:t * P + P], b_rs[:, b, t:t + 1], xt,
                                                 ALU.mult, ALU.add)
                ins.then_inc(x_added, 1)
                dve.wait_ge(x_added, 2 * s + b + 1)
                next_input(s + 1, b)

            def cross_attention_1():
                S = lambda name: sem(f"c_{name}")
                for b in range(NB):
                    dve.wait_ge(S("s_full"), b + 1)
                    for i in range(2):
                        ins = v.tensor_reduce(c_max[:, b, 2 * i:2 * i + 2], bank[2 + 2 * b + i][:, 0:2 * CTX]
                                              .rearrange("p (t k) -> p t k", t=2), AX, ALU.max)
                    link(ins)
                    v.tensor_scalar(c_neg[:, b, :], c_max[:, b, :], -L1X_SCALE, None, ALU.mult)\
                        .then_inc(S("neg_ready"), 1)
                for b in range(NB):
                    dve.wait_ge(S("p_ready"), NT * (b + 1))
                    link(v.reciprocal(b_rs[:, b, :], b_sum[:, b, :]))
                for b in range(NB):
                    add_normed(5, b, S("o_full"), bank[1 if b else 7])

            loaded(dve, "x")
            for b in range(NB):
                next_input(0, b)
            make_constants()
            dve.wait_ge(zeroed, 2)
            for b in range(NB):
                causal_attention(0, b)
            for b in range(NB):
                cross_attention(b)
            next_input(2, 1)
            for b in range(NB):
                causal_attention(2, b)
            experts(3)
            divergence_attention()
            cross_attention_1()
            experts(6)


CONTEXT = ([("keys", b, c) for b in range(NB) for c in range(XC)]
           + [(kind, b, c) for b in range(NB) for kind, c in (("values", 0), ("values", 1), ("rest", 0))]
           + [(kind, b, c) for b in range(NB) for kind, c in (("keys1", 0), ("values1", 0), ("values1", 1))])
CONTEXT_PARTS = (range(0, 8), range(8, 16), range(16, len(CONTEXT)))


VALUES_AFTER_EVEN = ((), (), (), (0,), (1,), (2, 3))
VALUES_AFTER_ODD = ((), (), (0,), (1,), (2,), (3,))


BIAS_STEP = 5


def zt_index(s, b):
    return 2 * s + b - (2 if s > 4 else 0)


def kernel(**inputs):
    import numpy as np
    import concourse.bacc as bacc
    from concourse.bass_utils import run_bass_kernel_spmd

    def arr(name):
        return np.asarray(inputs[name])

    con = np.zeros((P, C_END), np.float32)
    r = np.arange(P)
    con[:, C_ID:C_ID + P] = np.eye(P, dtype=np.float32)
    con[:, C_CAUSAL + TOK - P:C_CAUSAL + TOK] = np.where(r[None, :] <= r[:, None], 0.0, -3.0e38)
    con[:, C_CAUSALT:C_CAUSALT + P] = np.where(r[:, None] <= r[None, :], 0.0, -3.0e38)
    freqs = np.float32(32.0) ** (-np.arange(0, HD, 2, dtype=np.float32) / np.float32(HD))
    ang = np.arange(TOK, dtype=np.float32)[:, None] * freqs[None, :].astype(np.float32)
    cs = np.concatenate([np.cos(ang), np.cos(ang)], 1).astype(np.float32)
    sn = np.concatenate([-np.sin(ang), np.sin(ang)], 1).astype(np.float32)
    con[:, C_COS:C_COS + 32] = cs.reshape(NT, P, HD).transpose(1, 0, 2).reshape(P, 32)
    con[:, C_SIN:C_SIN + 32] = sn.reshape(NT, P, HD).transpose(1, 0, 2).reshape(P, 32)
    e = np.arange(E)
    con[:, C_TRI:C_TRI + 64] = (e[None, :] < e[:, None]).astype(np.float32).reshape(1, 64)

    cols = np.concatenate([arr("L1_xattn_bq").reshape(1, P), arr("L1_xattn_bk").reshape(1, P),
                           arr("L1_ffn_rb1").reshape(1, P), arr("L1_ffn_be1").reshape(E * F1, P)]).T
    ins = {
        "x": arr("x"), "con": con, "w_qkvT": arr("L0_attn_w_qkv").T, "w_projT": arr("L0_attn_w_proj").T,
        "qn": arr("L0_attn_q_norm_w").reshape(1, HD), "kn": arr("L0_attn_k_norm_w").reshape(1, HD),
        "ctxT": arr("ctx_1024").reshape(NB * CTX, P).T, "xWq": arr("L0_xattn_Wq"), "xWk": arr("L0_xattn_Wk"),
        "xWv": arr("L0_xattn_Wv"), "xWo": arr("L0_xattn_Wo"), "bo": arr("L0_xattn_bo").reshape(1, P),
        "mask": arr("mask_BxSxS2_bk1"), "ln1": arr("L0_ffn_ln1_w").reshape(1, P),
        "ln2": arr("L0_ffn_ln2_w").reshape(1, P), "c_attn": arr("L0_ffn_c_attn_w"),
        "c_proj": arr("L0_ffn_c_proj_w"), "router": arr("L0_ffn_router_w"), "w1": arr("L0_ffn_w1"),
        "w2": arr("L0_ffn_w2"), "l1_wqkv": np.stack([arr("L1_xattn_Wq"), arr("L1_xattn_Wk"), arr("L1_xattn_Wv")]),
        "bv": arr("L1_xattn_bv").reshape(1, P), "cols": cols, "rw1": arr("L1_ffn_rw1"), "rw2": arr("L1_ffn_rw2"),
        "rb2": arr("L1_ffn_rb2").reshape(1, E), "be2": arr("L1_ffn_be2"),
        "we1": arr("L1_ffn_we1").transpose(1, 0, 2).reshape(P, E * F1 * P),
        "we2": arr("L1_ffn_we2").reshape(E * F1 * P, P),
    }
    nc = bacc.Bacc("TRN2", target_bir_lowering=False, num_devices=1)
    arrays, aps = {}, {}
    for name, value in ins.items():
        value = np.ascontiguousarray(value)
        arrays[f"in_{name}"] = value
        aps[name] = nc.dram_tensor(f"in_{name}", value.shape, mybir.dt.from_np(value.dtype),
                                   kind="ExternalInput").ap()
    out = nc.dram_tensor("out_x", (NB, TOK, P), FP, kind="ExternalOutput").ap()
    decoder(nc, aps, out)
    result = run_bass_kernel_spmd(nc, [arrays], core_ids=[0])
    return result.results[0]["out_x"]
```
